# Optimizing a Trainium2 kernel written in Bass

```python
import numpy as np
import jax
import jax.numpy as jnp

def _softmax(x, axis=-1):
    return jax.nn.softmax(x, axis=axis)

def _gelu(x):
    return jax.nn.gelu(x, approximate=True)

def _silu(x):
    return jax.nn.silu(x)

def _sigmoid(x):
    return jax.nn.sigmoid(x)

def _layernorm(x, axis=-1, eps=1e-05):
    m = jnp.mean(x, axis=axis, keepdims=True)
    v = jnp.var(x, axis=axis, keepdims=True)
    return (x - m) / jnp.sqrt(v + eps)

def _scatter_add(tgt, idx, src, axis=0):
    return tgt.at[idx].add(src)

def _segment_sum(src, seg, n):
    return jax.ops.segment_sum(src, seg, n)
kernel_name = 'mk_decoder_preln_d1_seqx_r4_fae1e5'

def setup_inputs(seed: int=0):
    np.random.seed(seed)
    _w = jnp.asarray

    def _rec_inputs():
        import jax
        import jax.numpy as jnp
        _rk = jax.random.key(seed)
        x = 7.22e-05 + 1 * jax.random.normal(jax.random.fold_in(_rk, 1), (2, 1024, 256), jnp.float32)
        _lenS = 1024 - jax.random.randint(jax.random.fold_in(_rk, 7), (2,), 0, max(1, 1024 // 4) + 1, jnp.int32)
        _lenS2 = 154 - jax.random.randint(jax.random.fold_in(_rk, 8), (2,), 0, max(1, 154 // 4) + 1, jnp.int32)
        _ctx_768P = jax.random.normal(jax.random.fold_in(_rk, 11), (2, 16, 192), jnp.float32)
        _ctx_768c = jax.random.dirichlet(jax.random.fold_in(_rk, 511), 0.3 * jnp.ones((16,), jnp.float32), (2, 154))
        _ctx_768t = jnp.einsum('bsk,bkd->bsd', _ctx_768c, _ctx_768P)
        _ctx_768t = _ctx_768t * jax.lax.rsqrt(jnp.mean(jnp.square(_ctx_768t)) + 1e-12) * 0.953939
        ctx_768 = -0.000191848 + 0.999787 * (_ctx_768t + 0.3 * jax.random.normal(jax.random.fold_in(_rk, 611), (2, 154, 192), jnp.float32))
        return (x, ctx_768)
    x, ctx_768 = _rec_inputs()

    def _L0_attn_setup():
        import jax, jax.numpy as jnp
        import numpy as np
        EMB = 256
        NH = 16
        HS = EMB // NH
        key = jax.random.key(seed)
        ks = jax.random.split(key, 9)
        s = 0.02
        x = jax.random.normal(ks[0], (4, 512, EMB), dtype=jnp.float32)
        Wq = jax.random.normal(ks[1], (EMB, EMB), dtype=jnp.float32) * s
        bq = jnp.zeros((EMB,), jnp.float32)
        Wk = jax.random.normal(ks[2], (EMB, EMB), dtype=jnp.float32) * s
        bk = jnp.zeros((EMB,), jnp.float32)
        Wv = jax.random.normal(ks[3], (EMB, EMB), dtype=jnp.float32) * s
        bv = jnp.zeros((EMB,), jnp.float32)
        Wo = jax.random.normal(ks[4], (EMB, EMB), dtype=jnp.float32) * s
        bo = jnp.zeros((EMB,), jnp.float32)
        return {'x': x, 'Wq': Wq, 'bq': bq, 'Wk': Wk, 'bk': bk, 'Wv': Wv, 'bv': bv, 'Wo': Wo, 'bo': bo}
    _L0_attn_all = _L0_attn_setup()
    _L0_attn_in = {k: v for k, v in _L0_attn_all.items() if k in ('Wq', 'bq', 'Wk', 'bk', 'Wv', 'bv', 'Wo', 'bo')}
    del _L0_attn_all

    def _L0_xattn_setup():
        import jax, jax.numpy as jnp
        import numpy as np
        HEADS = 16
        DIM_HEAD = 64
        QUERY_DIM = 256
        CONTEXT_DIM = 192
        INNER = HEADS * DIM_HEAD
        SCALE = DIM_HEAD ** (-0.5)
        key = jax.random.key(seed)
        ks = jax.random.split(key, 7)
        B, Sq, Skv = (4, 512, 512)
        x = jax.random.normal(ks[0], (B, Sq, QUERY_DIM), dtype=jnp.float32)
        context = jax.random.normal(ks[1], (B, Skv, CONTEXT_DIM), dtype=jnp.float32)
        w_q = jax.random.normal(ks[2], (QUERY_DIM, INNER), dtype=jnp.float32) / np.sqrt(QUERY_DIM)
        w_k = jax.random.normal(ks[3], (CONTEXT_DIM, INNER), dtype=jnp.float32) / np.sqrt(CONTEXT_DIM)
        w_v = jax.random.normal(ks[4], (CONTEXT_DIM, INNER), dtype=jnp.float32) / np.sqrt(CONTEXT_DIM)
        w_o = jax.random.normal(ks[5], (INNER, QUERY_DIM), dtype=jnp.float32) / np.sqrt(INNER)
        b_o = jax.random.normal(ks[6], (QUERY_DIM,), dtype=jnp.float32) * 0.02
        return {'x': x, 'context': context, 'w_q': w_q, 'w_k': w_k, 'w_v': w_v, 'w_o': w_o, 'b_o': b_o}
    _L0_xattn_all = _L0_xattn_setup()
    _L0_xattn_in = {k: v for k, v in _L0_xattn_all.items() if k in ('w_q', 'w_k', 'w_v', 'w_o', 'b_o')}
    del _L0_xattn_all

    def _L0_ffn_setup():
        import jax, jax.numpy as jnp
        import numpy as np
        E = 16
        H = 256
        F = 512
        TOP_K = 1
        B, S = (2, 256)
        key = jax.random.key(seed)
        ks = jax.random.split(key, 7)
        s = 0.02
        return {'hidden_states': jax.random.normal(ks[0], (B, S, H), jnp.float32), 'w_router': jax.random.normal(ks[1], (E, H), jnp.float32) * s, 'gate_up_proj': jax.random.normal(ks[2], (E, H, 2 * F), jnp.float32) * s, 'down_proj': jax.random.normal(ks[3], (E, F, H), jnp.float32) * s, 'w_gate': jax.random.normal(ks[4], (F, H), jnp.float32) * s, 'w_up': jax.random.normal(ks[5], (F, H), jnp.float32) * s, 'w_down': jax.random.normal(ks[6], (H, F), jnp.float32) * s}
    _L0_ffn_all = _L0_ffn_setup()
    _L0_ffn_in = {k: v for k, v in _L0_ffn_all.items() if k in ('w_router', 'gate_up_proj', 'down_proj', 'w_gate', 'w_up', 'w_down')}
    del _L0_ffn_all
    return {'x': x, 'ctx_768': ctx_768, 'L0_attn_Wq': _L0_attn_in['Wq'], 'L0_attn_bq': _L0_attn_in['bq'], 'L0_attn_Wk': _L0_attn_in['Wk'], 'L0_attn_bk': _L0_attn_in['bk'], 'L0_attn_Wv': _L0_attn_in['Wv'], 'L0_attn_bv': _L0_attn_in['bv'], 'L0_attn_Wo': _L0_attn_in['Wo'], 'L0_attn_bo': _L0_attn_in['bo'], 'L0_xattn_w_q': _L0_xattn_in['w_q'], 'L0_xattn_w_k': _L0_xattn_in['w_k'], 'L0_xattn_w_v': _L0_xattn_in['w_v'], 'L0_xattn_w_o': _L0_xattn_in['w_o'], 'L0_xattn_b_o': _L0_xattn_in['b_o'], 'L0_ffn_w_router': _L0_ffn_in['w_router'], 'L0_ffn_gate_up_proj': _L0_ffn_in['gate_up_proj'], 'L0_ffn_down_proj': _L0_ffn_in['down_proj'], 'L0_ffn_w_gate': _L0_ffn_in['w_gate'], 'L0_ffn_w_up': _L0_ffn_in['w_up'], 'L0_ffn_w_down': _L0_ffn_in['w_down']}

def reference(x, ctx_768, L0_attn_Wq, L0_attn_bq, L0_attn_Wk, L0_attn_bk, L0_attn_Wv, L0_attn_bv, L0_attn_Wo, L0_attn_bo, L0_xattn_w_q, L0_xattn_w_k, L0_xattn_w_v, L0_xattn_w_o, L0_xattn_b_o, L0_ffn_w_router, L0_ffn_gate_up_proj, L0_ffn_down_proj, L0_ffn_w_gate, L0_ffn_w_up, L0_ffn_w_down):
    import jax
    import jax.numpy as jnp

    def _L0_attn_ref(x, Wq, bq, Wk, bk, Wv, bv, Wo, bo):
        import jax, jax.numpy as jnp
        import numpy as np
        EMB = 256
        NH = 16
        HS = EMB // NH
        B, T, C = x.shape
        q = x @ Wq + bq
        k = x @ Wk + bk
        v = x @ Wv + bv
        q = q.reshape(B, T, NH, HS).transpose(0, 2, 1, 3)
        k = k.reshape(B, T, NH, HS).transpose(0, 2, 1, 3)
        v = v.reshape(B, T, NH, HS).transpose(0, 2, 1, 3)
        scale = 1.0 / np.sqrt(HS).astype(np.float32)
        att = jnp.einsum('bhqd,bhkd->bhqk', q, k) * scale
        causal = jnp.tril(jnp.ones((T, T), dtype=bool))
        att = jnp.where(causal[None, None], att, jnp.float32(-jnp.inf))
        att = jax.nn.softmax(att, axis=-1)
        y = jnp.einsum('bhqk,bhkd->bhqd', att, v)
        y = y.transpose(0, 2, 1, 3).reshape(B, T, C)
        return y @ Wo + bo

    def _L0_xattn_ref(x, context, w_q, w_k, w_v, w_o, b_o):
        import jax, jax.numpy as jnp
        import numpy as np
        HEADS = 16
        DIM_HEAD = 64
        QUERY_DIM = 256
        CONTEXT_DIM = 192
        INNER = HEADS * DIM_HEAD
        SCALE = DIM_HEAD ** (-0.5)
        B, Sq, _ = x.shape
        Skv = context.shape[1]
        q = (x @ w_q).reshape(B, Sq, HEADS, DIM_HEAD).transpose(0, 2, 1, 3)
        k = (context @ w_k).reshape(B, Skv, HEADS, DIM_HEAD).transpose(0, 2, 1, 3)
        v = (context @ w_v).reshape(B, Skv, HEADS, DIM_HEAD).transpose(0, 2, 1, 3)
        sim = jnp.einsum('bhid,bhjd->bhij', q, k) * SCALE
        attn = jax.nn.softmax(sim, axis=-1)
        out = jnp.einsum('bhij,bhjd->bhid', attn, v)
        out = out.transpose(0, 2, 1, 3).reshape(B, Sq, INNER)
        return out @ w_o + b_o

    def _L0_ffn_ref(hidden_states, w_router, gate_up_proj, down_proj, w_gate, w_up, w_down):
        import jax, jax.numpy as jnp
        import numpy as np
        E = 16
        H = 256
        F = 512
        TOP_K = 1
        B, S = (2, 256)
        b, s, h = hidden_states.shape
        x = hidden_states.reshape(-1, h)
        logits = x @ w_router.T
        _, top_idx = jax.lax.top_k(logits, TOP_K)
        mask = jax.nn.one_hot(top_idx, E, dtype=logits.dtype).sum(axis=1)
        scores = jax.nn.sigmoid(logits) * mask
        masked_inputs = scores.T[:, :, None] * x[None, :, :]
        gate_up = jnp.einsum('eth,ehf->etf', masked_inputs, gate_up_proj)
        gate, up = jnp.split(gate_up, 2, axis=-1)
        expert_out = jnp.einsum('etf,efh->eth', up * jax.nn.silu(gate), down_proj)
        shared = jax.nn.silu(x @ w_gate.T) * (x @ w_up.T) @ w_down.T
        out = shared + expert_out.sum(axis=0)
        return out.reshape(b, s, h)
    x = x + _L0_attn_ref(_layernorm(x, axis=-1), L0_attn_Wq, L0_attn_bq, L0_attn_Wk, L0_attn_bk, L0_attn_Wv, L0_attn_bv, L0_attn_Wo, L0_attn_bo)
    x = x + _L0_xattn_ref(_layernorm(x, axis=-1), ctx_768, L0_xattn_w_q, L0_xattn_w_k, L0_xattn_w_v, L0_xattn_w_o, L0_xattn_b_o)
    x = x + _L0_ffn_ref(_layernorm(x, axis=-1), L0_ffn_w_router, L0_ffn_gate_up_proj, L0_ffn_down_proj, L0_ffn_w_gate, L0_ffn_w_up, L0_ffn_w_down)
    return x

_drawn_inputs = setup_inputs


def setup_inputs(seed=0):
    import zlib

    import numpy as np

    out = dict(_drawn_inputs(seed))
    spreads = {'L0_attn_bq': (0.0, 0.8),
     'L0_attn_bk': (0.0, 2.0),
     'L0_attn_bv': (0.0, 0.277),
     'L0_attn_bo': (0.0, 0.1)}
    factors = {'L0_attn_Wq': 8.0,
     'L0_attn_Wk': 8.0,
     'L0_attn_Wv': 7.349,
     'L0_xattn_b_o': 3.099,
     'L0_ffn_w_router': 6.86,
     'L0_ffn_gate_up_proj': 6.604,
     'L0_ffn_down_proj': 6.592,
     'L0_ffn_w_up': 18.606,
     'L0_ffn_w_gate': 7.072,
     'L0_ffn_w_down': 6.831}
    for name, (base, spread) in spreads.items():
        noise = np.random.default_rng([zlib.crc32(name.encode()), seed]).standard_normal(out[name].shape)
        drawn = base * np.exp(spread * noise) if base else spread * noise
        out[name] = jnp.asarray(drawn.astype(out[name].dtype))
    for name, factor in factors.items():
        out[name] = (out[name] * factor).astype(out[name].dtype)
    return out
```

```python
from contextlib import ExitStack

import numpy as np

import concourse.bass as bass
from concourse import mybir

F32 = mybir.dt.float32
BF16 = mybir.dt.bfloat16
U32 = mybir.dt.uint32
I32 = mybir.dt.int32
ALU = mybir.AluOpType
ACT = mybir.ActivationFunctionType
AX = mybir.AxisListType

P = 128
B, S, C = 2, 1024, 256
CB = 4
CT = CB * P
NCH = B * S // CT
FC = C // P
NBLK = B * S // P
EPS = 1e-5
NEG = -1.0e30

H, HD = 16, 16
GH = 4
NG = B * H // GH
VW = 32
SELF_SCALE = HD ** -0.5
Q_PART = (0, 0, 1, 0, 2, 1)
K_PART = (0, 1, 0, 2, 0, 1)
NPROD = len(Q_PART)
KROWS = NPROD * HD
KROWS_M = KROWS + 3
QB = S // P
STEPS = [(qc, kb) for qc in range(S // CT) for kb in range((qc + 1) * CB)]
NST = len(STEPS)
UNITS = [(h, qb) for h in range(GH) for qb in range(QB)]
NU = len(UNITS)
UNIT_STEPS = range(2, 2 + NU // GH)
SPLIT_STEP = 10
P_SLOTS, S_SLOTS = 8, 3

XH, XD = 16, 64
SK, CD = 154, 192
CK = CD // 2
PAIRS = XH // 2
PK = 2 * SK
KC = 103
NKC = 3
XI = XH * XD
XSCALE = XD ** -0.5
XU = PAIRS * CB
T_LAG, PV_LAG = 3, 5

E, F = 16, 512
FF = F // P
NT = 32


def bcast_rows(v):
    return v.rearrange("(o n) -> o n", o=1).to_broadcast((P, v.shape[0]))


def bcast_rows(v):
    return v.rearrange("(o n) -> o n", o=1).to_broadcast((P, v.shape[0]))


def bcast_rows(v):
    return v.rearrange("(o n) -> o n", o=1).to_broadcast((P, v.shape[0]))


def bcast_rows(v):
    return v.rearrange("(o n) -> o n", o=1).to_broadcast((P, v.shape[0]))


def bcast_rows(v):
    return v.rearrange("(o n) -> o n", o=1).to_broadcast((P, v.shape[0]))


def bcast_rows(v):
    return v.rearrange("(o n) -> o n", o=1).to_broadcast((P, v.shape[0]))


def bcast_rows(v):
    return v.rearrange("(o n) -> o n", o=1).to_broadcast((P, v.shape[0]))


def bcast_rows(v):
    return v.rearrange("(o n) -> o n", o=1).to_broadcast((P, v.shape[0]))


def bcast_rows(v):
    return v.rearrange("(o n) -> o n", o=1).to_broadcast((P, v.shape[0]))


def build(nc, x, ctxT, wq, bq, wk, bk, wv, bv, wo, bo, wqx, wkx, wvx, wox, box, wr, wgu, wdn, wsg, wsu, wsd, out):
    parts_d = nc.dram_tensor("qk_parts", (3, 2, B, C, S), BF16, kind="Internal").ap()
    vx_d = nc.dram_tensor("cross_values", (B, SK, XI), F32, kind="Internal").ap()
    xg_d = nc.dram_tensor("expert_rows_in", ((NT + 1) * P, C), F32, kind="Internal").ap()
    yg_d = nc.dram_tensor("expert_rows_out", (NT * P, C), F32, kind="Internal").ap()

    with ExitStack() as ctx:
        def sb(name, shape, dt=F32, where=ctx):
            return where.enter_context(nc.sbuf_tensor(name, shape, dt))

        def sem(name):
            return ctx.enter_context(nc.semaphore(name))

        x_all = sb("x_all", [P, NBLK, C])
        ident = sb("ident", [P, P])
        identb = sb("identb", [P, P], BF16)
        maskq = sb("maskq", [P, P], BF16)
        maskk = sb("maskk", [P, P], BF16)
        before = sb("before", [P, P], BF16)
        onesb = sb("onesb", [P, P], BF16)
        xn_all = sb("xn_all", [P, NBLK, C])
        stats = sb("stats", [P, CB, 6])
        mv = sb("mv", [P, CB, 2])
        vpe = sb("vpe", [P, CB])
        rstd = sb("rstd", [P, CB])
        mhalf = sb("mhalf", [P, CB])
        xnT = sb("xnT", [P, FC, CT])
        wo_s = sb("wo_s", [P, GH, C])
        bo_s = sb("bo_s", [P, C])
        box_s = sb("box_s", [P, C])
        wqx_s = sb("wqx_s", [P, FC, XI])
        wox_s = sb("wox_s", [P, PAIRS, C])
        wr_s = sb("wr_s", [P, FC, E])
        lg_all = sb("lg_all", [P, NBLK, E])
        zeros = sb("zeros", [P, C])

        with ExitStack() as attn:
            yT = sb("yT", [P, NG, S], F32, attn)
            kx = sb("kx", [P, B, PAIRS, PK], F32, attn)
            vx = sb("vx", [P, PAIRS, NKC, P], F32, attn)
            with ExitStack() as early:
                v_all = sb("v_all", [P, B, GH, QB, GH * HD], F32, early)
                vp = [sb(f"vp{s}", [P, QB, GH, VW], F32, early) for s in range(2)]
                nmax = sb("nmax", [P, P], F32, early)
                nmp = sb("nmp", [NU, 3, P], BF16, early)
                nmr = sb("nmr", [NU, P], F32, early)
                sums = sb("sums", [P, CT], F32, early)
                with ExitStack() as one:
                    wqkv = sb("wqkv", [P, FC, 3, C], F32, one)
                    bqk = sb("bqk", [P, 4], F32, one)
                    bv_s = sb("bv_s", [P, C], F32, one)
                    with ExitStack() as kv:
                        wkx_s = sb("wkx_s", [CK, 2, XI], F32, kv)
                        wvx_s = sb("wvx_s", [CK, 2, XI], F32, kv)
                        ctx_s = sb("ctx_s", [CK, 2, B * SK], F32, kv)
                        vtmp = sb("vtmp", [SK // 2, B, 2, XI], F32, kv)
                    with ExitStack() as proj:
                        qf = sb("qf", [P, 4, CT], F32, proj)
                        qr = sb("qr", [P, 4, CT], F32, proj)
                        qp = sb("qp", [P, 3, 4, CT], BF16, proj)
                with ExitStack() as two:
                    qst = [sb(f"qst{s}", [P, GH, S], BF16, two) for s in range(2)]
                    kst = [sb(f"kst{s}", [P, GH, S], BF16, two) for s in range(2)]
                    probs = sb("probs", [P, P_SLOTS, CT], F32, two)
            with ExitStack() as late:
                yc = sb("yc", [P, GH, CT], F32, late)
                xn2 = sb("xn2", [P, CB, C], F32, late)
                qT = sb("qT", [P, PAIRS, CT], F32, late)
                px = sb("px", [P, 4, NKC * KC], F32, late)
                nmx = sb("nmx", [P, 4, 2], F32, late)
                smx = sb("smx", [P, 4, 2], F32, late)
                rsx = sb("rsx", [P, 4, 2], F32, late)
                pT = sb("pT", [P, 2, NKC, CT], F32, late)
                xnT_all = sb("xnT_all", [P, FC, B * S], F32, late)
                wsg_s = sb("wsg_s", [P, FC, F], F32, late)
                wsu_s = sb("wsu_s", [P, FC, F], F32, late)
                wsd_s = sb("wsd_s", [P, FF, C], F32, late)
        with ExitStack() as moe:
            wgu_s = [sb(f"wgu{s}", [P, FC, 2 * F], F32, moe) for s in range(2)]
            wdn_s = [sb(f"wdn{s}", [P, FF, C], F32, moe) for s in range(2)]
            xg = [sb(f"xg{s}", [P, C], F32, moe) for s in range(2)]
            xgT = [sb(f"xgT{s}", [P, FC, P], F32, moe) for s in range(2)]
            act_s = [sb(f"act{s}", [P, FF, P], F32, moe) for s in range(2)]
            hT = [sb(f"hT{s}", [P, FF, P], F32, moe) for s in range(2)]
            yo = [sb(f"yo{s}", [P, C], F32, moe) for s in range(2)]
            sgl = sb("sgl", [P, CT], F32, moe)
            shT = sb("shT", [P, FF, CT], F32, moe)
            mx = sb("mx", [P, NBLK], F32, moe)
            emx = sb("emx", [P, NBLK], F32, moe)
            score = sb("score", [P, NBLK], F32, moe)
            em99 = sb("em99", [P, E], F32, moe)
            cand = sb("cand", [P, NBLK, E], F32, moe)
            pick = sb("pick", [P, NBLK], F32, moe)
            onehot = sb("onehot", [P, NBLK, E], F32, moe)
            onehotb = sb("onehotb", [P, NBLK, E], BF16, moe)
            steps128 = sb("steps128", [P, NBLK], F32, moe)
            over = sb("over", [P, E, NBLK], F32, moe)
            tiles = sb("tiles", [P, E], F32, moe)
            ones_e = sb("ones_e", [P, E], F32, moe)
            ends = sb("ends", [P, E], F32, moe)
            base_t = sb("base", [P, E], F32, moe)
            posf = sb("posf", [P, NBLK], F32, moe)
            pos = sb("pos", [P, NBLK], U32, moe)
            tno = sb("tno", [1, NT], F32, moe)
            passed = sb("passed", [1, NT, E], F32, moe)
            eotf = sb("eotf", [1, NT], F32, moe)
            eot = sb("eot", [1, NT], I32, moe)

        ps = ctx.enter_context(nc.psum_tensor("ps", [P, 8, 512], F32))

        passed_wait = {e: sem(f"passed_{e}") for e in ("dve", "pool", "pe")}

        def wait_apart(eng, name, which, value):
            eng.wait_ge(which, value)
            eng.sem_inc(passed_wait[name], 1)

        class Chain:

            def __init__(self, eng, name):
                self.eng, self.sem, self.base, self.n = eng, sem(name), 0, 0

            def add(self, ins):
                ins.then_inc(self.sem, 1)
                self.n += 1

            def wait(self):
                self.eng.wait_ge(self.sem, self.base + self.n)

            def wait_apart(self, name):
                wait_apart(self.eng, name, self.sem, self.base + self.n)

            def turn(self, i, per):
                self.start, self.per = self.base + self.n, per
                self.base, self.n = i * per + self.start, 0

            def turned(self, turns):
                assert self.n == self.per, (self.n, self.per)
                self.base, self.n = self.start + turns * self.per, 0

        ready_const = sem("ready_const")
        ready_zero = sem("ready_zero")
        in_ctx, in_x, in_qkv, in_rest = sem("in_ctx"), sem("in_x"), sem("in_qkv"), sem("in_rest")
        in_shared = sem("in_shared")
        zero_rows = sem("zero_rows")
        kx_ready, kx_act, kx_dve = sem("kx_ready"), sem("kx_act"), sem("kx_dve")
        vc_ready, vc_act, vc_dve, vc_out = sem("vc_ready"), sem("vc_act"), sem("vc_dve"), sem("vc_out")
        var_ready, rstd_ready, xn_ready = sem("var_ready"), sem("rstd_ready"), sem("xn_ready")
        t1_ready, xnT_ready = sem("t1_ready"), sem("xnT_ready")
        qk_ready, qk_taken, hi_ready, v_ready, v_taken = sem("qk_ready"), sem("qk_taken"), sem("hi_ready"), sem("v_ready"), sem("v_taken")
        qf_free, mid_ready, lo_ready = sem("qf_free"), sem("mid_ready"), sem("lo_ready")
        hi_out, mid_out, lo_out = sem("hi_out"), sem("mid_out"), sem("lo_out")
        bo_added = sem("bo_added")
        q_in = [sem(f"stack_in{s}") for s in range(2)]
        vp_ready = [sem(f"vp_ready{s}") for s in range(2)]
        shift_in = [sem(f"shift_in{s}") for s in range(2)]
        max_ready, max_taken = sem("max_ready"), sem("max_taken")
        nmT_ready, shift_ready = sem("nmT_ready"), sem("shift_ready")
        s_ready, p_ready, pv_done, o_taken = sem("s_ready"), sem("p_ready"), sem("pv_done"), sem("o_taken")
        vx_free, vx_in = sem("vx_free"), sem("vx_in")
        yc_ready, wo_done, x1_ready, xn2_ready, box_added = sem("yc_ready"), sem("wo_done"), sem("x1_ready"), sem("xn2_ready"), sem("box_added")
        t2_ready, xnT2_ready, t3_ready, xnT3_ready = sem("t2_ready"), sem("xnT2_ready"), sem("t3_ready"), sem("xnT3_ready")
        var2_ready, rstd2_ready = sem("var2_ready"), sem("rstd2_ready")
        qx_ready, qx_act, qx_dve = sem("qx_ready"), sem("qx_act"), sem("qx_dve")
        sx_ready, mx_ready, ex_ready, px_ready = sem("sx_ready"), sem("mx_ready"), sem("ex_ready"), sem("px_ready")
        tx_ready, tx_act, tx_dve = sem("tx_ready"), sem("tx_act"), sem("tx_dve")
        ox_ready, ox_act, ox_dve = sem("ox_ready"), sem("ox_act"), sem("ox_dve")
        wox_done, xn3_ready, lg_ready, lg_taken, t3_dve = sem("wox_done"), sem("xn3_ready"), sem("lg_ready"), sem("lg_taken"), sem("t3_dve")
        mxl_ready, exp_ready, oh_ready, rank_ready, tno_ready = sem("mxl_ready"), sem("exp_ready"), sem("oh_ready"), sem("rank_ready"), sem("tno_ready")
        xs_ready, pos_ready, eot_ready, scattered = sem("xs_ready"), sem("pos_ready"), sem("eot_ready"), sem("scattered")
        gs_ready, us_ready, gs_silu, hs_ready, us_taken, ds_ready, ds_taken = (sem(n) for n in ("gs_ready", "us_ready", "gs_silu", "hs_ready", "us_taken", "ds_ready", "ds_taken"))
        w_in = [sem(f"w_in{s}") for s in range(2)]
        xg_in = [sem(f"xg_in{s}") for s in range(2)]
        w_free = [sem(f"w_free{s}") for s in range(2)]
        te_ready, xgT_ready, ge_ready, ue_ready, silu_ready, he_ready, de_ready, yo_ready = (sem(n) for n in ("te_ready", "xgT_ready", "ge_ready", "ue_ready", "silu_ready", "he_ready", "de_ready", "yo_ready"))
        yo_out = [sem(f"yo_out{s}") for s in range(2)]
        gathered = [sem(f"gathered{n}") for n in range(4)]
        out_ready, stored = sem("out_ready"), sem("stored")

        block = ctx.enter_context(nc.Block())

        @block.sync
        def _(sp):
            def rows(w):
                return w.rearrange("(t p) n -> p t n", p=P)

            def load_context_and_weights():
                sp.dma_start(ctx_s[:], ctxT.rearrange("(t p) n -> p t n", p=CK)).then_inc(in_ctx, 16)
                sp.dma_start(wkx_s[:], wkx.rearrange("(t p) n -> p t n", p=CK)).then_inc(in_ctx, 16)
                sp.dma_start(wvx_s[:], wvx.rearrange("(t p) n -> p t n", p=CK)).then_inc(in_ctx, 16)
                sp.dma_start(x_all[:], x.rearrange("b (k p) c -> p (b k) c", p=P)).then_inc(in_x, 16)
                for n, w in enumerate((wq, wk, wv)):
                    sp.dma_start(wqkv[:, :, n, :], rows(w)).then_inc(in_qkv, 16)
                for n, b_ in enumerate((bq, bk)):
                    sp.dma_start(bqk[:, 2 * n:2 * n + 2], b_.rearrange("(t p) -> p t", p=P), allow_slow_non_contiguous=True).then_inc(in_qkv, 16)
                sp.dma_start(bv_s[:], bcast_rows(bv)).then_inc(in_qkv, 16)
                sp.dma_start(bo_s[:], bcast_rows(bo)).then_inc(in_rest, 16)
                sp.dma_start(box_s[:], bcast_rows(box)).then_inc(in_rest, 16)
                sp.wait_ge(ready_zero, 1)
                for h in range(GH):
                    sp.dma_start(wo_s[VW * h:VW * h + HD, :, :],
                                 wo.rearrange("(g h d) n -> h d g n", h=GH, d=HD)[h]).then_inc(in_rest, 16)
                sp.dma_start(wqx_s[:], rows(wqx)).then_inc(in_rest, 16)
                sp.dma_start(wox_s[:], rows(wox)).then_inc(in_rest, 16)
                sp.dma_start(wr_s[:], rows(wr)).then_inc(in_rest, 16)
                for t in range(NT + 1):
                    sp.dma_start(xg_d[t * P:(t + 1) * P, :], zeros[:]).then_inc(zero_rows, 16)

            def store_parts(b, cc):
                c = b * 2 + cc
                for j, (ready, done) in enumerate(((hi_ready, hi_out), (mid_ready, mid_out), (lo_ready, lo_out))):
                    for qk in range(2):
                        dst = parts_d[j, qk, bass.ds(b, 1), :, bass.ds(cc * CT, CT)].rearrange("o (m p) t -> p (o m) t", p=P)
                        if qk == 0:
                            sp.wait_ge(ready, c + 1)
                        sp.dma_start(dst, qp[:, j, 2 * qk:2 * qk + 2, :]).then_inc(done, 16)

            def load_stacks(g, s):
                for part, st, qk in ((Q_PART, qst, 0), (K_PART, kst, 1)):
                    for j in range(NPROD):
                        src = parts_d[part[j], qk].rearrange("b (g h d) t -> (b g) d h t", h=GH, d=HD)[bass.ds(g, 1)]
                        sp.dma_start(st[s][HD * j:HD * j + HD, :, :], src.rearrange("o d h t -> (o d) h t")).then_inc(q_in[s], 16)

            def load_shift(g, s):
                sp.wait_ge(shift_ready, g + 1)
                for j in range(3):
                    sp.dma_start(qst[s][KROWS + j:KROWS + j + 1, :, :].rearrange("o h (b q) -> o (h b) q", q=P),
                                 nmp[:, j, :]).then_inc(shift_in[s], 16)

            load_context_and_weights()
            sp.wait_ge(vc_act, 4)
            sp.wait_ge(vc_dve, 4)
            sp.dma_start(vx_d.rearrange("b (k p) n -> p b k n", p=SK // 2), vtmp[:]).then_inc(vc_out, 16)
            sp.sem_inc(hi_out, 32)
            sp.sem_inc(mid_out, 32)
            sp.sem_inc(lo_out, 32)
            with sp.Fori(0, B) as b:
                with sp.Fori(0, S // CT) as cc:
                    store_parts(b, cc)
            for done in (hi_out, mid_out, lo_out):
                sp.wait_ge(done, 32 * (NCH + 1))
            sp.wait_ge(v_taken, NCH + 1)
            load_stacks(0, 0)
            load_stacks(1, 1)
            load_shift(0, 0)
            load_shift(1, 1)
            with sp.Fori(1, NG // 2) as i:
                for s in range(2):
                    sp.wait_ge(s_ready, i * (2 * NST * GH) + (s - 1) * NST * GH)
                    load_stacks(i * 2 + s, s)
                    load_shift(i * 2 + s, s)

            sp.wait_ge(pv_done, NG * NST + 2)
            sp.dma_start(wsg_s[:], rows(wsg)).then_inc(in_shared, 16)
            sp.dma_start(wsu_s[:], rows(wsu)).then_inc(in_shared, 16)
            sp.dma_start(wsd_s[:], rows(wsd)).then_inc(in_shared, 16)
            sp.wait_ge(vc_out, 16)
            with sp.Fori(0, B) as b:
                sp.wait_ge(vx_free, b + 1)
                src = vx_d[bass.ds(b, 1)].rearrange("o k (m h d) -> (o k) m h d", m=PAIRS, h=2)
                r = 2 * KC - SK
                for rows_, c, h, k0 in (((0, KC), 0, 0, 0), ((0, SK - KC), 1, 0, KC), ((SK - KC, KC), 1, 1, 0),
                                        ((0, SK - r), 2, 1, r)):
                    n = rows_[1] - rows_[0]
                    sp.dma_start(vx[rows_[0]:rows_[1], :, c, XD * h:XD * h + XD], src[k0:k0 + n, :, h, :]).then_inc(vx_in, 16)
                del r

            sp.wait_ge(eot_ready, 1)
            sp.wait_ge(scattered, 16 * NBLK)
            with sp.Fori(0, NT // 2) as i:
                for s in range(2):
                    e = sp.value_load(eot[0:1, bass.ds(i * 2 + s, 1)], min_val=0, max_val=E - 1)
                    t = sp.snap(i * 2 + s)
                    sp.wait_ge(w_free[s], i + 1)
                    sp.dma_start(xg[s][:], xg_d.rearrange("(t p) c -> t p c", p=P)[bass.ds(t, 1)].rearrange("o p c -> (o p) c")).then_inc(xg_in[s], 16)
                    sp.dma_start(wgu_s[s][:], wgu[bass.ds(e, 1)].rearrange("o (t p) n -> p (o t) n", p=P)).then_inc(w_in[s], 16)
                    sp.dma_start(wdn_s[s][:], wdn[bass.ds(e, 1)].rearrange("o (t p) n -> p (o t) n", p=P)).then_inc(w_in[s], 16)
            sp.wait_ge(w_free[0], NT // 2 + 1)
            sp.dma_start(xg[0][:], xg_d[NT * P:(NT + 1) * P, :]).then_inc(xg_in[0], 16)
            for n in range(4):
                sp.wait_ge(out_ready, n + 1)
                sp.dma_start(out.rearrange("b (k p) c -> p (b k) c", p=P)[:, 4 * n:4 * n + 4, :], x_all[:, 4 * n:4 * n + 4, :]).then_inc(stored, 16)
            sp.wait_ge(stored, 64)

        @block.gpsimd
        def _(pool):
            chain = Chain(pool, "pool_chain")

            def do(ins):
                chain.add(ins)
                chain.wait()

            def tri(t, op, fill, base=0):
                return pool.affine_select(out=t[:], in_=t[:], compare_op=op, fill=fill, base=base,
                                          pattern=[[-1, P]], channel_multiplier=1)

            def powers(ready, done, turn):
                wait_apart(pool, "pool", ready, turn + 1)
                do(pool.tensor_scalar(vpe[:], mv[:, :, 1], EPS, None, ALU.add))
                pool.tensor_tensor(rstd[:], vpe[:], mhalf[:], ALU.pow).then_inc(done, 1)

            do(pool.memset(zeros[:], 0.0))
            do(pool.memset(wo_s[:], 0.0))
            pool.sem_inc(ready_zero, 1)
            do(pool.memset(ident[:], 0.0))
            do(tri(ident, ALU.not_equal, 1.0))
            do(pool.memset(identb[:], 0.0))
            do(tri(identb, ALU.not_equal, 1.0))
            pool.sem_inc(ready_const, 1)
            do(pool.memset(kx[:], 0.0))
            pool.sem_inc(ready_zero, 1)
            do(pool.memset(mhalf[:], -0.5))
            with pool.Fori(0, NCH) as c:
                chain.turn(c, 1)
                powers(var_ready, rstd_ready, c)
            chain.turned(NCH)
            do(pool.memset(maskq[:], 0.0))
            do(tri(maskq, ALU.is_ge, NEG))
            do(pool.memset(maskk[:], NEG))
            do(tri(maskk, ALU.is_gt, 0.0))
            do(pool.memset(before[:], 0.0))
            do(tri(before, ALU.is_ge, 1.0))
            do(pool.memset(onesb[:], 1.0))
            do(pool.memset(vx[:], 0.0))
            do(pool.memset(nmax[:], 0.0))
            for s in range(2):
                do(pool.memset(vp[s][:, :, :, HD:VW], 1.0))
            for done in (hi_out, mid_out, lo_out):
                pool.wait_ge(done, 32 * (NCH + 1))
            pool.wait_ge(v_taken, NCH + 1)
            for s in range(2):
                do(pool.memset(kst[s][KROWS:KROWS_M, :, :], 1.0))
            pool.sem_inc(ready_zero, 1)

            pool.wait_ge(in_rest, 16 * (5 + GH))
            pool.wait_ge(xn_ready, NCH)
            for k in range(NBLK):
                ins = pool.tensor_tensor(x_all[:, k, :], x_all[:, k, :], bo_s[:], ALU.add)
                chain.add(ins)
            chain.wait()
            pool.sem_inc(bo_added, 1)

            def copy_values(g, s):
                src = v_all[:].rearrange("p b g k n -> p (b g) k n")[:, bass.ds(g, 1)].rearrange("p o k (h d) -> p (o k) h d", h=GH)
                pool.tensor_copy(vp[s][:, :, :, 0:HD], src).then_inc(vp_ready[s], 1)

            pool.wait_ge(v_taken, NCH + 1)
            copy_values(0, 0)
            copy_values(1, 1)
            with pool.Fori(1, NG // 2) as i:
                for s in range(2):
                    pool.wait_ge(pv_done, i * (2 * NST) + ((s - 1) * NST + 2))
                    copy_values(i * 2 + s, s)

            pool.wait_ge(o_taken, 2 * NG + 1)
            do(pool.memset(px[:], 0.0))
            pool.sem_inc(vx_free, 1)
            with pool.Fori(0, B) as b:
                with pool.Fori(0, S // CT) as cc:
                    c = b * 2 + cc
                    chain.turn(c, 2 + CB)
                    src = yT[:, bass.ds(b * GH, GH), bass.ds(cc * CT, CT)]
                    pool.tensor_copy(yc[:], src).then_inc(yc_ready, 1)
                    powers(var2_ready, rstd2_ready, c * 2)
                    pool.wait_ge(xn2_ready, c + 1)
                    for k in range(CB):
                        chain.add(pool.tensor_tensor(x_all[:, bass.ds(c * CB + k, 1), :].rearrange("p o c -> p (o c)"),
                                                     x_all[:, bass.ds(c * CB + k, 1), :].rearrange("p o c -> p (o c)"), box_s[:], ALU.add))
                    chain.wait()
                    pool.sem_inc(box_added, 1)
                    powers(var2_ready, rstd2_ready, c * 2 + 1)
            chain.turned(NCH)

            pool.wait_ge(ox_act, NCH * PAIRS // 2)
            pool.wait_ge(ox_dve, NCH * PAIRS // 2)
            do(pool.iota(em99[:], [[1, E]], base=-99, channel_multiplier=0, allow_small_or_imprecise_dtypes=True))
            do(pool.iota(steps128[:], [[P, NBLK]], base=0, channel_multiplier=0, allow_small_or_imprecise_dtypes=True))
            do(pool.iota(tno[:], [[1, NT]], base=0, channel_multiplier=0, allow_small_or_imprecise_dtypes=True))
            do(pool.memset(ones_e[:], 1.0))
            pool.sem_inc(tno_ready, 1)
            pool.wait_ge(zero_rows, 16 * (NT + 1))
            pool.wait_ge(pos_ready, 1)
            for k in range(NBLK):
                pool.wait_ge(xs_ready, k + 1)
                pool.indirect_dma_start(out=xg_d, out_offset=bass.IndirectOffsetOnAxis(ap=pos[:, k:k + 1], axis=0),
                                        in_=xn_all[:, k, :], in_offset=None).then_inc(scattered, 16)
            pool.wait_ge(scattered, 16 * NBLK)
            for s in range(2):
                pool.wait_ge(yo_out[s], 16 * (NT // 2 + 1))
            for k in range(NBLK):
                pool.indirect_dma_start(out=xn_all[:, k, :], out_offset=None, in_=yg_d,
                                        in_offset=bass.IndirectOffsetOnAxis(ap=pos[:, k:k + 1], axis=0)).then_inc(gathered[k // 4], 16)

        @block.scalar
        def _(act):
            act.sem_inc(p_ready, S_SLOTS)
            act.sem_inc(qk_taken, 1)

            act.wait_ge(ready_zero, 2)
            for m in range(PAIRS):
                act.wait_ge(kx_ready, m + 1)
                act.copy(kx[0:XD, :, m, 0:SK], ps[0:XD, m % 4, 0:B * SK].rearrange("p (b k) -> p b k", b=B)).then_inc(kx_act, 1)
            for n in range(0, 8, 2):
                act.wait_ge(vc_ready, n + 1)
                act.copy(vtmp[:, n // 4, n // 2 % 2, 0:512], ps[0:SK // 2, 4 + n % 4, :]).then_inc(vc_act, 1)

            act.wait_ge(in_qkv, 96)
            act.wait_ge(vc_out, 16)
            with act.Fori(0, NCH) as c:
                act.wait_ge(t1_ready, c + 1)
                act.copy(xnT[:], ps[:, 0:2, :]).then_inc(xnT_ready, 1)
                act.wait_ge(qf_free, c + 1)
                act.wait_ge(hi_out, c * 32 + 32)
                for n in range(4):
                    act.wait_ge(qk_ready, c * 4 + (n + 1))
                    act.activation(qf[:, n, :], ps[:, 2 + n, :], ACT.Identity, bias=bqk[:, n:n + 1])
                    ins = act.activation(qp[:, 0, n, :], ps[:, 2 + n, :], ACT.Identity, bias=bqk[:, n:n + 1])
                ins.then_inc(hi_ready, 1)
                act.wait_ge(hi_ready, c + 1)
                act.sem_inc(qk_taken, 1)

            def exps(g, s, k):
                qc, kb = STEPS[k]
                n = (qc + 1) * CT - max(qc * CT, kb * P)
                act.wait_ge(pv_done, g * NST + (k + 1))
                for h in range(GH):
                    v = k * GH + h
                    act.wait_ge(s_ready, g * (NST * GH) + (v + 1))
                    act.activation(probs[:, v % P_SLOTS, 0:n], ps[:, 4 + v % S_SLOTS, 0:n], ACT.Exp, scale=SELF_SCALE).then_inc(p_ready, 1)

            for done in (hi_out, mid_out, lo_out):
                act.wait_ge(done, 32 * (NCH + 1))
            act.wait_ge(v_taken, NCH + 1)
            with act.Fori(0, NG // 2) as i:
                for s in range(2):
                    for k in range(NST):
                        exps(i * 2 + s, s, k)

            act.wait_ge(vx_free, 1)
            with act.Fori(0, NCH) as c:
                act.wait_ge(t2_ready, c + 1)
                act.copy(xnT[:], ps[:, 2:4, :]).then_inc(xnT2_ready, 1)
                for m in range(0, PAIRS, 2):
                    act.wait_ge(qx_ready, c * PAIRS + (m + 1))
                    act.activation(qT[:, m, :], ps[:, 4 + m % 4, :], ACT.Copy, scale=XSCALE).then_inc(qx_act, 1)
                for u in range(XU + PV_LAG + 2):
                    if u < XU:
                        if u >= 4:
                            act.wait_ge(tx_ready, c * XU + (u - 3))
                        act.wait_ge(mx_ready, c * XU + (u + 1))
                        for h in range(2):
                            ins = act.activation(px[:, u % 4, SK * h:SK * h + SK], ps[:, (0, 1, 4, 5)[u % 4], SK * h:SK * h + SK], ACT.Exp,
                                                 bias=nmx[:, u % 4, h:h + 1], accum_out=smx[:, u % 4, h:h + 1])
                        ins.then_inc(ex_ready, 1)
                    w = u - T_LAG - 1
                    if 0 <= w < XU and w % 2 == 0:
                        act.wait_ge(tx_ready, c * XU + (w + 1))
                        if w // CB >= 2:
                            act.wait_ge(ox_ready, c * PAIRS + (w // CB - 1))
                        act.copy(pT[0:KC, w // CB % 2, :, w % CB * P:(w % CB + 1) * P],
                                 ps[0:KC, 6, 0:NKC * P].rearrange("p (c q) -> p c q", c=NKC)).then_inc(tx_act, 1)
                    w = u - PV_LAG - 1
                    if w % CB == CB - 1 and w > 0 and w // CB % 2 == 0 and w // CB < PAIRS:
                        act.wait_ge(ox_ready, c * PAIRS + (w // CB + 1))
                        act.copy(qT[:, w // CB, :], ps[:, 2, :]).then_inc(ox_act, 1)
                act.wait_ge(t3_ready, c + 1)
                act.copy(xnT[:], ps[:, 2:4, :]).then_inc(xnT3_ready, 1)

            act.wait_ge(mxl_ready, 1)
            act.activation(emx[:], mx[:], ACT.Exp, scale=-1.0).then_inc(exp_ready, 1)

            with act.Fori(0, NCH) as c:
                for m in range(FF):
                    act.wait_ge(gs_ready, c * FF + (m + 1))
                    act.wait_ge(hs_ready, c * FF + (m + 1))
                    act.activation(sgl[:], ps[:, 2, :], ACT.Silu).then_inc(gs_silu, 1)

            for s in range(2):
                act.sem_inc(yo_out[s], 16)

            def put_rows(t, s, i1):
                act.wait_ge(de_ready, t + 1)
                act.wait_ge(yo_out[s], i1 * 16)
                act.copy(yo[s][:], ps[:, 6 + s, 0:C]).then_inc(yo_ready, 1)
                dst = yg_d.rearrange("(t p) c -> t p c", p=P)[bass.ds(t, 1)].rearrange("o p c -> (o p) c")
                act.wait_ge(yo_ready, t + 1)
                act.dma_start(dst, yo[s][:]).then_inc(yo_out[s], 16)

            def silu(t, s):
                act.wait_ge(ge_ready, t + 1)
                act.activation(act_s[s][:], ps[:, 2 + 2 * s, :].rearrange("p (f q) -> p f q", f=FF), ACT.Silu).then_inc(silu_ready, 1)

            silu(0, 0)
            with act.Fori(0, NT // 2 - 1) as i:
                silu(i * 2 + 1, 1)
                put_rows(i * 2, 0, i + 1)
                silu(i * 2 + 2, 0)
                put_rows(i * 2 + 1, 1, i + 1)
            silu(NT - 1, 1)
            put_rows(NT - 2, 0, NT // 2)
            put_rows(NT - 1, 1, NT // 2)

        @block.tensor
        def _(pe):
            def mm(out_, lhsT, rhs, start, stop):
                return pe.matmul(out_, lhsT, rhs, start=start, stop=stop, skip_group_check=True)

            pe.wait_ge(in_ctx, 48)
            for m in range(PAIRS):
                if m >= 4:
                    pe.wait_ge(kx_act, m - 3)
                    pe.wait_ge(kx_dve, m - 3)
                for t in range(2):
                    ins = mm(ps[:, m % 4, 0:B * SK], wkx_s[:, t, m * P:(m + 1) * P], ctx_s[:, t, :], t == 0, t == 1)
                ins.then_inc(kx_ready, 1)
            for n in range(8):
                b, k, half = n // 4, n // 2 % 2, n % 2
                if n >= 4:
                    pe.wait_ge((vc_act, vc_dve)[n % 2], (n - 4) // 2 + 1)
                r0 = b * SK + k * (SK // 2)
                for t in range(2):
                    ins = mm(ps[0:SK // 2, 4 + n % 4, :], ctx_s[:, t, r0:r0 + SK // 2], wvx_s[:, t, half * 512:half * 512 + 512], t == 0, t == 1)
                ins.then_inc(vc_ready, 1)

            def turn_rows(src, bank, done):
                for k in range(CB):
                    for f in range(FC):
                        ins = pe.transpose(ps[:, bank + f, k * P:(k + 1) * P], src(k, f), ident[:])
                ins.then_inc(done, 1)

            pe.wait_ge(ready_const, 1)
            pe.wait_ge(in_qkv, 96)
            pe.wait_ge(vc_act, 4)
            pe.wait_ge(vc_dve, 4)
            pe.wait_ge(kx_act, PAIRS)
            pe.wait_ge(kx_dve, PAIRS)
            for c in range(NCH):
                pe.wait_ge(xn_ready, c + 1)
                turn_rows(lambda k, f: xn_all[:, c * CB + k, f * P:(f + 1) * P], 0, t1_ready)
                pe.wait_ge(xnT_ready, c + 1)
                pe.wait_ge(qk_taken, c + 1)
                for n in range(4):
                    for f in range(FC):
                        ins = mm(ps[:, 2 + n, :], wqkv[:, f, n // 2, n % 2 * P:(n % 2 + 1) * P], xnT[:, f, :], f == 0, f == FC - 1)
                    ins.then_inc(qk_ready, 1)
                pe.wait_ge(v_taken, c + 1)
                for k in range(CB):
                    for f in range(FC):
                        ins = mm(ps[:, 6 + k // 2, k % 2 * C:(k % 2 + 1) * C], xnT[:, f, k * P:(k + 1) * P], wqkv[:, f, 2, :], f == 0, f == FC - 1)
                ins.then_inc(v_ready, 1)

            def max_unit(g, s, u):
                h, qb = UNITS[u]
                keys = (qb + 1) * P
                slot = 2 * (u % 2)
                pe.wait_ge(max_taken, g * NU + (u + 1))
                lhsT = qst[s][0:KROWS, h, qb * P:(qb + 1) * P]
                for k0 in range(0, keys, 512):
                    n = min(512, keys - k0)
                    mm(ps[:, slot + k0 // 512, 0:n], lhsT, kst[s][0:KROWS, h, k0:k0 + n], True, False)
                d = qb * P
                mm(ps[:, slot + d // 512, d % 512:d % 512 + P], identb[:], maskq[:], False, True).then_inc(max_ready, 1)

            def turn_max(g):
                pe.wait_ge(max_taken, g * NU + (NU + 2))
                pe.transpose(ps[:, 0, 0:P], nmax[:], ident[:]).then_inc(nmT_ready, 1)

            def scores(g, s, k):
                qc, kb = STEPS[k]
                q0 = max(qc * CT, kb * P)
                n = (qc + 1) * CT - q0
                for h in range(GH):
                    v = k * GH + h
                    bank = 4 + v % S_SLOTS
                    pe.wait_ge(p_ready, g * (NST * GH) + (v + 1))
                    ins = mm(ps[:, bank, 0:n], kst[s][0:KROWS_M, h, kb * P:(kb + 1) * P], qst[s][0:KROWS_M, h, q0:q0 + n], True, False)
                    if kb * P >= qc * CT:
                        ins = mm(ps[:, bank, 0:P], identb[:], maskk[:], False, True)
                    ins.then_inc(s_ready, 1)

            def values(g, s, k):
                qc, kb = STEPS[k]
                q0 = max(qc * CT, kb * P)
                n = (qc + 1) * CT - q0
                last_kb = (qc + 1) * CB - 1
                if kb == 0:
                    pe.wait_ge(o_taken, g * 2 + (qc + 1))
                pe.wait_ge(p_ready, g * (NST * GH) + (k * GH + GH + S_SLOTS))
                for h in range(GH):
                    ins = mm(ps[VW * h:VW * h + VW, 7, q0 - qc * CT:CT], vp[s][:, kb, h, :], probs[:, (k * GH + h) % P_SLOTS, 0:n],
                             kb == 0, kb == last_kb)
                ins.then_inc(pv_done, 1)

            pe.wait_ge(ready_zero, 3)
            pe.wait_ge(v_taken, NCH + 1)
            pe.wait_ge(qk_taken, NCH + 1)
            pe.wait_ge(q_in[0], 16 * 2 * NPROD)
            for u in range(NU):
                max_unit(0, 0, u)
            turn_max(0)

            def group(g, s, nth, nth_next, lookahead):
                pe.wait_ge(vp_ready[s], nth)
                pe.wait_ge(shift_in[s], nth * 48)
                for k in range(NST):
                    scores(g, s, k)
                    if lookahead and k in UNIT_STEPS:
                        if k == UNIT_STEPS[0]:
                            pe.wait_ge(q_in[1 - s], nth_next * (16 * 2 * NPROD))
                        for u in range((k - UNIT_STEPS[0]) * GH, (k - UNIT_STEPS[0] + 1) * GH):
                            max_unit(g + 1, 1 - s, u)
                    if lookahead and k == SPLIT_STEP:
                        turn_max(g + 1)
                    if k >= 1:
                        values(g, s, k - 1)
                values(g, s, NST - 1)

            with pe.Fori(0, NG // 2 - 1) as i:
                group(i * 2, 0, i + 1, i + 1, True)
                group(i * 2 + 1, 1, i + 1, i + 2, True)
            group(NG - 2, 0, NG // 2, NG // 2, True)
            group(NG - 1, 1, NG // 2, None, False)

            pe.wait_ge(in_rest, 16 * (5 + GH))
            pe.wait_ge(o_taken, 2 * NG + 1)
            with pe.Fori(0, B) as b:
                wait_apart(pe, "pe", vx_in, b * 64 + 64)
                with pe.Fori(0, S // CT) as cc:
                    c = b * 2 + cc
                    pe.wait_ge(lg_taken, c + 1)
                    pe.wait_ge(yc_ready, c + 1)
                    for k in range(CB):
                        for g in range(GH):
                            ins = mm(ps[:, k // 2, k % 2 * C:(k % 2 + 1) * C], yc[:, g, k * P:(k + 1) * P], wo_s[:, g, :], g == 0, g == GH - 1)
                    ins.then_inc(wo_done, 1)
                    pe.wait_ge(xn2_ready, c + 1)
                    turn_rows(lambda k, f: xn2[:, k, f * P:(f + 1) * P], 2, t2_ready)
                    pe.wait_ge(xnT2_ready, c + 1)
                    for m in range(PAIRS):
                        if m >= 4:
                            pe.wait_ge((qx_act, qx_dve)[m % 2], c * (PAIRS // 2) + ((m - 4) // 2 + 1))
                        for f in range(FC):
                            ins = mm(ps[:, 4 + m % 4, :], wqx_s[:, f, m * P:(m + 1) * P], xnT[:, f, :], f == 0, f == FC - 1)
                        ins.then_inc(qx_ready, 1)
                    pe.wait_ge(qx_act, c * (PAIRS // 2) + PAIRS // 2)
                    pe.wait_ge(qx_dve, c * (PAIRS // 2) + PAIRS // 2)
                    for u in range(XU + PV_LAG + 1):
                        if u < XU:
                            pair, k = u // CB, u % CB
                            if u >= 4:
                                pe.wait_ge(ex_ready, c * XU + (u - 3))
                            mm(ps[:, (0, 1, 4, 5)[u % 4], 0:PK], qT[:, pair, k * P:(k + 1) * P],
                               kx[:, bass.ds(b, 1), pair, :].rearrange("p o k -> p (o k)"), True, True).then_inc(sx_ready, 1)
                        w = u - T_LAG
                        if 0 <= w < XU:
                            pe.wait_ge(px_ready, c * XU + (w + 1))
                            if w >= 2:
                                pe.wait_ge((tx_act, tx_dve)[w % 2], c * (XU // 2) + w // 2)
                            for j in range(NKC):
                                ins = pe.transpose(ps[0:KC, 6 + w % 2, j * P:(j + 1) * P], px[:, w % 4, j * KC:(j + 1) * KC], ident[:])
                            ins.then_inc(tx_ready, 1)
                        w = u - PV_LAG
                        if w % CB == CB - 1 and w > 0:
                            pair = w // CB
                            pe.wait_ge(tx_act, c * (XU // 2) + 2 * (pair + 1))
                            pe.wait_ge(tx_dve, c * (XU // 2) + 2 * (pair + 1))
                            if pair >= 2:
                                pe.wait_ge((ox_act, ox_dve)[pair % 2], c * (PAIRS // 2) + pair // 2)
                            for j in range(NKC):
                                ins = mm(ps[:, 2 + pair % 2, :], vx[0:KC, pair, j, :], pT[0:KC, pair % 2, j, :], j == 0, j == NKC - 1)
                            ins.then_inc(ox_ready, 1)
                    pe.wait_ge(ox_act, c * (PAIRS // 2) + PAIRS // 2)
                    pe.wait_ge(ox_dve, c * (PAIRS // 2) + PAIRS // 2)
                    for k in range(CB):
                        for m in range(PAIRS):
                            ins = mm(ps[:, k // 2, k % 2 * C:(k % 2 + 1) * C], qT[:, m, k * P:(k + 1) * P], wox_s[:, m, :], m == 0, m == PAIRS - 1)
                    ins.then_inc(wox_done, 1)
                    pe.wait_ge(xn3_ready, c + 1)
                    turn_rows(lambda k, f: xn2[:, k, f * P:(f + 1) * P], 2, t3_ready)
                    pe.wait_ge(xnT3_ready, c + 1)
                    for k in range(CB):
                        for f in range(FC):
                            ins = mm(ps[:, 0, k * E:(k + 1) * E], xnT[:, f, k * P:(k + 1) * P], wr_s[:, f, :], f == 0, f == FC - 1)
                    ins.then_inc(lg_ready, 1)
                pe.wait_ge(ox_dve, c * (PAIRS // 2) + PAIRS // 2)
                pe.sem_inc(vx_free, 1)

            pe.wait_ge(oh_ready, 1)
            mm(ps[:, 0, 0:NBLK * E], before[:], onehotb[:], True, False)
            for k in range(NBLK - 1):
                n = NBLK - 1 - k
                mm(ps[:, 0, (k + 1) * E:NBLK * E], onesb[:], onehotb[:, k:k + 1, :].to_broadcast((P, n, E)), False, k == NBLK - 2)
            for k in range(NBLK):
                ins = mm(ps[:, 1, 0:E], onesb[:], onehotb[:, k, :], k == 0, k == NBLK - 1)
            ins.then_inc(rank_ready, 1)

            pe.wait_ge(in_shared, 48)
            with pe.Fori(0, NCH) as c:
                for m in range(FF):
                    pe.wait_ge(gs_silu, c * FF + (m + 1))
                    for f in range(FC):
                        ins = mm(ps[:, 2, :], wsg_s[:, f, m * P:(m + 1) * P], xnT_all[:, f, bass.ds(c * CT, CT)], f == 0, f == FC - 1)
                    ins.then_inc(gs_ready, 1)
                    pe.wait_ge(us_taken, c * FF + (m + 1))
                    for f in range(FC):
                        ins = mm(ps[:, 3, :], wsu_s[:, f, m * P:(m + 1) * P], xnT_all[:, f, bass.ds(c * CT, CT)], f == 0, f == FC - 1)
                    ins.then_inc(us_ready, 1)
                pe.wait_ge(us_taken, c * FF + (FF + 1))
                pe.wait_ge(ds_taken, c + 1)
                for k in range(CB):
                    for m in range(FF):
                        ins = mm(ps[:, 4 + k // 2, k % 2 * C:(k % 2 + 1) * C], shT[:, m, k * P:(k + 1) * P], wsd_s[:, m, :], m == 0, m == FF - 1)
                ins.then_inc(ds_ready, 1)

            def turn_tile(t, s, i1):
                pe.wait_ge(xg_in[s], i1 * 16)
                for f in range(FC):
                    ins = pe.transpose(ps[:, s, f * P:(f + 1) * P], xg[s][:, f * P:(f + 1) * P], ident[:])
                ins.then_inc(te_ready, 1)

            def gate_up(t, s, i1):
                pe.wait_ge(w_in[s], i1 * 32)
                pe.wait_ge(xgT_ready, t + 1)
                for half, done in ((0, ge_ready), (1, ue_ready)):
                    for m in range(FF):
                        for f in range(FC):
                            ins = mm(ps[:, 2 + 2 * s + half, m * P:(m + 1) * P], wgu_s[s][:, f, half * F + m * P:half * F + (m + 1) * P],
                                     xgT[s][:, f, :], f == 0, f == FC - 1)
                    ins.then_inc(done, 1)

            def down(t, s):
                pe.wait_ge(he_ready, t + 1)
                for m in range(FF):
                    ins = mm(ps[:, 6 + s, 0:C], hT[s][:, m, :], wdn_s[s][:, m, :], m == 0, m == FF - 1)
                ins.then_inc(de_ready, 1)
                pe.wait_ge(de_ready, t + 1)
                pe.sem_inc(w_free[s], 1)

            pe.wait_ge(ds_taken, NCH + 1)
            for s in range(2):
                pe.sem_inc(w_free[s], 1)
            turn_tile(0, 0, 1)
            gate_up(0, 0, 1)
            turn_tile(1, 1, 1)
            with pe.Fori(0, NT // 2 - 1) as i:
                gate_up(i * 2 + 1, 1, i + 1)
                down(i * 2, 0)
                turn_tile(i * 2 + 2, 0, i + 2)
                gate_up(i * 2 + 2, 0, i + 2)
                down(i * 2 + 1, 1)
                turn_tile(i * 2 + 3, 1, i + 2)
            gate_up(NT - 1, 1, NT // 2)
            down(NT - 2, 0)
            down(NT - 1, 1)

        @block.vector
        def _(dve):
            chain = Chain(dve, "dve_chain")

            def do(ins):
                chain.add(ins)
                chain.wait()

            def norm(block_of, out_of, var, rst, done, turn):
                for k in range(CB):
                    ins = dve.bn_stats(stats[:, k, :], block_of(k))
                    chain.add(ins)
                chain.wait_apart("dve")
                for k in range(CB):
                    ins = dve.bn_aggr(mv[:, k, :], stats[:, k, :])
                ins.then_inc(var, 1)
                dve.wait_ge(rst, turn + 1)
                for k in range(CB):
                    for o in out_of(k):
                        ins = dve.tensor_scalar(o, block_of(k), mv[:, k, 0:1], rstd[:, k:k + 1], ALU.subtract, ALU.mult)
                ins.then_inc(done, 1)

            dve.sem_inc(v_taken, 1)
            dve.sem_inc(qf_free, 1)
            dve.sem_inc(max_taken, 2)
            dve.sem_inc(pv_done, 2)
            dve.sem_inc(o_taken, 1)
            dve.sem_inc(lg_taken, 1)

            dve.wait_ge(ready_zero, 2)
            for m in range(PAIRS):
                dve.wait_ge(kx_ready, m + 1)
                dve.tensor_copy(kx[XD:P, :, m, SK:PK], ps[XD:P, m % 4, 0:B * SK].rearrange("p (b k) -> p b k", b=B)).then_inc(kx_dve, 1)
            for n in range(1, 8, 2):
                dve.wait_ge(vc_ready, n + 1)
                dve.tensor_copy(vtmp[:, n // 4, n // 2 % 2, 512:1024], ps[0:SK // 2, 4 + n % 4, :]).then_inc(vc_dve, 1)

            dve.wait_ge(in_x, 16)
            with dve.Fori(0, NCH) as c:
                chain.turn(c, CB)
                norm(lambda k: x_all[:, bass.ds(c * CB + k, 1), :].rearrange("p o c -> p (o c)"),
                     lambda k: [xn_all[:, bass.ds(c * CB + k, 1), :].rearrange("p o c -> p (o c)")],
                     var_ready, rstd_ready, xn_ready, c)
            chain.turned(NCH)
            dve.wait_ge(in_qkv, 96)
            with dve.Fori(0, B) as b:
                with dve.Fori(0, S // CT) as cc:
                    c = b * 2 + cc
                    dve.wait_ge(hi_ready, c + 1)
                    chain.turn(c, 1)
                    do(dve.tensor_tensor(qr[:], qf[:], qp[:, 0], ALU.subtract))
                    dve.sem_inc(qf_free, 1)
                    dve.wait_ge(mid_out, c * 32 + 32)
                    dve.tensor_copy(qp[:, 1], qr[:]).then_inc(mid_ready, 1)
                    dve.wait_ge(mid_ready, c + 1)
                    dve.wait_ge(lo_out, c * 32 + 32)
                    dve.tensor_tensor(qp[:, 2], qr[:], qp[:, 1], ALU.subtract).then_inc(lo_ready, 1)
                    dve.wait_ge(v_ready, c + 1)
                    for k in range(CB):
                        ins = dve.tensor_tensor(v_all[:, bass.ds(b, 1), :, bass.ds(cc * CB + k, 1), :].rearrange("p o g q n -> p (o g) (q n)"),
                                                ps[:, 6 + k // 2, k % 2 * C:(k % 2 + 1) * C].rearrange("p (g n) -> p g n", g=GH),
                                                bv_s[:].rearrange("p (g n) -> p g n", g=GH), ALU.add)
                    ins.then_inc(v_taken, 1)
                    dve.wait_ge(lo_ready, c + 1)
            chain.turned(NCH)

            def take_max(g, u):
                h, qb = UNITS[u]
                slot = 2 * (u % 2)
                keys = (qb + 1) * P
                dve.wait_ge(max_ready, g * NU + (u + 1))
                dve.tensor_reduce(nmax[:, u:u + 1], ps[:, slot:slot + 2, :].rearrange("p a n -> p (a n)")[:, 0:keys], AX.X, ALU.max,
                                  negate=True).then_inc(max_taken, 1)

            def split_max(g):
                dve.wait_ge(nmT_ready, g + 1)
                t = ps[0:NU, 0, 0:P]
                do(dve.tensor_copy(nmp[:, 0, :], t))
                do(dve.tensor_tensor(nmr[:], t, nmp[:, 0, :], ALU.subtract))
                do(dve.tensor_copy(nmp[:, 1, :], nmr[:]))
                dve.tensor_tensor(nmp[:, 2, :], nmr[:], nmp[:, 1, :], ALU.subtract).then_inc(shift_ready, 1)

            def take_output(g, qc):
                wait_apart(dve, "dve", pv_done, g * NST + ((CB, NST)[qc] + 2))
                do(dve.stream_shuffle(sums[:], ps[:, 7, :], [HD] * VW))
                do(dve.reciprocal(sums[:], sums[:]))
                dve.tensor_tensor(yT[:, bass.ds(g, 1), qc * CT:(qc + 1) * CT].rearrange("p o t -> p (o t)"), ps[:, 7, :], sums[:], ALU.mult).then_inc(o_taken, 1)

            def group(g, lookahead):
                for k in range(NST):
                    if lookahead and k in UNIT_STEPS:
                        for u in range((k - UNIT_STEPS[0]) * GH, (k - UNIT_STEPS[0] + 1) * GH):
                            take_max(g + 1, u)
                    if lookahead and k == SPLIT_STEP:
                        split_max(g + 1)
                    if k == CB:
                        take_output(g, 0)
                take_output(g, 1)

            dve.wait_ge(ready_zero, 3)
            for u in range(NU):
                take_max(0, u)
            split_max(0)
            with dve.Fori(0, NG // 2 - 1) as i:
                chain.turn(i, 14)
                group(i * 2, True)
                group(i * 2 + 1, True)
            chain.turned(NG // 2 - 1)
            group(NG - 2, True)
            group(NG - 1, False)

            dve.wait_ge(bo_added, 1)
            dve.wait_ge(vx_free, 1)
            with dve.Fori(0, NCH) as c:
                chain.turn(c, 2 * CB + 2 + XU)
                def rows(k):
                    return x_all[:, bass.ds(c * CB + k, 1), :].rearrange("p o c -> p (o c)")
                xc = x_all[:, bass.ds(c * CB, CB), :]
                dve.wait_ge(wo_done, c + 1)
                chain.add(dve.tensor_tensor(xc, xc, ps[:, 0:2, :].rearrange("p a (k c) -> p (a k) c", k=2), ALU.add))
                chain.wait_apart("dve")
                norm(rows, lambda k: [xn2[:, k, :]], var2_ready, rstd2_ready, xn2_ready, c * 2)
                for m in range(1, PAIRS, 2):
                    dve.wait_ge(qx_ready, c * PAIRS + (m + 1))
                    dve.tensor_scalar(qT[:, m, :], ps[:, 4 + m % 4, :], XSCALE, None, ALU.mult).then_inc(qx_dve, 1)
                for u in range(XU + PV_LAG + 2):
                    if u < XU:
                        dve.wait_ge(sx_ready, c * XU + (u + 1))
                        dve.tensor_reduce(nmx[:, u % 4, :], ps[:, (0, 1, 4, 5)[u % 4], 0:PK].rearrange("p (h k) -> p h k", h=2), AX.X, ALU.max,
                                          negate=True).then_inc(mx_ready, 1)
                    w = u - 1
                    if 0 <= w < XU:
                        dve.wait_ge(ex_ready, c * XU + (w + 1))
                        do(dve.reciprocal(rsx[:, w % 4, :], smx[:, w % 4, :]))
                        for h in range(2):
                            pp = px[:, w % 4, SK * h:SK * h + SK]
                            ins = dve.tensor_scalar(pp, pp, rsx[:, w % 4, h:h + 1], None, ALU.mult)
                        ins.then_inc(px_ready, 1)
                    w = u - T_LAG - 1
                    if 0 <= w < XU and w % 2 == 1:
                        dve.wait_ge(tx_ready, c * XU + (w + 1))
                        if w // CB >= 2:
                            dve.wait_ge(ox_ready, c * PAIRS + (w // CB - 1))
                        dve.tensor_copy(pT[0:KC, w // CB % 2, :, w % CB * P:(w % CB + 1) * P],
                                        ps[0:KC, 7, 0:NKC * P].rearrange("p (c q) -> p c q", c=NKC)).then_inc(tx_dve, 1)
                    w = u - PV_LAG - 1
                    if w % CB == CB - 1 and w > 0 and w // CB % 2 == 1 and w // CB < PAIRS:
                        dve.wait_ge(ox_ready, c * PAIRS + (w // CB + 1))
                        dve.tensor_copy(qT[:, w // CB, :], ps[:, 3, :]).then_inc(ox_dve, 1)
                dve.wait_ge(wox_done, c + 1)
                dve.wait_ge(box_added, c + 1)
                chain.add(dve.tensor_tensor(xc, xc, ps[:, 0:2, :].rearrange("p a (k c) -> p (a k) c", k=2), ALU.add))
                chain.wait_apart("dve")
                norm(rows, lambda k: [xn_all[:, bass.ds(c * CB + k, 1), :].rearrange("p o c -> p (o c)"), xn2[:, k, :]],
                     var2_ready, rstd2_ready, xn3_ready, c * 2 + 1)
                dve.wait_ge(xnT3_ready, c + 1)
                dve.tensor_copy(xnT_all[:, :, bass.ds(c * CT, CT)], ps[:, 2:4, :]).then_inc(t3_dve, 1)
                dve.wait_ge(lg_ready, c + 1)
                dve.tensor_copy(lg_all[:, bass.ds(c * CB, CB), :], ps[:, 0, 0:CB * E].rearrange("p (k e) -> p k e", e=E)).then_inc(lg_taken, 1)
            chain.turned(NCH)

            dve.wait_ge(tno_ready, 1)
            dve.wait_ge(lg_taken, NCH + 1)
            shape = (P, NBLK, E)

            def per_block(t):
                return t[:].rearrange("p (k o) -> p k o", o=1).to_broadcast(shape)

            def per_expert(t):
                return t[:].rearrange("p (o e) -> p o e", o=1).to_broadcast(shape)

            dve.tensor_reduce(mx[:], lg_all[:], AX.X, ALU.max).then_inc(mxl_ready, 1)
            dve.wait_ge(mxl_ready, 1)
            do(dve.tensor_tensor(cand[:], lg_all[:], per_block(mx), ALU.is_ge))
            do(dve.tensor_tensor(cand[:], cand[:], per_expert(em99), ALU.mult))
            do(dve.tensor_reduce(pick[:], cand[:], AX.X, ALU.min))
            do(dve.tensor_tensor(onehot[:], per_expert(em99), per_block(pick), ALU.is_equal))
            dve.tensor_copy(onehotb[:], onehot[:]).then_inc(oh_ready, 1)
            dve.wait_ge(exp_ready, 1)
            do(dve.tensor_scalar(score[:], emx[:], 1.0, None, ALU.add))
            do(dve.reciprocal(score[:], score[:]))
            for k in range(NBLK):
                dve.tensor_scalar(xn_all[:, k, :], xn_all[:, k, :], score[:, k:k + 1], None, ALU.mult).then_inc(xs_ready, 1)
            dve.wait_ge(rank_ready, 1)
            do(dve.tensor_tensor(over[:], ps[:, 1, 0:E].rearrange("p (e o) -> p e o", o=1).to_broadcast((P, E, NBLK)),
                                 steps128[:].rearrange("p (o k) -> p o k", o=1).to_broadcast((P, E, NBLK)), ALU.is_gt))
            do(dve.tensor_reduce(tiles[:], over[:], AX.X, ALU.add))
            do(dve.tensor_tensor_scan(ends[:], ones_e[:], tiles[:], 0.0, ALU.mult, ALU.add))
            do(dve.tensor_tensor(passed[:], ends[0:1, :].rearrange("p (o e) -> p o e", o=1).to_broadcast((1, NT, E)),
                                 tno[:].rearrange("p (t o) -> p t o", o=1).to_broadcast((1, NT, E)), ALU.is_le))
            do(dve.tensor_reduce(eotf[:], passed[:], AX.X, ALU.add))
            do(dve.tensor_scalar(eotf[:], eotf[:], float(E - 1), None, ALU.min))
            dve.tensor_copy(eot[:], eotf[:]).then_inc(eot_ready, 1)
            do(dve.tensor_tensor(base_t[:], ends[:], tiles[:], ALU.subtract))
            do(dve.tensor_scalar(base_t[:], base_t[:], float(P), None, ALU.mult))
            do(dve.tensor_tensor(cand[:], ps[:, 0, 0:NBLK * E].rearrange("p (k e) -> p k e", e=E), per_expert(base_t), ALU.add))
            do(dve.tensor_tensor(cand[:], cand[:], onehot[:], ALU.mult))
            do(dve.tensor_reduce(posf[:], cand[:], AX.X, ALU.add))
            dve.tensor_copy(pos[:], posf[:]).then_inc(pos_ready, 1)

            dve.sem_inc(hs_ready, 1)
            dve.sem_inc(us_taken, 1)
            dve.sem_inc(ds_taken, 1)
            dve.sem_inc(gs_silu, 1)
            with dve.Fori(0, NCH) as c:
                chain.turn(c, 1)
                for m in range(FF):
                    dve.wait_ge(gs_silu, c * FF + (m + 2))
                    dve.wait_ge(us_ready, c * FF + (m + 1))
                    dve.tensor_tensor(shT[:, m, :], sgl[:], ps[:, 3, :], ALU.mult).then_inc(us_taken, 1)
                    dve.wait_ge(us_taken, c * FF + (m + 2))
                    dve.sem_inc(hs_ready, 1)
                dve.wait_ge(ds_ready, c + 1)
                xc = x_all[:, bass.ds(c * CB, CB), :]
                do(dve.tensor_tensor(xc, xc, ps[:, 4:6, :].rearrange("p a (k c) -> p (a k) c", k=2), ALU.add))
                dve.sem_inc(ds_taken, 1)
            chain.turned(NCH)

            def take_rows(t, s):
                dve.wait_ge(te_ready, t + 1)
                dve.tensor_copy(xgT[s][:], ps[:, s, 0:C].rearrange("p (f q) -> p f q", f=FC)).then_inc(xgT_ready, 1)

            def gated(t, s):
                dve.wait_ge(silu_ready, t + 1)
                dve.wait_ge(ue_ready, t + 1)
                dve.tensor_tensor(hT[s][:], act_s[s][:], ps[:, 3 + 2 * s, :].rearrange("p (f q) -> p f q", f=FF), ALU.mult).then_inc(he_ready, 1)

            take_rows(0, 0)
            gated(0, 0)
            take_rows(1, 1)
            with dve.Fori(0, NT // 2 - 1) as i:
                gated(i * 2 + 1, 1)
                take_rows(i * 2 + 2, 0)
                gated(i * 2 + 2, 0)
                take_rows(i * 2 + 3, 1)
            gated(NT - 1, 1)

            for n in range(4):
                dve.wait_ge(gathered[n], 64)
                xc = x_all[:, 4 * n:4 * n + 4, :]
                dve.tensor_tensor(xc, xc, xn_all[:, 4 * n:4 * n + 4, :], ALU.add).then_inc(out_ready, 1)


_OUT = ("out_dram", (B, S, C))


def kernel(**inputs):
    import concourse.bacc as bacc
    from concourse.bass_utils import run_bass_kernel_spmd

    def a(name):
        return np.asarray(inputs[name])

    arrays = {
        "x": a("x"), "ctxT": a("ctx_768").transpose(2, 0, 1).reshape(CD, B * SK),
        "wq": a("L0_attn_Wq"), "bq": a("L0_attn_bq"), "wk": a("L0_attn_Wk"), "bk": a("L0_attn_bk"),
        "wv": a("L0_attn_Wv"), "bv": a("L0_attn_bv"), "wo": a("L0_attn_Wo"), "bo": a("L0_attn_bo"),
        "wqx": a("L0_xattn_w_q"), "wkx": a("L0_xattn_w_k"), "wvx": a("L0_xattn_w_v"), "wox": a("L0_xattn_w_o"), "box": a("L0_xattn_b_o"),
        "wr": a("L0_ffn_w_router").T, "wgu": a("L0_ffn_gate_up_proj"), "wdn": a("L0_ffn_down_proj"),
        "wsg": a("L0_ffn_w_gate").T, "wsu": a("L0_ffn_w_up").T, "wsd": a("L0_ffn_w_down").T,
    }
    arrays = {k: np.ascontiguousarray(v) for k, v in arrays.items()}
    nc = bacc.Bacc("TRN2", target_bir_lowering=False, num_devices=1)
    aps = {k: nc.dram_tensor(k + "_dram", v.shape, mybir.dt.from_np(v.dtype), kind="ExternalInput").ap() for k, v in arrays.items()}
    out = nc.dram_tensor(_OUT[0], _OUT[1], F32, kind="ExternalOutput").ap()
    build(nc, **aps, out=out)
    r = run_bass_kernel_spmd(nc, [{k + "_dram": v for k, v in arrays.items()}], core_ids=[0])
    return np.asarray(r.results[0][_OUT[0]])
```

```python
from contextlib import ExitStack

import numpy as np

import concourse.bass as bass
from concourse import mybir

F32 = mybir.dt.float32
BF16 = mybir.dt.bfloat16
U32 = mybir.dt.uint32
I32 = mybir.dt.int32
ALU = mybir.AluOpType
ACT = mybir.ActivationFunctionType
AX = mybir.AxisListType

P = 128
B, S, C = 2, 1024, 256
CB = 4
CT = CB * P
NCH = B * S // CT
FC = C // P
NBLK = B * S // P
EPS = 1e-5
NEG = -1.0e30

H, HD = 16, 16
GH = 4
NG = B * H // GH
VW = 32
SELF_SCALE = HD ** -0.5
Q_PART = (0, 0, 1, 0, 2, 1)
K_PART = (0, 1, 0, 2, 0, 1)
NPROD = len(Q_PART)
KROWS = NPROD * HD
KROWS_M = KROWS + 3
QB = S // P
STEPS = [(qc, kb) for qc in range(S // CT) for kb in range((qc + 1) * CB)]
NST = len(STEPS)
UNITS = [(h, qb) for h in range(GH) for n in range(QB // 2) for qb in (n, QB - 1 - n)]
NU = len(UNITS)
UNIT_STEPS = range(2, 2 + NU // GH)
SPLIT_STEP = UNIT_STEPS[-1] + 1
TURN_STEP = (CB + 1, 1)
TURNS = NU + 3
P_SLOTS, S_SLOTS = 8, 3

XH, XD = 16, 64
SK, CD = 154, 192
CK = CD // 2
PAIRS = XH // 2
PK = 2 * SK
KC = 103
NKC = 3
XI = XH * XD
XSCALE = XD ** -0.5
XU = PAIRS * CB
T_LAG, PV_LAG = 3, 5

E, F = 16, 512
FF = F // P
WS = 4
NT = 32


def bcast_rows(v):
    return v.rearrange("(o n) -> o n", o=1).to_broadcast((P, v.shape[0]))


def build(nc, x, ctxT, wq, bq, wk, bk, wv, bv, wo, bo, wqx, wkx, wvx, wox, box, wr, wgu, wdn, wsg, wsu, wsd, out):
    parts_d = nc.dram_tensor("qk_parts", (3, 2, B, C, S), BF16, kind="Internal").ap()
    vx_d = nc.dram_tensor("cross_values", (B, SK, XI), F32, kind="Internal").ap()
    xg_d = nc.dram_tensor("expert_rows_in", (NT * P, C), F32, kind="Internal").ap()
    yg_d = nc.dram_tensor("expert_rows_out", (NT * P, C), F32, kind="Internal").ap()

    with ExitStack() as ctx:
        def sb(name, shape, dt=F32, where=ctx):
            return where.enter_context(nc.sbuf_tensor(name, shape, dt))

        def sem(name):
            return ctx.enter_context(nc.semaphore(name))

        x_all = sb("x_all", [P, NBLK, C])
        ident = sb("ident", [P, P])
        identb = sb("identb", [P, P], BF16)
        maskq = sb("maskq", [P, P], BF16)
        maskk = sb("maskk", [P, P], BF16)
        before = sb("before", [P, P], BF16)
        onesb = sb("onesb", [P, P], BF16)
        xn_all = sb("xn_all", [P, NBLK, C])
        stats = sb("stats", [P, CB, 6])
        mv = sb("mv", [P, CB, 2])
        vpe = sb("vpe", [P, CB])
        rstd = sb("rstd", [P, CB])
        mhalf = sb("mhalf", [P, CB])
        xnT = sb("xnT", [P, FC, CT])
        wo_s = sb("wo_s", [P, FC, C])
        bo_s = sb("bo_s", [P, C])
        box_s = sb("box_s", [P, C])
        wr_s = sb("wr_s", [P, FC, E])
        zeros = sb("zeros", [P, C])

        with ExitStack() as attn:
            y_tok = sb("y_tok", [P, NG // 2, QB, 2 * GH * HD], F32, attn)
            kx = sb("kx", [P, B, PAIRS, PK], F32, attn)
            vx = sb("vx", [P, PAIRS, NKC, P], F32, attn)
            with ExitStack() as early:
                v_all = sb("v_all", [P, B, GH, QB, GH * HD], F32, early)
                vp = [sb(f"vp{s}", [P, QB, GH, VW], F32, early) for s in range(2)]
                nmax = sb("nmax", [P, P], F32, early)
                nmp = sb("nmp", [NU, 3, P], BF16, early)
                nmr = sb("nmr", [NU, P], F32, early)
                osb = sb("osb", [P, 2, CT], F32, early)
                rsum = sb("rsum", [P, 2, CB, GH, 1], F32, early)
                qst = [sb(f"qst{s}", [P, GH, S], BF16, early) for s in range(2)]
                kst = [sb(f"kst{s}", [P, GH, S], BF16, early) for s in range(2)]
                with ExitStack() as one:
                    wqkv = sb("wqkv", [P, FC, 3, C], F32, one)
                    bqk = sb("bqk", [P, 4], F32, one)
                    bv_s = sb("bv_s", [P, C], F32, one)
                    with ExitStack() as kv:
                        wkx_s = sb("wkx_s", [CK, 2, XI], F32, kv)
                        wvx_s = sb("wvx_s", [CK, 2, XI], F32, kv)
                        ctx_s = sb("ctx_s", [CK, 2, B * SK], F32, kv)
                        vtmp = sb("vtmp", [SK // 2, B, 2, XI], F32, kv)
                    with ExitStack() as proj:
                        qf = sb("qf", [P, 4, CT], F32, proj)
                        qr = sb("qr", [P, 4, CT], F32, proj)
                        qp = sb("qp", [P, 3, 4, CT], BF16, proj)
                with ExitStack() as two:
                    probs = sb("probs", [P, P_SLOTS, CT], F32, two)
            with ExitStack() as late:
                wqx_s = sb("wqx_s", [P, FC, XI], F32, late)
                wox_s = sb("wox_s", [P, PAIRS, C], F32, late)
                yT = [sb(f"yT{s}", [P, FC, CT], F32, late) for s in range(2)]
                qT = sb("qT", [P, PAIRS, CT], F32, late)
                px = sb("px", [P, 4, NKC * KC], F32, late)
                nmx = sb("nmx", [P, 4, 2], F32, late)
                smx = sb("smx", [P, 4, 2], F32, late)
                rsx = sb("rsx", [P, 4, 2], F32, late)
                pT = sb("pT", [P, 2, NKC, CT], F32, late)
                xnT_all = sb("xnT_all", [P, FC, B * S], F32, late)
                wsg_s = sb("wsg_s", [P, FC, F], F32, late)
                wsu_s = sb("wsu_s", [P, FC, F], F32, late)
                wsd_s = sb("wsd_s", [P, FF, C], F32, late)
        with ExitStack() as moe:
            sgl = sb("sgl", [P, CT], F32, moe)
            shT = sb("shT", [P, FF, CT], F32, moe)
            lg_all = sb("lg_all", [P, NBLK, E], F32, moe)
            mx = sb("mx", [P, NBLK], F32, moe)
            emx = sb("emx", [P, NBLK], F32, moe)
            score = sb("score", [P, NBLK], F32, moe)
            em99 = sb("em99", [P, E], F32, moe)
            cand = sb("cand", [P, NBLK, E], F32, moe)
            pick = sb("pick", [P, NBLK], F32, moe)
            onehot = sb("onehot", [P, NBLK, E], F32, moe)
            onehotb = sb("onehotb", [P, NBLK, E], BF16, moe)
            steps128 = sb("steps128", [P, NBLK], F32, moe)
            over = sb("over", [P, E, NBLK], F32, moe)
            tiles = sb("tiles", [P, E], F32, moe)
            ones_e = sb("ones_e", [P, E], F32, moe)
            ends = sb("ends", [P, E], F32, moe)
            base_t = sb("base", [P, E], F32, moe)
            posf = sb("posf", [P, NBLK], F32, moe)
            pos = sb("pos", [P, NBLK], U32, moe)
            tno = sb("tno", [1, NT], F32, moe)
            passed = sb("passed", [1, NT, E], F32, moe)
            eotf = sb("eotf", [1, NT], F32, moe)
            eot = sb("eot", [1, NT], I32, moe)
            act_s = [sb(f"act{s}", [P, FF, P], F32, moe) for s in range(2)]
            hT = [sb(f"hT{s}", [P, FF, P], F32, moe) for s in range(2)]
            yo = [sb(f"yo{s}", [P, C], F32, moe) for s in range(2)]
            xgT = [sb(f"xgT{s}", [P, FC, P], F32, moe) for s in range(2)]
            xg = [sb(f"xg{s}", [P, C], F32, moe) for s in range(WS)]
            wgu_s = [sb(f"wgu{s}", [P, FC, 2 * F], F32, moe) for s in range(WS)]
            wdn_s = [sb(f"wdn{s}", [P, FF, C], F32, moe) for s in range(WS)]

        ps = ctx.enter_context(nc.psum_tensor("ps", [P, 8, 512], F32))

        passed_wait = {e: sem(f"passed_{e}") for e in ("dve", "pool", "pe")}

        def wait_apart(eng, name, which, value):
            eng.wait_ge(which, value)
            eng.sem_inc(passed_wait[name], 1)

        class Use:

            def __init__(self, n, slot):
                self.n, self.slot = n, slot

        def use_before(j):
            return Use(j, j % 2)

        def units_of(k):
            return range((k - UNIT_STEPS[0]) * GH, (k - UNIT_STEPS[0] + 1) * GH)

        def use_of(g, s, what, u=0, last=False):
            before_out = (TURN_STEP[0] - UNIT_STEPS[0] + 1) * GH
            j = {"unit": u + (u >= before_out), "out0": before_out, "max": NU + 1, "out1": NU + 2}[what]
            if last:
                j = {"out0": 0, "out1": 1}[what]
            return Use(g * TURNS + (NU + 1 + j), (NU + 1 + s * TURNS + j) % 2)

        MT_ALL = NU + 1 + (NG - 1) * TURNS + 2 + 2

        class Chain:

            def __init__(self, eng, name):
                self.eng, self.sem, self.base, self.n = eng, sem(name), 0, 0

            def add(self, ins):
                ins.then_inc(self.sem, 1)
                self.n += 1

            def wait(self):
                self.eng.wait_ge(self.sem, self.base + self.n)

            def wait_apart(self, name):
                wait_apart(self.eng, name, self.sem, self.base + self.n)

            def turn(self, i, per):
                self.start, self.per = self.base + self.n, per
                self.base, self.n = i * per + self.start, 0

            def turned(self, turns):
                assert self.n == self.per, (self.n, self.per)
                self.base, self.n = self.start + turns * self.per, 0

        ready_const = sem("ready_const")
        ready_zero = sem("ready_zero")
        in_ctx, in_x, in_qkv, in_rest = sem("in_ctx"), sem("in_x"), sem("in_qkv"), sem("in_rest")
        in_cross, in_shared = sem("in_cross"), sem("in_shared")
        zero_rows = sem("zero_rows")
        kx_ready, kx_act, kx_dve = sem("kx_ready"), sem("kx_act"), sem("kx_dve")
        vc_ready, vc_act, vc_dve, vc_out = sem("vc_ready"), sem("vc_act"), sem("vc_dve"), sem("vc_out")
        var_ready, rstd_ready, xn_ready = sem("var_ready"), sem("rstd_ready"), sem("xn_ready")
        t1_ready, xnT_ready = sem("t1_ready"), sem("xnT_ready")
        qk_ready, qk_taken, hi_ready, v_ready, v_taken = sem("qk_ready"), sem("qk_taken"), sem("hi_ready"), sem("v_ready"), sem("v_taken")
        qf_free, mid_ready, lo_ready = sem("qf_free"), sem("mid_ready"), sem("lo_ready")
        hi_out, mid_out, lo_out = sem("hi_out"), sem("mid_out"), sem("lo_out")
        bo_added = sem("bo_added")
        q_in = [sem(f"stack_in{s}") for s in range(2)]
        vp_ready = [sem(f"vp_ready{s}") for s in range(2)]
        shift_in = [sem(f"shift_in{s}") for s in range(2)]
        m_ready, m_taken = sem("m_ready"), sem("m_taken")
        shift_ready = sem("shift_ready")
        s_ready, p_ready, pv_done, o_copied = sem("s_ready"), sem("p_ready"), sem("pv_done"), sem("o_copied")
        ty_ready, yT_ready, wo_done, xn2_ready, box_added = sem("ty_ready"), sem("yT_ready"), sem("wo_done"), sem("xn2_ready"), sem("box_added")
        t2_ready, xnT2_ready = sem("t2_ready"), sem("xnT2_ready")
        vx_free, vx_in = sem("vx_free"), sem("vx_in")
        t3_ready, xnT3_ready = sem("t3_ready"), sem("xnT3_ready")
        var2_ready, rstd2_ready = sem("var2_ready"), sem("rstd2_ready")
        qx_ready, qx_taken = sem("qx_ready"), sem("qx_taken")
        sx_ready, mx_ready, ex_ready, px_ready = sem("sx_ready"), sem("mx_ready"), sem("ex_ready"), sem("px_ready")
        tx_ready, tx_act, tx_dve = sem("tx_ready"), sem("tx_act"), sem("tx_dve")
        ox_ready, ox_act, ox_dve = sem("ox_ready"), sem("ox_act"), sem("ox_dve")
        wox_done, x2_ready, xn3_ready, lg_ready = sem("wox_done"), sem("x2_ready"), sem("xn3_ready"), sem("lg_ready")
        mxl_ready, exp_ready, oh_ready, rank_ready, tno_ready = sem("mxl_ready"), sem("exp_ready"), sem("oh_ready"), sem("rank_ready"), sem("tno_ready")
        xs_ready, pos_ready, eot_ready, scattered = sem("xs_ready"), sem("pos_ready"), sem("eot_ready"), sem("scattered")
        gs_ready, us_ready, gs_silu, hs_ready, us_taken, ds_ready, ds_taken = (sem(n) for n in ("gs_ready", "us_ready", "gs_silu", "hs_ready", "us_taken", "ds_ready", "ds_taken"))
        w_in = [sem(f"w_in{s}") for s in range(WS)]
        xg_in = [sem(f"xg_in{s}") for s in range(WS)]
        te_ready, xgT_ready, ge_ready, ue_ready, silu_ready, he_ready, de_ready, yo_ready = (sem(n) for n in ("te_ready", "xgT_ready", "ge_ready", "ue_ready", "silu_ready", "he_ready", "de_ready", "yo_ready"))
        yo_out = [sem(f"yo_out{s}") for s in range(2)]
        gathered = [sem(f"gathered{n}") for n in range(4)]
        out_ready, stored = sem("out_ready"), sem("stored")

        block = ctx.enter_context(nc.Block())

        @block.sync
        def _(sp):
            def rows(w):
                return w.rearrange("(t p) n -> p t n", p=P)

            def load_context_and_weights():
                sp.dma_start(ctx_s[:], ctxT.rearrange("(t p) n -> p t n", p=CK)).then_inc(in_ctx, 16)
                sp.dma_start(wkx_s[:], wkx.rearrange("(t p) n -> p t n", p=CK)).then_inc(in_ctx, 16)
                sp.dma_start(wvx_s[:], wvx.rearrange("(t p) n -> p t n", p=CK)).then_inc(in_ctx, 16)
                sp.dma_start(x_all[:], x.rearrange("b (k p) c -> p (b k) c", p=P)).then_inc(in_x, 16)
                for n, w in enumerate((wq, wk, wv)):
                    sp.dma_start(wqkv[:, :, n, :], rows(w)).then_inc(in_qkv, 16)
                for n, b_ in enumerate((bq, bk)):
                    sp.dma_start(bqk[:, 2 * n:2 * n + 2], b_.rearrange("(t p) -> p t", p=P), allow_slow_non_contiguous=True).then_inc(in_qkv, 16)
                sp.dma_start(bv_s[:], bcast_rows(bv)).then_inc(in_qkv, 16)
                sp.dma_start(bo_s[:], bcast_rows(bo)).then_inc(in_rest, 16)
                sp.dma_start(box_s[:], bcast_rows(box)).then_inc(in_rest, 16)
                sp.dma_start(wo_s[:], rows(wo)).then_inc(in_rest, 16)
                sp.dma_start(wr_s[:], rows(wr)).then_inc(in_rest, 16)
                sp.wait_ge(ready_zero, 1)
                for t in range(NT):
                    sp.dma_start(xg_d[t * P:(t + 1) * P, :], zeros[:]).then_inc(zero_rows, 16)

            def store_parts(b, cc):
                c = b * 2 + cc
                for j, (ready, done) in enumerate(((hi_ready, hi_out), (mid_ready, mid_out), (lo_ready, lo_out))):
                    for qk in range(2):
                        dst = parts_d[j, qk, bass.ds(b, 1), :, bass.ds(cc * CT, CT)].rearrange("o (m p) t -> p (o m) t", p=P)
                        if qk == 0:
                            sp.wait_ge(ready, c + 1)
                        sp.dma_start(dst, qp[:, j, 2 * qk:2 * qk + 2, :]).then_inc(done, 16)

            def load_stacks(g, s):
                for part, st, qk in ((Q_PART, qst, 0), (K_PART, kst, 1)):
                    for j in range(NPROD):
                        src = parts_d[part[j], qk].rearrange("b (g h d) t -> (b g) d h t", h=GH, d=HD)[bass.ds(g, 1)]
                        sp.dma_start(st[s][HD * j:HD * j + HD, :, :], src.rearrange("o d h t -> (o d) h t")).then_inc(q_in[s], 16)

            def load_shift(g, s):
                sp.wait_ge(shift_ready, g + 1)
                for j in range(3):
                    sp.dma_start(qst[s][KROWS + j:KROWS + j + 1, :, :].rearrange("o h (b q) -> o (h b) q", q=P),
                                 nmp[:, j, :]).then_inc(shift_in[s], 16)

            load_context_and_weights()
            sp.wait_ge(vc_act, 4)
            sp.wait_ge(vc_dve, 4)
            sp.dma_start(vx_d.rearrange("b (k p) n -> p b k n", p=SK // 2), vtmp[:]).then_inc(vc_out, 16)
            sp.sem_inc(hi_out, 32)
            sp.sem_inc(mid_out, 32)
            sp.sem_inc(lo_out, 32)
            store_parts(0, 0)
            store_parts(0, 1)
            for done in (hi_out, mid_out, lo_out):
                sp.wait_ge(done, 32 * (NCH // 2 + 1))
            load_stacks(0, 0)
            load_stacks(1, 1)
            store_parts(1, 0)
            store_parts(1, 1)
            for done in (hi_out, mid_out, lo_out):
                sp.wait_ge(done, 32 * (NCH + 1))
            load_shift(0, 0)
            load_shift(1, 1)
            with sp.Fori(1, NG // 2) as i:
                for s in range(2):
                    sp.wait_ge(s_ready, i * (2 * NST * GH) + (s - 1) * NST * GH)
                    load_stacks(i * 2 + s, s)
                    load_shift(i * 2 + s, s)

            sp.wait_ge(o_copied, 2 * NG + 1)
            sp.wait_ge(m_taken, MT_ALL)
            sp.dma_start(wqx_s[:], rows(wqx)).then_inc(in_cross, 16)
            sp.dma_start(wox_s[:], rows(wox)).then_inc(in_cross, 16)
            sp.dma_start(wsg_s[:], rows(wsg)).then_inc(in_shared, 16)
            sp.dma_start(wsu_s[:], rows(wsu)).then_inc(in_shared, 16)
            sp.dma_start(wsd_s[:], rows(wsd)).then_inc(in_shared, 16)
            sp.wait_ge(vc_out, 16)
            with sp.Fori(0, B) as b:
                sp.wait_ge(vx_free, b + 1)
                src = vx_d[bass.ds(b, 1)].rearrange("o k (m h d) -> (o k) m h d", m=PAIRS, h=2)
                r = 2 * KC - SK
                for rows_, c, h, k0 in (((0, KC), 0, 0, 0), ((0, SK - KC), 1, 0, KC), ((SK - KC, KC), 1, 1, 0),
                                        ((0, SK - r), 2, 1, r)):
                    n = rows_[1] - rows_[0]
                    sp.dma_start(vx[rows_[0]:rows_[1], :, c, XD * h:XD * h + XD], src[k0:k0 + n, :, h, :]).then_inc(vx_in, 16)
                del r

            sp.wait_ge(eot_ready, 1)
            sp.wait_ge(scattered, 16 * NBLK)
            def load_tile(t, s):
                e = sp.value_load(eot[0:1, bass.ds(t, 1)], min_val=0, max_val=E - 1)
                row = sp.snap(t)
                sp.dma_start(xg[s][:], xg_d.rearrange("(t p) c -> t p c", p=P)[bass.ds(row, 1)].rearrange("o p c -> (o p) c")).then_inc(xg_in[s], 16)
                sp.dma_start(wgu_s[s][:], wgu[bass.ds(e, 1)].rearrange("o (t p) n -> p (o t) n", p=P)).then_inc(w_in[s], 16)
                sp.dma_start(wdn_s[s][:], wdn[bass.ds(e, 1)].rearrange("o (t p) n -> p (o t) n", p=P)).then_inc(w_in[s], 16)

            for s in range(WS):
                load_tile(s, s)
            with sp.Fori(1, NT // WS) as i:
                for s in range(WS):
                    sp.wait_ge(de_ready, i * WS + (s + 1 - WS))
                    load_tile(i * WS + s, s)
            for n in range(4):
                sp.wait_ge(out_ready, n + 1)
                sp.dma_start(out.rearrange("b (k p) c -> p (b k) c", p=P)[:, 4 * n:4 * n + 4, :], x_all[:, 4 * n:4 * n + 4, :]).then_inc(stored, 16)
            sp.wait_ge(stored, 64)

        @block.gpsimd
        def _(pool):
            chain = Chain(pool, "pool_chain")

            def do(ins):
                chain.add(ins)
                chain.wait()

            def tri(t, op, fill, base=0):
                return pool.affine_select(out=t[:], in_=t[:], compare_op=op, fill=fill, base=base,
                                          pattern=[[-1, P]], channel_multiplier=1)

            def powers(ready, done, turn):
                wait_apart(pool, "pool", ready, turn + 1)
                do(pool.tensor_scalar(vpe[:], mv[:, :, 1], EPS, None, ALU.add))
                pool.tensor_tensor(rstd[:], vpe[:], mhalf[:], ALU.pow).then_inc(done, 1)

            do(pool.memset(zeros[:], 0.0))
            pool.sem_inc(ready_zero, 1)
            do(pool.memset(ident[:], 0.0))
            do(tri(ident, ALU.not_equal, 1.0))
            do(pool.memset(identb[:], 0.0))
            do(tri(identb, ALU.not_equal, 1.0))
            pool.sem_inc(ready_const, 1)
            do(pool.memset(kx[:], 0.0))
            pool.sem_inc(ready_zero, 1)
            do(pool.memset(mhalf[:], -0.5))
            with pool.Fori(0, NCH) as c:
                chain.turn(c, 1)
                powers(var_ready, rstd_ready, c)
            chain.turned(NCH)
            do(pool.memset(maskq[:], 0.0))
            do(tri(maskq, ALU.is_ge, NEG))
            do(pool.memset(maskk[:], NEG))
            do(tri(maskk, ALU.is_gt, 0.0))
            do(pool.memset(before[:], 0.0))
            do(tri(before, ALU.is_ge, 1.0))
            do(pool.memset(onesb[:], 1.0))
            do(pool.memset(vx[:], 0.0))
            do(pool.memset(nmax[:], 0.0))
            for s in range(2):
                do(pool.memset(vp[s][:, :, :, HD:VW], 1.0))
            for s in range(2):
                do(pool.memset(kst[s][KROWS:KROWS_M, :, :], 1.0))
            pool.sem_inc(ready_zero, 1)

            pool.wait_ge(in_rest, 64)
            pool.wait_ge(xn_ready, NCH)
            for k in range(NBLK):
                ins = pool.tensor_tensor(x_all[:, k, :], x_all[:, k, :], bo_s[:], ALU.add)
                chain.add(ins)
            chain.wait()
            pool.sem_inc(bo_added, 1)

            def copy_values(g, s):
                src = v_all[:].rearrange("p b g k n -> p (b g) k n")[:, bass.ds(g, 1)].rearrange("p o k (h d) -> p (o k) h d", h=GH)
                pool.tensor_copy(vp[s][:, :, :, 0:HD], src).then_inc(vp_ready[s], 1)

            pool.wait_ge(v_taken, NCH + 1)
            copy_values(0, 0)
            copy_values(1, 1)
            with pool.Fori(1, NG // 2) as i:
                for s in range(2):
                    pool.wait_ge(pv_done, i * (2 * NST) + ((s - 1) * NST + 2))
                    copy_values(i * 2 + s, s)

            pool.wait_ge(o_copied, 2 * NG + 1)
            do(pool.memset(px[:], 0.0))
            pool.sem_inc(vx_free, 1)
            for c in range(NCH):
                powers(var2_ready, rstd2_ready, c)
                pool.wait_ge(xn2_ready, c + 1)
                for k in range(c * CB, c * CB + CB):
                    chain.add(pool.tensor_tensor(x_all[:, k, :], x_all[:, k, :], box_s[:], ALU.add))
                chain.wait()
                pool.sem_inc(box_added, 1)
            with pool.Fori(0, NCH) as c:
                chain.turn(c, 1)
                powers(var2_ready, rstd2_ready, c + NCH)
            chain.turned(NCH)

            pool.wait_ge(ox_act, NCH * PAIRS // 2)
            pool.wait_ge(ox_dve, NCH * PAIRS // 2)
            do(pool.iota(em99[:], [[1, E]], base=-99, channel_multiplier=0, allow_small_or_imprecise_dtypes=True))
            do(pool.iota(steps128[:], [[P, NBLK]], base=0, channel_multiplier=0, allow_small_or_imprecise_dtypes=True))
            do(pool.iota(tno[:], [[1, NT]], base=0, channel_multiplier=0, allow_small_or_imprecise_dtypes=True))
            do(pool.memset(ones_e[:], 1.0))
            pool.sem_inc(tno_ready, 1)
            pool.wait_ge(zero_rows, 16 * NT)
            pool.wait_ge(pos_ready, 1)
            for k in range(NBLK):
                pool.wait_ge(xs_ready, k + 1)
                pool.indirect_dma_start(out=xg_d, out_offset=bass.IndirectOffsetOnAxis(ap=pos[:, k:k + 1], axis=0),
                                        in_=xn_all[:, k, :], in_offset=None).then_inc(scattered, 16)
            pool.wait_ge(scattered, 16 * NBLK)
            for s in range(2):
                pool.wait_ge(yo_out[s], 16 * (NT // 2 + 1))
            for k in range(NBLK):
                pool.indirect_dma_start(out=xn_all[:, k, :], out_offset=None, in_=yg_d,
                                        in_offset=bass.IndirectOffsetOnAxis(ap=pos[:, k:k + 1], axis=0)).then_inc(gathered[k // 4], 16)

        @block.scalar
        def _(act):
            act.sem_inc(p_ready, S_SLOTS)
            act.sem_inc(qk_taken, 1)

            act.wait_ge(ready_zero, 2)
            for m in range(PAIRS):
                act.wait_ge(kx_ready, m + 1)
                act.copy(kx[0:XD, :, m, 0:SK], ps[0:XD, m % 4, 0:B * SK].rearrange("p (b k) -> p b k", b=B)).then_inc(kx_act, 1)
            for n in range(0, 8, 2):
                act.wait_ge(vc_ready, n + 1)
                act.copy(vtmp[:, n // 4, n // 2 % 2, 0:512], ps[0:SK // 2, 4 + n % 4, :]).then_inc(vc_act, 1)

            act.wait_ge(in_qkv, 96)
            act.wait_ge(vc_out, 16)
            with act.Fori(0, NCH) as c:
                act.wait_ge(t1_ready, c + 1)
                act.copy(xnT[:], ps[:, 0:2, :]).then_inc(xnT_ready, 1)
                act.wait_ge(qf_free, c + 1)
                act.wait_ge(hi_out, c * 32 + 32)
                for n in range(4):
                    act.wait_ge(qk_ready, c * 4 + (n + 1))
                    act.activation(qf[:, n, :], ps[:, 2 + n, :], ACT.Identity, bias=bqk[:, n:n + 1])
                    ins = act.activation(qp[:, 0, n, :], ps[:, 2 + n, :], ACT.Identity, bias=bqk[:, n:n + 1])
                ins.then_inc(hi_ready, 1)
                act.wait_ge(hi_ready, c + 1)
                act.sem_inc(qk_taken, 1)

            def exps(g, k):
                qc, kb = STEPS[k]
                n = (qc + 1) * CT - max(qc * CT, kb * P)
                act.wait_ge(pv_done, g * NST + (k + 1))
                for h in range(GH):
                    v = k * GH + h
                    act.wait_ge(s_ready, g * (NST * GH) + (v + 1))
                    act.activation(probs[:, v % P_SLOTS, 0:n], ps[:, 4 + v % S_SLOTS, 0:n], ACT.Exp, scale=SELF_SCALE).then_inc(p_ready, 1)

            for done in (hi_out, mid_out, lo_out):
                act.wait_ge(done, 32 * (NCH + 1))
            act.wait_ge(v_taken, NCH + 1)
            def copy_output(g, qc):
                act.wait_ge(pv_done, g * NST + ((CB, NST)[qc] + 2))
                act.copy(osb[:, qc, :], ps[:, 7, :]).then_inc(o_copied, 1)

            def steps_from_2(g):
                for k in range(2, NST):
                    exps(g, k)
                    if k == CB:
                        copy_output(g, 0)

            exps(0, 0)
            exps(0, 1)
            with act.Fori(0, NG - 1) as g:
                steps_from_2(g)
                exps(g + 1, 0)
                copy_output(g, 1)
                exps(g + 1, 1)
            steps_from_2(NG - 1)
            copy_output(NG - 1, 1)

            act.wait_ge(m_taken, MT_ALL)
            for c in range(NCH):
                act.wait_ge(ty_ready, c + 1)
                act.copy(yT[c % 2][:], ps[:, 0:2, :]).then_inc(yT_ready, 1)
                if c >= 1:
                    act.wait_ge(t2_ready, c)
                    act.copy(xnT_all[:, :, (c - 1) * CT:c * CT], ps[:, 6:8, :]).then_inc(xnT2_ready, 1)
            act.wait_ge(t2_ready, NCH)
            act.copy(xnT_all[:, :, (NCH - 1) * CT:NCH * CT], ps[:, 6:8, :]).then_inc(xnT2_ready, 1)

            act.wait_ge(vx_free, 1)
            with act.Fori(0, NCH) as c:
                for m in range(PAIRS):
                    act.wait_ge(qx_ready, c * PAIRS + (m + 1))
                    act.activation(qT[:, m, :], ps[:, 4 + m % 4, :], ACT.Copy, scale=XSCALE).then_inc(qx_taken, 1)
                for u in range(XU + PV_LAG + 2):
                    if u < XU:
                        if u >= 4:
                            act.wait_ge(tx_ready, c * XU + (u - 3))
                        act.wait_ge(mx_ready, c * XU + (u + 1))
                        for h in range(2):
                            ins = act.activation(px[:, u % 4, SK * h:SK * h + SK], ps[:, (0, 1, 4, 5)[u % 4], SK * h:SK * h + SK], ACT.Exp,
                                                 bias=nmx[:, u % 4, h:h + 1], accum_out=smx[:, u % 4, h:h + 1])
                        ins.then_inc(ex_ready, 1)
                    w = u - T_LAG - 1
                    if 0 <= w < XU and w % 2 == 0:
                        act.wait_ge(tx_ready, c * XU + (w + 1))
                        if w // CB >= 2:
                            act.wait_ge(ox_ready, c * PAIRS + (w // CB - 1))
                        act.copy(pT[0:KC, w // CB % 2, :, w % CB * P:(w % CB + 1) * P],
                                 ps[0:KC, 6, 0:NKC * P].rearrange("p (c q) -> p c q", c=NKC)).then_inc(tx_act, 1)
                    w = u - PV_LAG - 1
                    if w % CB == CB - 1 and w > 0 and w // CB % 2 == 0 and w // CB < PAIRS:
                        act.wait_ge(ox_ready, c * PAIRS + (w // CB + 1))
                        act.copy(qT[:, w // CB, :], ps[:, 2, :]).then_inc(ox_act, 1)

            for c in range(NCH):
                act.wait_ge(t3_ready, c + 1)
                act.copy(xnT_all[:, :, c * CT:(c + 1) * CT], ps[:, 2 + c % 2 * 2:4 + c % 2 * 2, :]).then_inc(xnT3_ready, 1)

            act.wait_ge(mxl_ready, 1)
            act.activation(emx[:], mx[:], ACT.Exp, scale=-1.0).then_inc(exp_ready, 1)

            with act.Fori(0, NCH) as c:
                for m in range(FF):
                    act.wait_ge(gs_ready, c * FF + (m + 1))
                    act.wait_ge(hs_ready, c * FF + (m + 1))
                    act.activation(sgl[:], ps[:, 2, :], ACT.Silu).then_inc(gs_silu, 1)

            for s in range(2):
                act.sem_inc(yo_out[s], 16)

            def put_rows(t, s, i1):
                act.wait_ge(de_ready, t + 1)
                act.wait_ge(yo_out[s], i1 * 16)
                act.copy(yo[s][:], ps[:, 6 + s, 0:C]).then_inc(yo_ready, 1)
                dst = yg_d.rearrange("(t p) c -> t p c", p=P)[bass.ds(t, 1)].rearrange("o p c -> (o p) c")
                act.wait_ge(yo_ready, t + 1)
                act.dma_start(dst, yo[s][:]).then_inc(yo_out[s], 16)

            def silu(t, s):
                act.wait_ge(ge_ready, t + 1)
                act.activation(act_s[s][:], ps[:, 2 + 2 * s, :].rearrange("p (f q) -> p f q", f=FF), ACT.Silu).then_inc(silu_ready, 1)

            silu(0, 0)
            with act.Fori(0, NT // 2 - 1) as i:
                silu(i * 2 + 1, 1)
                put_rows(i * 2, 0, i + 1)
                silu(i * 2 + 2, 0)
                put_rows(i * 2 + 1, 1, i + 1)
            silu(NT - 1, 1)
            put_rows(NT - 2, 0, NT // 2)
            put_rows(NT - 1, 1, NT // 2)

        @block.tensor
        def _(pe):
            def mm(out_, lhsT, rhs, start, stop):
                return pe.matmul(out_, lhsT, rhs, start=start, stop=stop, skip_group_check=True)

            pe.wait_ge(in_ctx, 48)
            for m in range(PAIRS):
                if m >= 4:
                    pe.wait_ge(kx_act, m - 3)
                    pe.wait_ge(kx_dve, m - 3)
                for t in range(2):
                    ins = mm(ps[:, m % 4, 0:B * SK], wkx_s[:, t, m * P:(m + 1) * P], ctx_s[:, t, :], t == 0, t == 1)
                ins.then_inc(kx_ready, 1)
            for n in range(8):
                b, k, half = n // 4, n // 2 % 2, n % 2
                if n >= 4:
                    pe.wait_ge((vc_act, vc_dve)[n % 2], (n - 4) // 2 + 1)
                r0 = b * SK + k * (SK // 2)
                for t in range(2):
                    ins = mm(ps[0:SK // 2, 4 + n % 4, :], ctx_s[:, t, r0:r0 + SK // 2], wvx_s[:, t, half * 512:half * 512 + 512], t == 0, t == 1)
                ins.then_inc(vc_ready, 1)

            def turn_rows(src, bank, done):
                for k in range(CB):
                    for f in range(FC):
                        ins = pe.transpose(ps[:, bank + f, k * P:(k + 1) * P], src(k, f), ident[:])
                ins.then_inc(done, 1)

            pe.wait_ge(ready_const, 1)
            pe.wait_ge(in_qkv, 96)
            pe.wait_ge(vc_act, 4)
            pe.wait_ge(vc_dve, 4)
            pe.wait_ge(kx_act, PAIRS)
            pe.wait_ge(kx_dve, PAIRS)
            for c in range(NCH):
                pe.wait_ge(xn_ready, c + 1)
                turn_rows(lambda k, f: xn_all[:, c * CB + k, f * P:(f + 1) * P], 0, t1_ready)
                pe.wait_ge(xnT_ready, c + 1)
                pe.wait_ge(qk_taken, c + 1)
                for n in range(4):
                    for f in range(FC):
                        ins = mm(ps[:, 2 + n, :], wqkv[:, f, n // 2, n % 2 * P:(n % 2 + 1) * P], xnT[:, f, :], f == 0, f == FC - 1)
                    ins.then_inc(qk_ready, 1)
                pe.wait_ge(v_taken, c + 1)
                for k in range(CB):
                    for f in range(FC):
                        ins = mm(ps[:, 6 + k // 2, k % 2 * C:(k % 2 + 1) * C], xnT[:, f, k * P:(k + 1) * P], wqkv[:, f, 2, :], f == 0, f == FC - 1)
                ins.then_inc(v_ready, 1)

            def max_unit(use, s, u):
                h, qb = UNITS[u]
                keys = (qb + 1) * P
                slot = 2 * use.slot
                pe.wait_ge(m_taken, use.n + 1)
                lhsT = qst[s][0:KROWS, h, qb * P:(qb + 1) * P]
                for k0 in range(0, keys, 512):
                    n = min(512, keys - k0)
                    mm(ps[:, slot + k0 // 512, 0:n], lhsT, kst[s][0:KROWS, h, k0:k0 + n], True, False)
                d = qb * P
                mm(ps[:, slot + d // 512, d % 512:d % 512 + P], identb[:], maskq[:], False, True).then_inc(m_ready, 1)

            def turn_max(use):
                pe.wait_ge(m_taken, use.n + 2)
                pe.transpose(ps[:, 2 * use.slot, 0:P], nmax[:], ident[:]).then_inc(m_ready, 1)

            def turn_output(use, g, qc):
                pe.wait_ge(o_copied, g * 2 + (qc + 2))
                pe.wait_ge(m_taken, use.n + 1)
                for k in range(CB):
                    ins = pe.transpose(ps[:, 2 * use.slot, k * P:(k + 1) * P], osb[:, qc, k * P:(k + 1) * P], ident[:])
                ins.then_inc(m_ready, 1)

            def scores(g, s, k, between=None):
                qc, kb = STEPS[k]
                q0 = max(qc * CT, kb * P)
                n = (qc + 1) * CT - q0
                for h in range(GH):
                    v = k * GH + h
                    bank = 4 + v % S_SLOTS
                    pe.wait_ge(p_ready, g * (NST * GH) + (v + 1))
                    ins = mm(ps[:, bank, 0:n], kst[s][0:KROWS_M, h, kb * P:(kb + 1) * P], qst[s][0:KROWS_M, h, q0:q0 + n], True, False)
                    if kb * P >= qc * CT:
                        ins = mm(ps[:, bank, 0:P], identb[:], maskk[:], False, True)
                    ins.then_inc(s_ready, 1)
                    if between:
                        between(h)

            def values(g, s, k):
                qc, kb = STEPS[k]
                q0 = max(qc * CT, kb * P)
                n = (qc + 1) * CT - q0
                last_kb = (qc + 1) * CB - 1
                if kb == 0:
                    pe.wait_ge(o_copied, g * 2 + (qc + 1))
                pe.wait_ge(p_ready, g * (NST * GH) + (k * GH + GH + S_SLOTS))
                for h in range(GH):
                    ins = mm(ps[VW * h:VW * h + VW, 7, q0 - qc * CT:CT], vp[s][:, kb, h, :], probs[:, (k * GH + h) % P_SLOTS, 0:n],
                             kb == 0, kb == last_kb)
                ins.then_inc(pv_done, 1)

            pe.wait_ge(ready_zero, 3)
            pe.wait_ge(v_taken, NCH + 1)
            pe.wait_ge(qk_taken, NCH + 1)
            pe.wait_ge(q_in[0], 16 * 2 * NPROD)
            for u in range(NU):
                max_unit(use_before(u), 0, u)
            turn_max(use_before(NU))

            def first_steps(g, s, i1):
                pe.wait_ge(vp_ready[s], i1)
                pe.wait_ge(shift_in[s], i1 * 48)
                scores(g, s, 0)

            def steps_from_2(g, s, next_i1):
                for k in range(2, NST):
                    if next_i1 is not None and k in UNIT_STEPS:
                        if k == UNIT_STEPS[0]:
                            pe.wait_ge(q_in[1 - s], next_i1 * (16 * 2 * NPROD))
                        scores(g, s, k, lambda h: max_unit(use_of(g, s, "unit", units_of(k)[h]), 1 - s, units_of(k)[h]))
                    else:
                        scores(g, s, k)
                    if next_i1 is not None and k == SPLIT_STEP:
                        turn_max(use_of(g, s, "max"))
                    if k == TURN_STEP[0]:
                        turn_output(use_of(g, s, "out0", last=next_i1 is None), g, 0)
                    values(g, s, k - 1)

            def turn_group(g, s, next_i1):
                steps_from_2(g, s, next_i1)
                first_steps(g + 1, 1 - s, next_i1)
                values(g, s, NST - 1)
                scores(g + 1, 1 - s, 1)
                turn_output(use_of(g, s, "out1"), g, 1)
                values(g + 1, 1 - s, 0)

            first_steps(0, 0, 1)
            scores(0, 0, 1)
            values(0, 0, 0)
            with pe.Fori(0, NG // 2 - 1) as i:
                turn_group(i * 2, 0, i + 1)
                turn_group(i * 2 + 1, 1, i + 2)
            turn_group(NG - 2, 0, NG // 2)
            steps_from_2(NG - 1, 1, None)
            values(NG - 1, 1, NST - 1)
            turn_output(use_of(NG - 1, 1, "out1", last=True), NG - 1, 1)

            pe.wait_ge(in_rest, 64)
            pe.wait_ge(m_taken, MT_ALL)
            pe.wait_ge(p_ready, NG * NST * GH + S_SLOTS)

            def project(c):
                pe.wait_ge(yT_ready, c + 1)
                for k in range(CB):
                    for f in range(FC):
                        ins = mm(ps[:, 2 + c % 2 * 2 + k // 2, k % 2 * C:(k % 2 + 1) * C], yT[c % 2][:, f, k * P:(k + 1) * P], wo_s[:, f, :], f == 0, f == FC - 1)
                ins.then_inc(wo_done, 1)

            def turn_normed(c):
                pe.wait_ge(xn2_ready, c + 1)
                if c >= 1:
                    pe.wait_ge(xnT2_ready, c)
                turn_rows(lambda k, f: xn_all[:, c * CB + k, f * P:(f + 1) * P], 6, t2_ready)

            for c in range(NCH):
                b, qb = c // 2, c % 2 * CB
                if c >= 1:
                    pe.wait_ge(yT_ready, c)
                turn_rows(lambda k, f: y_tok[:, b * FC + f, qb + k, :], 0, ty_ready)
                project(c)
                if c >= 1:
                    turn_normed(c - 1)
            turn_normed(NCH - 1)
            pe.wait_ge(in_cross, 32)
            pe.wait_ge(xnT2_ready, NCH)
            with pe.Fori(0, B) as b:
                wait_apart(pe, "pe", vx_in, b * 64 + 64)
                with pe.Fori(0, S // CT) as cc:
                    c = b * 2 + cc
                    for m in range(PAIRS):
                        if m >= 4:
                            pe.wait_ge(qx_taken, c * PAIRS + (m - 3))
                        for f in range(FC):
                            ins = mm(ps[:, 4 + m % 4, :], wqx_s[:, f, m * P:(m + 1) * P], xnT_all[:, f, bass.ds(c * CT, CT)], f == 0, f == FC - 1)
                        ins.then_inc(qx_ready, 1)
                    pe.wait_ge(qx_taken, c * PAIRS + PAIRS)
                    pe.wait_ge(x2_ready, c + 1)
                    for u in range(XU + PV_LAG + 1):
                        if u < XU:
                            pair, k = u // CB, u % CB
                            if u >= 4:
                                pe.wait_ge(ex_ready, c * XU + (u - 3))
                            mm(ps[:, (0, 1, 4, 5)[u % 4], 0:PK], qT[:, pair, k * P:(k + 1) * P],
                               kx[:, bass.ds(b, 1), pair, :].rearrange("p o k -> p (o k)"), True, True).then_inc(sx_ready, 1)
                        w = u - T_LAG
                        if 0 <= w < XU:
                            pe.wait_ge(px_ready, c * XU + (w + 1))
                            if w >= 2:
                                pe.wait_ge((tx_act, tx_dve)[w % 2], c * (XU // 2) + w // 2)
                            for j in range(NKC):
                                ins = pe.transpose(ps[0:KC, 6 + w % 2, j * P:(j + 1) * P], px[:, w % 4, j * KC:(j + 1) * KC], ident[:])
                            ins.then_inc(tx_ready, 1)
                        w = u - PV_LAG
                        if w % CB == CB - 1 and w > 0:
                            pair = w // CB
                            pe.wait_ge(tx_act, c * (XU // 2) + 2 * (pair + 1))
                            pe.wait_ge(tx_dve, c * (XU // 2) + 2 * (pair + 1))
                            if pair >= 2:
                                pe.wait_ge((ox_act, ox_dve)[pair % 2], c * (PAIRS // 2) + pair // 2)
                            for j in range(NKC):
                                ins = mm(ps[:, 2 + pair % 2, :], vx[0:KC, pair, j, :], pT[0:KC, pair % 2, j, :], j == 0, j == NKC - 1)
                            ins.then_inc(ox_ready, 1)
                    pe.wait_ge(ox_act, c * (PAIRS // 2) + PAIRS // 2)
                    pe.wait_ge(ox_dve, c * (PAIRS // 2) + PAIRS // 2)
                    for k in range(CB):
                        for m in range(PAIRS):
                            ins = mm(ps[:, k // 2, k % 2 * C:(k % 2 + 1) * C], qT[:, m, k * P:(k + 1) * P], wox_s[:, m, :], m == 0, m == PAIRS - 1)
                    ins.then_inc(wox_done, 1)
                pe.wait_ge(ox_dve, c * (PAIRS // 2) + PAIRS // 2)
                pe.sem_inc(vx_free, 1)

            for c in range(NCH):
                pe.wait_ge(xn3_ready, c + 1)
                if c >= 2:
                    pe.wait_ge(xnT3_ready, c - 1)
                turn_rows(lambda k, f: xn_all[:, c * CB + k, f * P:(f + 1) * P], 2 + c % 2 * 2, t3_ready)
                if c == 0:
                    pe.wait_ge(x2_ready, NCH + 1)
                pe.wait_ge(xnT3_ready, c + 1)
                for k in range(c * CB, c * CB + CB):
                    for f in range(FC):
                        ins = mm(ps[:, 0, k * E:(k + 1) * E], xnT_all[:, f, k * P:(k + 1) * P], wr_s[:, f, :], f == 0, f == FC - 1)
            ins.then_inc(lg_ready, 1)

            pe.wait_ge(oh_ready, 1)
            mm(ps[:, 0, 0:NBLK * E], before[:], onehotb[:], True, False)
            for k in range(NBLK - 1):
                n = NBLK - 1 - k
                mm(ps[:, 0, (k + 1) * E:NBLK * E], onesb[:], onehotb[:, k:k + 1, :].to_broadcast((P, n, E)), False, k == NBLK - 2)
            for k in range(NBLK):
                ins = mm(ps[:, 1, 0:E], onesb[:], onehotb[:, k, :], k == 0, k == NBLK - 1)
            ins.then_inc(rank_ready, 1)

            pe.wait_ge(in_shared, 48)
            with pe.Fori(0, NCH) as c:
                for m in range(FF):
                    pe.wait_ge(gs_silu, c * FF + (m + 1))
                    for f in range(FC):
                        ins = mm(ps[:, 2, :], wsg_s[:, f, m * P:(m + 1) * P], xnT_all[:, f, bass.ds(c * CT, CT)], f == 0, f == FC - 1)
                    ins.then_inc(gs_ready, 1)
                    pe.wait_ge(us_taken, c * FF + (m + 1))
                    for f in range(FC):
                        ins = mm(ps[:, 3, :], wsu_s[:, f, m * P:(m + 1) * P], xnT_all[:, f, bass.ds(c * CT, CT)], f == 0, f == FC - 1)
                    ins.then_inc(us_ready, 1)
                pe.wait_ge(us_taken, c * FF + (FF + 1))
                pe.wait_ge(ds_taken, c + 1)
                for k in range(CB):
                    for m in range(FF):
                        ins = mm(ps[:, 4 + k // 2, k % 2 * C:(k % 2 + 1) * C], shT[:, m, k * P:(k + 1) * P], wsd_s[:, m, :], m == 0, m == FF - 1)
                ins.then_inc(ds_ready, 1)

            def turn_tile(t, s, i1):
                pe.wait_ge(xg_in[s], i1 * 16)
                for f in range(FC):
                    ins = pe.transpose(ps[:, s % 2, f * P:(f + 1) * P], xg[s][:, f * P:(f + 1) * P], ident[:])
                ins.then_inc(te_ready, 1)

            def gate_up(t, s, i1):
                pe.wait_ge(w_in[s], i1 * 32)
                pe.wait_ge(xgT_ready, t + 1)
                for half, done in ((0, ge_ready), (1, ue_ready)):
                    for m in range(FF):
                        for f in range(FC):
                            ins = mm(ps[:, 2 + 2 * (s % 2) + half, m * P:(m + 1) * P], wgu_s[s][:, f, half * F + m * P:half * F + (m + 1) * P],
                                     xgT[s % 2][:, f, :], f == 0, f == FC - 1)
                    ins.then_inc(done, 1)

            def down(t, s):
                pe.wait_ge(he_ready, t + 1)
                for m in range(FF):
                    ins = mm(ps[:, 6 + s % 2, 0:C], hT[s % 2][:, m, :], wdn_s[s][:, m, :], m == 0, m == FF - 1)
                ins.then_inc(de_ready, 1)

            pe.wait_ge(ds_taken, NCH + 1)
            turn_tile(0, 0, 1)
            gate_up(0, 0, 1)
            turn_tile(1, 1, 1)

            def tile(t, s, i):
                gate_up(t + 1, (s + 1) % WS, i + 1 + (s + 1) // WS)
                down(t, s)
                turn_tile(t + 2, (s + 2) % WS, i + 1 + (s + 2) // WS)

            with pe.Fori(0, NT // WS - 1) as i:
                for s in range(WS):
                    tile(i * WS + s, s, i)
            i = NT // WS - 1
            for s in range(WS - 2):
                tile(i * WS + s, s, i)
            gate_up(NT - 1, WS - 1, NT // WS)
            down(NT - 2, WS - 2)
            down(NT - 1, WS - 1)

        @block.vector
        def _(dve):
            chain = Chain(dve, "dve_chain")

            def do(ins):
                chain.add(ins)
                chain.wait()

            def norm(block_of, out_of, var, rst, done, turn):
                for k in range(CB):
                    ins = dve.bn_stats(stats[:, k, :], block_of(k))
                    chain.add(ins)
                chain.wait_apart("dve")
                for k in range(CB):
                    ins = dve.bn_aggr(mv[:, k, :], stats[:, k, :])
                ins.then_inc(var, 1)
                dve.wait_ge(rst, turn + 1)
                for k in range(CB):
                    for o in out_of(k):
                        ins = dve.tensor_scalar(o, block_of(k), mv[:, k, 0:1], rstd[:, k:k + 1], ALU.subtract, ALU.mult)
                ins.then_inc(done, 1)

            dve.sem_inc(v_taken, 1)
            dve.sem_inc(qf_free, 1)
            dve.sem_inc(m_taken, 2)
            dve.sem_inc(pv_done, 2)
            dve.sem_inc(o_copied, 1)
            dve.sem_inc(x2_ready, 1)

            dve.wait_ge(ready_zero, 2)
            for m in range(PAIRS):
                dve.wait_ge(kx_ready, m + 1)
                dve.tensor_copy(kx[XD:P, :, m, SK:PK], ps[XD:P, m % 4, 0:B * SK].rearrange("p (b k) -> p b k", b=B)).then_inc(kx_dve, 1)
            for n in range(1, 8, 2):
                dve.wait_ge(vc_ready, n + 1)
                dve.tensor_copy(vtmp[:, n // 4, n // 2 % 2, 512:1024], ps[0:SK // 2, 4 + n % 4, :]).then_inc(vc_dve, 1)

            dve.wait_ge(in_x, 16)
            with dve.Fori(0, NCH) as c:
                chain.turn(c, CB)
                norm(lambda k: x_all[:, bass.ds(c * CB + k, 1), :].rearrange("p o c -> p (o c)"),
                     lambda k: [xn_all[:, bass.ds(c * CB + k, 1), :].rearrange("p o c -> p (o c)")],
                     var_ready, rstd_ready, xn_ready, c)
            chain.turned(NCH)
            dve.wait_ge(in_qkv, 96)
            with dve.Fori(0, B) as b:
                with dve.Fori(0, S // CT) as cc:
                    c = b * 2 + cc
                    dve.wait_ge(hi_ready, c + 1)
                    chain.turn(c, 1)
                    do(dve.tensor_tensor(qr[:], qf[:], qp[:, 0], ALU.subtract))
                    dve.sem_inc(qf_free, 1)
                    dve.wait_ge(mid_out, c * 32 + 32)
                    dve.tensor_copy(qp[:, 1], qr[:]).then_inc(mid_ready, 1)
                    dve.wait_ge(mid_ready, c + 1)
                    dve.wait_ge(lo_out, c * 32 + 32)
                    dve.tensor_tensor(qp[:, 2], qr[:], qp[:, 1], ALU.subtract).then_inc(lo_ready, 1)
                    dve.wait_ge(v_ready, c + 1)
                    for k in range(CB):
                        ins = dve.tensor_tensor(v_all[:, bass.ds(b, 1), :, bass.ds(cc * CB + k, 1), :].rearrange("p o g q n -> p (o g) (q n)"),
                                                ps[:, 6 + k // 2, k % 2 * C:(k % 2 + 1) * C].rearrange("p (g n) -> p g n", g=GH),
                                                bv_s[:].rearrange("p (g n) -> p g n", g=GH), ALU.add)
                    ins.then_inc(v_taken, 1)
                    dve.wait_ge(lo_ready, c + 1)
            chain.turned(NCH)

            def take_max(use, u):
                h, qb = UNITS[u]
                keys = (qb + 1) * P
                slot = 2 * use.slot
                dve.wait_ge(m_ready, use.n + 1)
                dve.tensor_reduce(nmax[:, h * QB + qb:h * QB + qb + 1], ps[:, slot:slot + 2, :].rearrange("p a n -> p (a n)")[:, 0:keys], AX.X, ALU.max,
                                  negate=True).then_inc(m_taken, 1)

            def split_max(use):
                dve.wait_ge(m_ready, use.n + 1)
                t = ps[0:NU, 2 * use.slot, 0:P]
                do(dve.tensor_copy(nmp[:, 0, :], t))
                dve.tensor_tensor(nmr[:], t, nmp[:, 0, :], ALU.subtract).then_inc(m_taken, 1)
                dve.wait_ge(m_taken, use.n + 3)
                do(dve.tensor_copy(nmp[:, 1, :], nmr[:]))
                dve.tensor_tensor(nmp[:, 2, :], nmr[:], nmp[:, 1, :], ALU.subtract).then_inc(shift_ready, 1)

            def take_output(use, i, s, qc):
                dve.wait_ge(m_ready, use.n + 1)
                o = ps[:, 2 * use.slot, :].rearrange("p (k h w) -> p k h w", k=CB, h=GH)
                do(dve.reciprocal(rsum[:, qc], o[:, :, :, HD:HD + 1]))
                dst = y_tok[:, bass.ds(i, 1), qc * CB:(qc + 1) * CB, s * GH * HD:(s + 1) * GH * HD].rearrange("p o k (h d) -> p (o k) h d", h=GH)
                dve.tensor_tensor(dst, o[:, :, :, 0:HD], rsum[:, qc].to_broadcast((P, CB, GH, HD)), ALU.mult).then_inc(m_taken, 1)

            def steps_from_2(i, s, lookahead):
                g = i * 2 + s
                for k in range(2, NST):
                    if lookahead and k in UNIT_STEPS:
                        for u in units_of(k):
                            take_max(use_of(g, s, "unit", u), u)
                    if lookahead and k == SPLIT_STEP:
                        split_max(use_of(g, s, "max"))
                    if k == TURN_STEP[0]:
                        take_output(use_of(g, s, "out0", last=not lookahead), i, s, 0)

            for u in range(NU):
                take_max(use_before(u), u)
            split_max(use_before(NU))
            with dve.Fori(0, NG // 2 - 1) as i:
                chain.turn(i, 8)
                for s in range(2):
                    steps_from_2(i, s, True)
                    take_output(use_of(i * 2 + s, s, "out1"), i, s, 1)
            chain.turned(NG // 2 - 1)
            i = NG // 2 - 1
            steps_from_2(i, 0, True)
            take_output(use_of(NG - 2, 0, "out1"), i, 0, 1)
            steps_from_2(i, 1, False)
            take_output(use_of(NG - 1, 1, "out1", last=True), i, 1, 1)

            dve.wait_ge(bo_added, 1)
            for c in range(NCH):
                dve.wait_ge(wo_done, c + 1)
                xc = x_all[:, c * CB:(c + 1) * CB, :]
                do(dve.tensor_tensor(xc, xc, ps[:, 2 + c % 2 * 2:4 + c % 2 * 2, :].rearrange("p a (k c) -> p (a k) c", k=2), ALU.add))
                norm(lambda k: x_all[:, c * CB + k, :], lambda k: [xn_all[:, c * CB + k, :]], var2_ready, rstd2_ready, xn2_ready, c)

            dve.wait_ge(vx_free, 1)
            with dve.Fori(0, NCH) as c:
                chain.turn(c, CB + 1 + XU)
                def rows(k):
                    return x_all[:, bass.ds(c * CB + k, 1), :].rearrange("p o c -> p (o c)")
                xc = x_all[:, bass.ds(c * CB, CB), :]
                for u in range(XU + PV_LAG + 2):
                    if u < XU:
                        dve.wait_ge(sx_ready, c * XU + (u + 1))
                        dve.tensor_reduce(nmx[:, u % 4, :], ps[:, (0, 1, 4, 5)[u % 4], 0:PK].rearrange("p (h k) -> p h k", h=2), AX.X, ALU.max,
                                          negate=True).then_inc(mx_ready, 1)
                    w = u - 1
                    if 0 <= w < XU:
                        dve.wait_ge(ex_ready, c * XU + (w + 1))
                        do(dve.reciprocal(rsx[:, w % 4, :], smx[:, w % 4, :]))
                        for h in range(2):
                            pp = px[:, w % 4, SK * h:SK * h + SK]
                            ins = dve.tensor_scalar(pp, pp, rsx[:, w % 4, h:h + 1], None, ALU.mult)
                        ins.then_inc(px_ready, 1)
                    w = u - T_LAG - 1
                    if 0 <= w < XU and w % 2 == 1:
                        dve.wait_ge(tx_ready, c * XU + (w + 1))
                        if w // CB >= 2:
                            dve.wait_ge(ox_ready, c * PAIRS + (w // CB - 1))
                        dve.tensor_copy(pT[0:KC, w // CB % 2, :, w % CB * P:(w % CB + 1) * P],
                                        ps[0:KC, 7, 0:NKC * P].rearrange("p (c q) -> p c q", c=NKC)).then_inc(tx_dve, 1)
                    w = u - PV_LAG - 1
                    if w % CB == CB - 1 and w > 0 and w // CB % 2 == 1 and w // CB < PAIRS:
                        dve.wait_ge(ox_ready, c * PAIRS + (w // CB + 1))
                        dve.tensor_copy(qT[:, w // CB, :], ps[:, 3, :]).then_inc(ox_dve, 1)
                dve.wait_ge(wox_done, c + 1)
                dve.wait_ge(box_added, c + 1)
                chain.add(dve.tensor_tensor(xc, xc, ps[:, 0:2, :].rearrange("p a (k c) -> p (a k) c", k=2), ALU.add))
                chain.wait_apart("dve")
                dve.sem_inc(x2_ready, 1)
                norm(rows, lambda k: [xn_all[:, bass.ds(c * CB + k, 1), :].rearrange("p o c -> p (o c)")],
                     var2_ready, rstd2_ready, xn3_ready, c + NCH)
            chain.turned(NCH)

            dve.wait_ge(tno_ready, 1)
            dve.wait_ge(lg_ready, 1)
            do(dve.tensor_copy(lg_all[:], ps[:, 0, 0:NBLK * E].rearrange("p (k e) -> p k e", e=E)))
            shape = (P, NBLK, E)

            def per_block(t):
                return t[:].rearrange("p (k o) -> p k o", o=1).to_broadcast(shape)

            def per_expert(t):
                return t[:].rearrange("p (o e) -> p o e", o=1).to_broadcast(shape)

            dve.tensor_reduce(mx[:], lg_all[:], AX.X, ALU.max).then_inc(mxl_ready, 1)
            dve.wait_ge(mxl_ready, 1)
            do(dve.tensor_tensor(cand[:], lg_all[:], per_block(mx), ALU.is_ge))
            do(dve.tensor_tensor(cand[:], cand[:], per_expert(em99), ALU.mult))
            do(dve.tensor_reduce(pick[:], cand[:], AX.X, ALU.min))
            do(dve.tensor_tensor(onehot[:], per_expert(em99), per_block(pick), ALU.is_equal))
            dve.tensor_copy(onehotb[:], onehot[:]).then_inc(oh_ready, 1)
            dve.wait_ge(exp_ready, 1)
            do(dve.tensor_scalar(score[:], emx[:], 1.0, None, ALU.add))
            do(dve.reciprocal(score[:], score[:]))
            for k in range(NBLK):
                dve.tensor_scalar(xn_all[:, k, :], xn_all[:, k, :], score[:, k:k + 1], None, ALU.mult).then_inc(xs_ready, 1)
            dve.wait_ge(rank_ready, 1)
            do(dve.tensor_tensor(over[:], ps[:, 1, 0:E].rearrange("p (e o) -> p e o", o=1).to_broadcast((P, E, NBLK)),
                                 steps128[:].rearrange("p (o k) -> p o k", o=1).to_broadcast((P, E, NBLK)), ALU.is_gt))
            do(dve.tensor_reduce(tiles[:], over[:], AX.X, ALU.add))
            do(dve.tensor_tensor_scan(ends[:], ones_e[:], tiles[:], 0.0, ALU.mult, ALU.add))
            do(dve.tensor_tensor(passed[:], ends[0:1, :].rearrange("p (o e) -> p o e", o=1).to_broadcast((1, NT, E)),
                                 tno[:].rearrange("p (t o) -> p t o", o=1).to_broadcast((1, NT, E)), ALU.is_le))
            do(dve.tensor_reduce(eotf[:], passed[:], AX.X, ALU.add))
            do(dve.tensor_scalar(eotf[:], eotf[:], float(E - 1), None, ALU.min))
            dve.tensor_copy(eot[:], eotf[:]).then_inc(eot_ready, 1)
            do(dve.tensor_tensor(base_t[:], ends[:], tiles[:], ALU.subtract))
            do(dve.tensor_scalar(base_t[:], base_t[:], float(P), None, ALU.mult))
            do(dve.tensor_tensor(cand[:], ps[:, 0, 0:NBLK * E].rearrange("p (k e) -> p k e", e=E), per_expert(base_t), ALU.add))
            do(dve.tensor_tensor(cand[:], cand[:], onehot[:], ALU.mult))
            do(dve.tensor_reduce(posf[:], cand[:], AX.X, ALU.add))
            dve.tensor_copy(pos[:], posf[:]).then_inc(pos_ready, 1)

            dve.sem_inc(hs_ready, 1)
            dve.sem_inc(us_taken, 1)
            dve.sem_inc(ds_taken, 1)
            dve.sem_inc(gs_silu, 1)
            with dve.Fori(0, NCH) as c:
                chain.turn(c, 1)
                for m in range(FF):
                    dve.wait_ge(gs_silu, c * FF + (m + 2))
                    dve.wait_ge(us_ready, c * FF + (m + 1))
                    dve.tensor_tensor(shT[:, m, :], sgl[:], ps[:, 3, :], ALU.mult).then_inc(us_taken, 1)
                    dve.wait_ge(us_taken, c * FF + (m + 2))
                    dve.sem_inc(hs_ready, 1)
                dve.wait_ge(ds_ready, c + 1)
                xc = x_all[:, bass.ds(c * CB, CB), :]
                do(dve.tensor_tensor(xc, xc, ps[:, 4:6, :].rearrange("p a (k c) -> p (a k) c", k=2), ALU.add))
                dve.sem_inc(ds_taken, 1)
            chain.turned(NCH)

            def take_rows(t, s):
                dve.wait_ge(te_ready, t + 1)
                dve.tensor_copy(xgT[s][:], ps[:, s, 0:C].rearrange("p (f q) -> p f q", f=FC)).then_inc(xgT_ready, 1)

            def gated(t, s):
                dve.wait_ge(silu_ready, t + 1)
                dve.wait_ge(ue_ready, t + 1)
                dve.tensor_tensor(hT[s][:], act_s[s][:], ps[:, 3 + 2 * s, :].rearrange("p (f q) -> p f q", f=FF), ALU.mult).then_inc(he_ready, 1)

            take_rows(0, 0)
            gated(0, 0)
            take_rows(1, 1)
            with dve.Fori(0, NT // 2 - 1) as i:
                gated(i * 2 + 1, 1)
                take_rows(i * 2 + 2, 0)
                gated(i * 2 + 2, 0)
                take_rows(i * 2 + 3, 1)
            gated(NT - 1, 1)

            for n in range(4):
                dve.wait_ge(gathered[n], 64)
                xc = x_all[:, 4 * n:4 * n + 4, :]
                dve.tensor_tensor(xc, xc, xn_all[:, 4 * n:4 * n + 4, :], ALU.add).then_inc(out_ready, 1)


_OUT = ("out_dram", (B, S, C))


def kernel(**inputs):
    import concourse.bacc as bacc
    from concourse.bass_utils import run_bass_kernel_spmd

    def a(name):
        return np.asarray(inputs[name])

    arrays = {
        "x": a("x"), "ctxT": a("ctx_768").transpose(2, 0, 1).reshape(CD, B * SK),
        "wq": a("L0_attn_Wq"), "bq": a("L0_attn_bq"), "wk": a("L0_attn_Wk"), "bk": a("L0_attn_bk"),
        "wv": a("L0_attn_Wv"), "bv": a("L0_attn_bv"), "wo": a("L0_attn_Wo"), "bo": a("L0_attn_bo"),
        "wqx": a("L0_xattn_w_q"), "wkx": a("L0_xattn_w_k"), "wvx": a("L0_xattn_w_v"), "wox": a("L0_xattn_w_o"), "box": a("L0_xattn_b_o"),
        "wr": a("L0_ffn_w_router").T, "wgu": a("L0_ffn_gate_up_proj"), "wdn": a("L0_ffn_down_proj"),
        "wsg": a("L0_ffn_w_gate").T, "wsu": a("L0_ffn_w_up").T, "wsd": a("L0_ffn_w_down").T,
    }
    arrays = {k: np.ascontiguousarray(v) for k, v in arrays.items()}
    nc = bacc.Bacc("TRN2", target_bir_lowering=False, num_devices=1)
    aps = {k: nc.dram_tensor(k + "_dram", v.shape, mybir.dt.from_np(v.dtype), kind="ExternalInput").ap() for k, v in arrays.items()}
    out = nc.dram_tensor(_OUT[0], _OUT[1], F32, kind="ExternalOutput").ap()
    build(nc, **aps, out=out)
    r = run_bass_kernel_spmd(nc, [{k + "_dram": v for k, v in arrays.items()}], core_ids=[0])
    return np.asarray(r.results[0][_OUT[0]])
```

```python
from contextlib import ExitStack

import numpy as np

import concourse.bass as bass
from concourse import mybir

F32 = mybir.dt.float32
BF16 = mybir.dt.bfloat16
F32R = mybir.dt.float32r
U32 = mybir.dt.uint32
I32 = mybir.dt.int32
ALU = mybir.AluOpType
ACT = mybir.ActivationFunctionType
AX = mybir.AxisListType

P = 128
B, S, C = 2, 1024, 256
CB = 4
CT = CB * P
NCH = B * S // CT
FC = C // P
NBLK = B * S // P
EPS = 1e-5
NEG = -1.0e30

H, HD = 16, 16
GH = 4
NG = B * H // GH
VW = 32
SELF_SCALE = HD ** -0.5
Q_PART = (0, 0, 0, 1, 1, 2)
K_PART = (0, 1, 2, 0, 1, 0)
NPROD = len(Q_PART)
RUNS = ((0, 3), (3, 2), (5, 1))
KROWS = NPROD * HD
KROWS_M = KROWS + 3
QB = S // P
STEPS = [(qc, kb) for qc in range(S // CT) for kb in [*range(qc * CB, (qc + 1) * CB), *range(qc * CB)]]
NST = len(STEPS)
UNITS = [(h, qb) for h in range(GH) for qb in range(QB)]
NU = len(UNITS)
UNITS_AT = {0: 4, 1: 4, 2: 4, 3: 4, 4: 3, 5: 3, 6: 3, 7: 3, 8: 4}
assert sum(UNITS_AT.values()) == NU
NEARLY = UNITS_AT[0] + UNITS_AT[1]
SPLIT_STEP = max(UNITS_AT) + 1
TURN_STEP = CB + 1
TURNS = NU + 3
GS = 3
P_SLOTS, S_SLOTS = 8, 3

XH, XD = 16, 64
SK, CD = 154, 192
CK = CD // 2
PAIRS = XH // 2
PK = 2 * SK
KC = 103
NKC = 3
XI = XH * XD
XSCALE = XD ** -0.5
XU = PAIRS * CB
T_LAG, PV_LAG = 3, 5

E, F = 16, 512
FF = F // P
WS = 5
RS = 4
NT = B * S // P + E - 1
NTT = NT + NT % 2


def bcast_rows(v):
    return v.rearrange("(o n) -> o n", o=1).to_broadcast((P, v.shape[0]))


def build(nc, x, ctxT, wq, bq, wk, bk, wv, bv, wo, bo, wqx, wkx, wvx, wox, box, wr, wgu, wdn, wsg, wsu, wsd, out):
    parts_d = nc.dram_tensor("qk_parts", (3, 2, B, C, S), BF16, kind="Internal").ap()
    vx_d = nc.dram_tensor("cross_values", (B, SK, XI), F32, kind="Internal").ap()
    xg_d = nc.dram_tensor("expert_rows_in", (NT * P, C), F32, kind="Internal").ap()
    yg_d = nc.dram_tensor("expert_rows_out", (NT * P, C), F32, kind="Internal").ap()

    with ExitStack() as ctx:
        def sb(name, shape, dt=F32, where=ctx):
            return where.enter_context(nc.sbuf_tensor(name, shape, dt))

        def sem(name):
            return ctx.enter_context(nc.semaphore(name))

        x_all = sb("x_all", [P, NBLK, C])
        ident = sb("ident", [P, P])
        identb = sb("identb", [P, P], BF16)
        maskq = sb("maskq", [P, P], BF16)
        maskk = sb("maskk", [P, P], BF16)
        before = sb("before", [P, P], BF16)
        onesb = sb("onesb", [P, P], BF16)
        xn_all = sb("xn_all", [P, NBLK, C])
        stats = sb("stats", [P, CB, 6])
        mv = sb("mv", [P, 2, CB, 2])
        vpe = sb("vpe", [P, 2, CB])
        rstd = sb("rstd", [P, 2, CB])
        mhalf = sb("mhalf", [P, CB])
        xnT = sb("xnT", [P, FC, CT])
        wo_s = sb("wo_s", [P, FC, C])
        bo_s = sb("bo_s", [P, C])
        box_s = sb("box_s", [P, C])
        wr_s = sb("wr_s", [P, FC, E])
        zeros = sb("zeros", [P, C])

        with ExitStack() as attn:
            y_tok = sb("y_tok", [P, QB, NG * GH * HD], F32, attn)
            kx = sb("kx", [P, B, PAIRS, PK], F32, attn)
            vx = sb("vx", [P, PAIRS, NKC, P], F32, attn)
            with ExitStack() as early:
                v_all = sb("v_all", [P, B, GH, QB, GH * HD], F32, early)
                vp = [sb(f"vp{s}", [P, QB, GH, VW], F32, early) for s in range(GS)]
                nmax = sb("nmax", [P, P], F32, early)
                nmp = sb("nmp", [NU, 3, P], BF16, early)
                nmr = sb("nmr", [NU, P], F32, early)
                osb = sb("osb", [P, 2, CT], F32, early)
                rsum = sb("rsum", [P, 2, CB, GH, 1], F32, early)
                wqkv = sb("wqkv", [P, FC, 3, C], F32, early)
                bqk = sb("bqk", [P, 4], F32, early)
                bv_s = sb("bv_s", [P, C], F32, early)
                with ExitStack() as kv:
                    wkx_s = sb("wkx_s", [CK, 2, XI], F32, kv)
                    wvx_s = sb("wvx_s", [CK, 2, XI], F32, kv)
                    ctx_s = sb("ctx_s", [CK, 2, B * SK], F32, kv)
                    vtmp = sb("vtmp", [SK // 2, B, 2, XI], F32, kv)
                with ExitStack() as stacks:
                    qst = [sb(f"qst{s}", [P, GH, S], BF16, stacks) for s in range(GS)]
                    kst = [sb(f"kst{s}", [P, GH, S], BF16, stacks) for s in range(GS)]
                    with ExitStack() as proj:
                        qf = sb("qf", [P, 4, CT], F32, proj)
                        qr = sb("qr", [P, 4, CT], F32, proj)
                        qp = sb("qp", [P, 3, 4, CT], BF16, proj)
                    with ExitStack() as two:
                        probs = sb("probs", [P, P_SLOTS, CT], F32, two)
            with ExitStack() as late:
                wqx_s = sb("wqx_s", [P, FC, XI], F32, late)
                wox_s = sb("wox_s", [P, PAIRS, C], F32, late)
                yT = [sb(f"yT{s}", [P, FC, CT], F32, late) for s in range(2)]
                qT = sb("qT", [P, PAIRS, CT], F32, late)
                px = sb("px", [P, 4, NKC * KC], F32, late)
                nmx = sb("nmx", [P, 4, 2], F32, late)
                smx = sb("smx", [P, 4, 2], F32, late)
                rsx = sb("rsx", [P, 4, 2], F32, late)
                pT = sb("pT", [P, 2, NKC, CT], F32, late)
                xnT_all = sb("xnT_all", [P, FC, B * S], F32, late)
                wsg_s = sb("wsg_s", [P, FC, F], F32, late)
                wsu_s = sb("wsu_s", [P, FC, F], F32, late)
                wsd_s = sb("wsd_s", [P, FF, C], F32, late)
                wsg_h, wsg_l = sb("wsg_h", [P, FC, F], F32R, late), sb("wsg_l", [P, FC, F], F32R, late)
                wsu_h, wsu_l = sb("wsu_h", [P, FC, F], F32R, late), sb("wsu_l", [P, FC, F], F32R, late)
                wsd_h, wsd_l = sb("wsd_h", [P, FF, C], F32R, late), sb("wsd_l", [P, FF, C], F32R, late)
                wr_hl = sb("wr_hl", [P, FC, 2 * E], F32R, late)
        with ExitStack() as moe:
            lg_all = sb("lg_all", [P, NBLK, E], F32, moe)
            mx = sb("mx", [P, NBLK], F32, moe)
            emx = sb("emx", [P, NBLK], F32, moe)
            score = sb("score", [P, NBLK], F32, moe)
            em99 = sb("em99", [P, E], F32, moe)
            cand = sb("cand", [P, NBLK, E], F32, moe)
            pick = sb("pick", [P, NBLK], F32, moe)
            onehot = sb("onehot", [P, NBLK, E], F32, moe)
            onehotb = sb("onehotb", [P, NBLK, E], BF16, moe)
            steps128 = sb("steps128", [P, NBLK], F32, moe)
            over = cand[:].rearrange("p k e -> p (k e)").rearrange("p (e k) -> p e k", e=E)
            tiles = sb("tiles", [P, E], F32, moe)
            ones_e = sb("ones_e", [P, E], F32, moe)
            ends = sb("ends", [P, E], F32, moe)
            base_t = sb("base", [P, E], F32, moe)
            posf = sb("posf", [P, NBLK], F32, moe)
            pos = sb("pos", [P, NBLK], U32, moe)
            tno = sb("tno", [1, NTT], F32, moe)
            passed = sb("passed", [1, NTT, E], F32, moe)
            some = sb("some", [1, E], F32, moe)
            upto, upto1 = sb("upto", [1, E], F32, moe), sb("upto1", [1, E], F32, moe)
            numf = sb("numf", [1, NTT], F32, moe)
            numbered, endj, lastj = (sb(n, [1, E], F32, moe) for n in ("numbered", "endj", "lastj"))
            expert = sb("expert", [1, E], I32, moe)
            need = sb("need", [1, NTT], I32, moe)
            used = sb("used", [1, NTT], F32, moe)
            usedn = sb("usedn", [1, 2], F32, moe)
            filled = sb("filled", [1, 2], I32, moe)
            slotf = sb("slotf", [1, NTT], F32, moe)
            slot = sb("slot", [1, NTT], I32, moe)
            freed = sb("freed", [1, E], I32, moe)
            xg = [sb(f"xg{s}", [P, C], F32, moe) for s in range(RS)]
            wgu_s = sb("wgu", [P, WS, FC, 2 * F], F32, moe)
            wdn_s = sb("wdn", [P, WS, FF, C], F32, moe)
            with ExitStack() as shared:
                xnT_h = sb("xnT_h", [P, FC, B * S], F32R, shared)
                xnT_l = sb("xnT_l", [P, FC, B * S], F32R, shared)
                sgl = sb("sgl", [P, 2, CT], F32, shared)
                prod = sb("prod", [P, 2, CT], F32, shared)
                shT_h = sb("shT_h", [P, FF, CT], F32R, shared)
                shT_l = sb("shT_l", [P, FF, CT], F32R, shared)
                lgT = [xnT, sb("lgT", [2 * E, FC, CT], F32, shared)]
            with ExitStack() as tile_bufs:
                wgu_h = [sb(f"wgu_h{s}", [P, FC, 2 * F], F32R, tile_bufs) for s in range(2)]
                wgu_l = [sb(f"wgu_l{s}", [P, FC, 2 * F], F32R, tile_bufs) for s in range(2)]
                xgT_h = [sb(f"xgT_h{s}", [P, FC, P], F32R, tile_bufs) for s in range(2)]
                xgT_l = [sb(f"xgT_l{s}", [P, FC, P], F32R, tile_bufs) for s in range(2)]
                act_s = [sb(f"act{s}", [P, F], F32, tile_bufs) for s in range(2)]
                h_tok = [sb(f"h{s}", [P, F], F32, tile_bufs) for s in range(2)]
                hT = [sb(f"hT{s}", [P, FF, P], F32, tile_bufs) for s in range(2)]
                yo = [sb(f"yo{s}", [P, C], F32, tile_bufs) for s in range(2)]

        ps = ctx.enter_context(nc.psum_tensor("ps", [P, 8, 512], F32))

        passed_wait = {e: sem(f"passed_{e}") for e in ("dve", "pool", "pe", "act", "sp")}

        def wait_apart(eng, name, which, value):
            eng.wait_ge(which, value)
            eng.sem_inc(passed_wait[name], 1)

        class Use:

            def __init__(self, base, j):
                self.n, self.slot = base + j, j % 2
                self.free = self.n + (2 if j == 0 else 1)

        def units_of(k):
            first = sum(n for kk, n in UNITS_AT.items() if kk < k)
            return range(first, first + UNITS_AT[k])

        BEFORE_OUT = units_of(TURN_STEP)[-1] + 1 - NEARLY

        def use_before(j):
            return Use(0, j)

        def use_of(g, what, u=0):
            j = {"unit": u - NEARLY + (u - NEARLY >= BEFORE_OUT), "out0": BEFORE_OUT, "max": NU - NEARLY + 1,
                 "early": NU - NEARLY + 2 + u, "out1": NU + 2}[what]
            base = g * TURNS + (NU + 1 + NEARLY)
            if isinstance(g, int) and g == NG - 2 and what == "out1":
                j -= NEARLY
            if isinstance(g, int) and g == NG - 1:
                base, j = base - NEARLY, {"out0": 0, "out1": 1}[what]
            return Use(base, j)

        MT_ALL = NU + 1 + (NG - 1) * TURNS + 2 + 2

        class Chain:

            def __init__(self, eng, name):
                self.eng, self.sem, self.base, self.n = eng, sem(name), 0, 0

            def add(self, ins):
                ins.then_inc(self.sem, 1)
                self.n += 1

            def wait(self):
                self.eng.wait_ge(self.sem, self.base + self.n)

            def wait_apart(self, name):
                wait_apart(self.eng, name, self.sem, self.base + self.n)

            def turn(self, i, per):
                self.start, self.per = self.base + self.n, per
                self.base, self.n = i * per + self.start, 0

            def turned(self, turns):
                assert self.n == self.per, (self.n, self.per)
                self.base, self.n = self.start + turns * self.per, 0

        ready_const = sem("ready_const")
        ready_zero = sem("ready_zero")
        in_ctx, in_wvx, in_x, in_qkv = sem("in_ctx"), sem("in_wvx"), sem("in_x"), sem("in_qkv")
        in_rest = sem("in_rest")
        in_cross, in_shared = sem("in_cross"), sem("in_shared")
        zero_rows = sem("zero_rows")
        kx_ready, kx_act, kx_dve = sem("kx_ready"), sem("kx_act"), sem("kx_dve")
        vc_ready, vc_act, vc_dve, vc_out = sem("vc_ready"), sem("vc_act"), sem("vc_dve"), sem("vc_out")
        var_ready, rstd_ready, xn_ready = sem("var_ready"), sem("rstd_ready"), sem("xn_ready")
        t1_ready, xnT_ready = sem("t1_ready"), sem("xnT_ready")
        qk_ready, qk_taken = sem("qk_ready"), sem("qk_taken")
        v_ready, v_taken = sem("v_ready"), sem("v_taken")
        qf_free = sem("qf_free")
        hi_ready, mid_ready, lo_ready = sem("hi_ready"), sem("mid_ready"), sem("lo_ready")
        hi_out, mid_out, lo_out = sem("hi_out"), sem("mid_out"), sem("lo_out")
        bo_added = sem("bo_added")
        q_in = [sem(f"stack_in{s}") for s in range(GS)]
        vp_ready = [sem(f"vp_ready{s}") for s in range(GS)]
        shift_in = [sem(f"shift_in{s}") for s in range(GS)]
        m_ready, m_taken = sem("m_ready"), sem("m_taken")
        shift_ready = sem("shift_ready")
        s_ready, p_ready = sem("s_ready"), sem("p_ready")
        pv_done, o_copied = sem("pv_done"), sem("o_copied")
        ty_ready, yT_ready = sem("ty_ready"), sem("yT_ready")
        wo_done, x1_ready = sem("wo_done"), sem("x1_ready")
        var2_ready, rstd2_ready, xn2_ready = sem("var2_ready"), sem("rstd2_ready"), sem("xn2_ready")
        box_added = sem("box_added")
        t2_ready, xnT2_ready = sem("t2_ready"), sem("xnT2_ready")
        vx_free, vx_in = sem("vx_free"), sem("vx_in")
        qx_ready, qx_taken = sem("qx_ready"), sem("qx_taken")
        sx_ready, mx_ready, ex_ready, px_ready = sem("sx_ready"), sem("mx_ready"), sem("ex_ready"), sem("px_ready")
        tx_ready, tx_act, tx_dve = sem("tx_ready"), sem("tx_act"), sem("tx_dve")
        ox_ready, ox_act, ox_dve = sem("ox_ready"), sem("ox_act"), sem("ox_dve")
        wox_done, x2_ready, xn3_ready = sem("wox_done"), sem("x2_ready"), sem("xn3_ready")
        ws_split = sem("ws_split")
        t3_ready, xnT3_ready, xnT3l_ready = sem("t3_ready"), sem("xnT3_ready"), sem("xnT3l_ready")
        gs_ready, us_ready = sem("gs_ready"), sem("us_ready")
        gs_silu, us_taken, hs_ready = sem("gs_silu"), sem("us_taken"), sem("hs_ready")
        prod_ready, shh_ready, shl_ready = sem("prod_ready"), sem("shh_ready"), sem("shl_ready")
        ds_ready, ds_taken = sem("ds_ready"), sem("ds_taken")
        tno_ready = sem("tno_ready")
        lgT_ready, lgT_taken, lg_ready = sem("lgT_ready"), sem("lgT_taken"), sem("lg_ready")
        mxl_ready, exp_ready, score_ready = sem("mxl_ready"), sem("exp_ready"), sem("score_ready")
        oh_ready, rank_ready, pos_ready = sem("oh_ready"), sem("rank_ready"), sem("pos_ready")
        xs_ready, scattered = sem("xs_ready"), sem("scattered")
        list_ready, tables_ready, filled_ready = sem("list_ready"), sem("tables_ready"), sem("filled_ready")
        w_in = [sem(f"w_in{s}") for s in range(WS)]
        w_here = sem("w_here")
        xg_in = [sem(f"xg_in{s}") for s in range(RS)]
        wh_ready, wl_ready = sem("wh_ready"), sem("wl_ready")
        te_ready, xh_ready, xl_ready = sem("te_ready"), sem("xh_ready"), sem("xl_ready")
        ge_ready, ue_ready, silu_ready, he_ready = sem("ge_ready"), sem("ue_ready"), sem("silu_ready"), sem("he_ready")
        th_ready, hT_ready, de_ready = sem("th_ready"), sem("hT_ready"), sem("de_ready")
        yo_ready, yo_out = sem("yo_ready"), [sem(f"yo_out{s}") for s in range(2)]
        gathered = [sem(f"gathered{n}") for n in range(4)]
        out_ready, stored = sem("out_ready"), sem("stored")

        def ahead(i, s, d):
            return i * RS + (s + d), (s + d) % RS, i + (s + d) // RS, i * (RS // 2) + (s + d) // 2

        def load_rows(eng, t, slot_):
            src = xg_d.rearrange("(t p) c -> t p c", p=P)[bass.ds(t, 1)].rearrange("o p c -> (o p) c")
            eng.dma_start(xg[slot_][:], src).then_inc(xg_in[slot_], 16)

        block = ctx.enter_context(nc.Block())

        @block.sync
        def _(sp):
            def rows(w):
                return w.rearrange("(t p) n -> p t n", p=P)

            def load_context_and_weights():
                sp.dma_start(ctx_s[:], ctxT.rearrange("(t p) n -> p t n", p=CK)).then_inc(in_ctx, 16)
                sp.dma_start(wkx_s[:], wkx.rearrange("(t p) n -> p t n", p=CK)).then_inc(in_ctx, 16)
                sp.dma_start(wvx_s[:], wvx.rearrange("(t p) n -> p t n", p=CK)).then_inc(in_wvx, 16)
                sp.dma_start(x_all[:], x.rearrange("b (k p) c -> p (b k) c", p=P)).then_inc(in_x, 16)
                for n, w in enumerate((wq, wk, wv)):
                    sp.dma_start(wqkv[:, :, n, :], rows(w)).then_inc(in_qkv, 16)
                for n, b_ in enumerate((bq, bk)):
                    sp.dma_start(bqk[:, 2 * n:2 * n + 2], b_.rearrange("(t p) -> p t", p=P), allow_slow_non_contiguous=True).then_inc(in_qkv, 16)
                sp.dma_start(bv_s[:], bcast_rows(bv)).then_inc(in_qkv, 16)
                sp.dma_start(bo_s[:], bcast_rows(bo)).then_inc(in_rest, 16)
                sp.dma_start(box_s[:], bcast_rows(box)).then_inc(in_rest, 16)
                sp.dma_start(wo_s[:], rows(wo)).then_inc(in_rest, 16)
                sp.dma_start(wr_s[:], rows(wr)).then_inc(in_rest, 16)
                sp.wait_ge(ready_zero, 1)
                for t in range(NT):
                    sp.dma_start(xg_d[t * P:(t + 1) * P, :], zeros[:]).then_inc(zero_rows, 16)
                for t in range(E, NT):
                    sp.dma_start(yg_d[t * P:(t + 1) * P, :], zeros[:]).then_inc(zero_rows, 16)

            def store_parts(b, cc):
                c = b * 2 + cc
                for j, (ready, done) in enumerate(((hi_ready, hi_out), (mid_ready, mid_out), (lo_ready, lo_out))):
                    for qk in range(2):
                        dst = parts_d[j, qk, bass.ds(b, 1), :, bass.ds(cc * CT, CT)].rearrange("o (m p) t -> p (o m) t", p=P)
                        if qk == 0:
                            sp.wait_ge(ready, c + 1)
                        sp.dma_start(dst, qp[:, j, 2 * qk:2 * qk + 2, :]).then_inc(done, 16)

            def load_stacks(g, s):
                for part, st, qk in ((Q_PART, qst, 0), (K_PART, kst, 1)):
                    for j, n in RUNS:
                        if qk == 0:
                            src = parts_d[part[j]:part[j] + 1, qk].to_broadcast((n, B, C, S))
                        else:
                            src = parts_d[part[j]:part[j] + n, qk]
                        src = src.rearrange("a b (g d h) t -> a (b g) d (h t)", h=GH, d=HD)[:, bass.ds(g, 1)]
                        sp.dma_start(st[s][HD * j:HD * (j + n), :, :].rearrange("p h t -> p (h t)"),
                                     src.rearrange("a o d n -> a (o d) n")).then_inc(q_in[s], 16)

            def load_shift(g, s):
                sp.wait_ge(shift_ready, g + 1)
                for j in range(3):
                    sp.dma_start(qst[s][KROWS + j:KROWS + j + 1, :, :].rearrange("o h (b q) -> o (h b) q", q=P),
                                 nmp[:, j, :]).then_inc(shift_in[s], 16)

            load_context_and_weights()
            sp.wait_ge(vc_act, 4)
            sp.wait_ge(vc_dve, 4)
            sp.dma_start(vx_d.rearrange("b (k p) n -> p b k n", p=SK // 2), vtmp[:]).then_inc(vc_out, 16)
            sp.sem_inc(hi_out, 32)
            sp.sem_inc(mid_out, 32)
            sp.sem_inc(lo_out, 32)
            store_parts(0, 0)
            store_parts(0, 1)
            store_parts(1, 0)
            for done in (hi_out, mid_out, lo_out):
                sp.wait_ge(done, 32 * (NCH // 2 + 2))
            load_stacks(0, 0)
            store_parts(1, 1)
            load_stacks(1, 1)
            load_stacks(2, 2)
            for done in (hi_out, mid_out, lo_out):
                sp.wait_ge(done, 32 * (NCH + 1))
            load_shift(0, 0)
            for g in range(GS, NG):
                load_shift(g - 2, (g - 2) % GS)
                sp.wait_ge(s_ready, (g - GS + 1) * NST * GH)
                load_stacks(g, g % GS)
            for g in range(NG - 2, NG):
                load_shift(g, g % GS)

            sp.wait_ge(o_copied, 2 * NG + 1)
            sp.wait_ge(m_taken, MT_ALL)
            sp.dma_start(wqx_s[:], rows(wqx)).then_inc(in_cross, 16)
            sp.dma_start(wox_s[:], rows(wox)).then_inc(in_cross, 16)
            sp.dma_start(wsg_s[:], rows(wsg)).then_inc(in_shared, 16)
            sp.dma_start(wsu_s[:], rows(wsu)).then_inc(in_shared, 16)
            sp.dma_start(wsd_s[:], rows(wsd)).then_inc(in_shared, 16)
            sp.wait_ge(vc_out, 16)
            with sp.Fori(0, B) as b:
                sp.wait_ge(vx_free, b + 1)
                src = vx_d[bass.ds(b, 1)].rearrange("o k (m h d) -> (o k) m h d", m=PAIRS, h=2)
                split = 2 * KC - SK
                for first, end, c, h, key in ((0, KC, 0, 0, 0), (0, SK - KC, 1, 0, KC), (SK - KC, KC, 1, 1, 0), (0, SK - split, 2, 1, split)):
                    sp.dma_start(vx[first:end, :, c, XD * h:XD * h + XD], src[key:key + end - first, :, h, :]).then_inc(vx_in, 16)

            def load_expert(j, s):
                e = sp.value_load(expert[0:1, bass.ds(j, 1)], min_val=0, max_val=E - 1)
                sp.dma_start(wgu_s[:, s], wgu[bass.ds(e, 1)].rearrange("o (t p) n -> p (o t) n", p=P)).then_inc(w_in[s], 16)
                sp.dma_start(wdn_s[:, s], wdn[bass.ds(e, 1)].rearrange("o (t p) n -> p (o t) n", p=P)).then_inc(w_in[s], 16)

            def next_expert(i, s):
                wait_apart(sp, "sp", w_in[(s - 2) % WS], (i + (s + WS - 2) // WS) * 32)
                sp.sem_inc(w_here, 1)
                done = sp.value_load(freed[0:1, bass.ds(i * WS + (s - WS), 1)], min_val=1, max_val=NT + 1)
                wait_apart(sp, "sp", de_ready, done)
                load_expert(i * WS + s, s)

            sp.wait_ge(list_ready, 1)
            load_expert(0, 0)
            sp.wait_ge(scattered, 16 * NBLK)
            for t in range(RS):
                load_rows(sp, t, t)
            for s in range(1, WS):
                load_expert(s, s)
            sp.wait_ge(tables_ready, 1)
            for s in range(WS - 2):
                sp.wait_ge(w_in[s], 32)
                sp.sem_inc(w_here, 1)
            with sp.Fori(1, E // WS) as i:
                for s in range(WS):
                    next_expert(i, s)
            for s in range(E % WS):
                next_expert(E // WS, s)
            for j in (E - 2, E - 1):
                sp.wait_ge(w_in[j % WS], 32 * (j // WS + 1))
                sp.sem_inc(w_here, 1)
            for n in range(4):
                sp.wait_ge(out_ready, n + 1)
                sp.dma_start(out.rearrange("b (k p) c -> p (b k) c", p=P)[:, 4 * n:4 * n + 4, :], x_all[:, 4 * n:4 * n + 4, :]).then_inc(stored, 16)
            sp.wait_ge(stored, 64)
            for s in range(2):
                sp.wait_ge(yo_out[s], 16 * ((NT + 1 - s) // 2 + 1))

        @block.gpsimd
        def _(pool):
            chain = Chain(pool, "pool_chain")

            def do(ins):
                chain.add(ins)
                chain.wait()

            def tri(t, op, fill, base=0):
                return pool.affine_select(out=t[:], in_=t[:], compare_op=op, fill=fill, base=base,
                                          pattern=[[-1, P]], channel_multiplier=1)

            def powers(ready, done, turn, half=0):
                wait_apart(pool, "pool", ready, turn + 1)
                do(pool.tensor_scalar(vpe[:, half], mv[:, half, :, 1], EPS, None, ALU.add))
                pool.tensor_tensor(rstd[:, half], vpe[:, half], mhalf[:], ALU.pow).then_inc(done, 1)

            do(pool.memset(zeros[:], 0.0))
            pool.sem_inc(ready_zero, 1)
            do(pool.memset(ident[:], 0.0))
            do(tri(ident, ALU.not_equal, 1.0))
            do(pool.memset(identb[:], 0.0))
            do(tri(identb, ALU.not_equal, 1.0))
            pool.sem_inc(ready_const, 1)
            do(pool.memset(kx[:], 0.0))
            pool.sem_inc(ready_zero, 1)
            do(pool.memset(mhalf[:], -0.5))
            with pool.Fori(0, NCH) as c:
                chain.turn(c, 1)
                powers(var_ready, rstd_ready, c)
            chain.turned(NCH)
            do(pool.memset(maskq[:], 0.0))
            do(tri(maskq, ALU.is_ge, NEG))
            do(pool.memset(maskk[:], NEG))
            do(tri(maskk, ALU.is_gt, 0.0))
            do(pool.memset(before[:], 0.0))
            do(tri(before, ALU.is_ge, 1.0))
            do(pool.memset(onesb[:], 1.0))
            do(pool.memset(vx[:], 0.0))
            do(pool.memset(nmax[:], 0.0))
            for s in range(GS):
                do(pool.memset(vp[s][:, :, :, HD:VW], 1.0))
            for s in range(GS):
                do(pool.memset(kst[s][KROWS:KROWS_M, :, :], 1.0))
            pool.sem_inc(ready_zero, 1)

            pool.wait_ge(in_rest, 64)
            pool.wait_ge(xn_ready, NCH)
            for k in range(NBLK):
                ins = pool.tensor_tensor(x_all[:, k, :], x_all[:, k, :], bo_s[:], ALU.add)
                chain.add(ins)
            chain.wait()
            pool.sem_inc(bo_added, 1)

            def copy_values(g, s):
                src = v_all[:].rearrange("p b g k n -> p (b g) k n")[:, bass.ds(g, 1)].rearrange("p o k (h d) -> p (o k) h d", h=GH)
                pool.tensor_copy(vp[s][:, :, :, 0:HD], src).then_inc(vp_ready[s], 1)

            pool.wait_ge(v_taken, NCH + 1)
            for g in range(NG):
                if g >= GS:
                    pool.wait_ge(pv_done, (g - GS + 1) * NST + 2)
                copy_values(g, g % GS)

            pool.wait_ge(o_copied, 2 * NG + 1)
            do(pool.memset(px[:], 0.0))
            pool.sem_inc(vx_free, 1)
            for c in range(NCH + 1):
                if c < NCH:
                    powers(var2_ready, rstd2_ready, c, c % 2)
                if c >= 1:
                    pool.wait_ge(xn2_ready, c)
                    for k in range((c - 1) * CB, c * CB):
                        chain.add(pool.tensor_tensor(x_all[:, k, :], x_all[:, k, :], box_s[:], ALU.add))
                    chain.wait()
                    pool.sem_inc(box_added, 1)
            pool.wait_ge(in_shared, 48)
            for w, h, l in ((wsg_s, wsg_h, wsg_l), (wsu_s, wsu_h, wsu_l), (wsd_s, wsd_h, wsd_l)):
                do(pool.tensor_copy(h[:], w[:]))
                chain.add(pool.tensor_tensor(l[:], w[:], h[:].bitcast(F32), ALU.subtract))
            do(pool.tensor_copy(wr_hl[:, :, 0:E], wr_s[:]))
            do(pool.tensor_tensor(wr_hl[:, :, E:2 * E], wr_s[:], wr_hl[:, :, 0:E].bitcast(F32), ALU.subtract))
            pool.sem_inc(ws_split, 1)

            with pool.Fori(0, NCH) as c:
                chain.turn(c, 1)
                powers(var2_ready, rstd2_ready, c + NCH)
            chain.turned(NCH)

            pool.wait_ge(ox_act, NCH * PAIRS // 2)
            pool.wait_ge(ox_dve, NCH * PAIRS // 2)
            do(pool.iota(em99[:], [[1, E]], base=-99, channel_multiplier=0, allow_small_or_imprecise_dtypes=True))
            do(pool.iota(steps128[:], [[P, NBLK]], base=0, channel_multiplier=0, allow_small_or_imprecise_dtypes=True))
            do(pool.iota(tno[:], [[1, NTT]], base=0, channel_multiplier=0, allow_small_or_imprecise_dtypes=True))
            do(pool.memset(ones_e[:], 1.0))
            pool.sem_inc(tno_ready, 1)
            pool.wait_ge(zero_rows, 16 * (2 * NT - E))
            pool.wait_ge(pos_ready, 1)
            for k in range(NBLK):
                pool.wait_ge(xs_ready, k + 1)
                pool.indirect_dma_start(out=xg_d, out_offset=bass.IndirectOffsetOnAxis(ap=pos[:, k:k + 1], axis=0),
                                        in_=xn_all[:, k, :], in_offset=None).then_inc(scattered, 16)
            pool.wait_ge(filled_ready, 1)
            pool.wait_ge(scattered, 16 * NBLK)
            counts = [pool.value_load(filled[0:1, s:s + 1], min_val=16 * (E // 2 + 1), max_val=16 * (NTT // 2 + 1)) for s in range(2)]
            for s in range(2):
                wait_apart(pool, "pool", yo_out[s], counts[s])
            for k in range(NBLK):
                pool.indirect_dma_start(out=xn_all[:, k, :], out_offset=None, in_=yg_d,
                                        in_offset=bass.IndirectOffsetOnAxis(ap=pos[:, k:k + 1], axis=0)).then_inc(gathered[k // 4], 16)
            pool.wait_ge(ds_taken, NCH + 1)
            for n in range(4):
                pool.wait_ge(gathered[n], 64)
                for k in range(4 * n, 4 * n + 4):
                    ins = pool.tensor_tensor(x_all[:, k, :], x_all[:, k, :], xn_all[:, k, :], ALU.add)
                    chain.add(ins)
                chain.wait()
                pool.sem_inc(out_ready, 1)

        @block.scalar
        def _(act):
            act.sem_inc(p_ready, S_SLOTS)
            act.sem_inc(qk_taken, 1)

            act.wait_ge(ready_zero, 2)
            for m in range(PAIRS):
                act.wait_ge(kx_ready, m + 1)
                act.copy(kx[0:XD, :, m, 0:SK], ps[0:XD, m % 4, 0:B * SK].rearrange("p (b k) -> p b k", b=B)).then_inc(kx_act, 1)
            for n in range(0, 8, 2):
                act.wait_ge(vc_ready, n + 1)
                act.copy(vtmp[:, n // 4, n // 2 % 2, 0:512], ps[0:SK // 2, 4 + n % 4, :]).then_inc(vc_act, 1)

            act.wait_ge(in_qkv, 96)
            act.wait_ge(vc_out, 16)
            with act.Fori(0, NCH) as c:
                act.wait_ge(t1_ready, c + 1)
                act.copy(xnT[:], ps[:, 0:2, :]).then_inc(xnT_ready, 1)
                act.wait_ge(qf_free, c + 1)
                act.wait_ge(hi_out, c * 32 + 32)
                for n in range(4):
                    act.wait_ge(qk_ready, c * 4 + (n + 1))
                    act.activation(qf[:, n, :], ps[:, 2 + n, :], ACT.Identity, bias=bqk[:, n:n + 1])
                    ins = act.activation(qp[:, 0, n, :], ps[:, 2 + n, :], ACT.Identity, bias=bqk[:, n:n + 1])
                ins.then_inc(hi_ready, 1)
                act.wait_ge(hi_ready, c + 1)
                act.sem_inc(qk_taken, 1)

            def exps(g, k):
                qc, kb = STEPS[k]
                n = (qc + 1) * CT - max(qc * CT, kb * P)
                act.wait_ge(pv_done, g * NST + (k + 1))
                for h in range(GH):
                    v = k * GH + h
                    act.wait_ge(s_ready, g * (NST * GH) + (v + 1))
                    act.activation(probs[:, v % P_SLOTS, 0:n], ps[:, 4 + v % S_SLOTS, 0:n], ACT.Exp, scale=SELF_SCALE).then_inc(p_ready, 1)

            for done in (hi_out, mid_out, lo_out):
                act.wait_ge(done, 32 * (NCH + 1))
            act.wait_ge(v_taken, NCH + 1)
            def copy_output(g, qc):
                act.wait_ge(pv_done, g * NST + ((CB, NST)[qc] + 2))
                act.copy(osb[:, qc, :], ps[:, 7, :]).then_inc(o_copied, 1)

            def steps_from_2(g):
                for k in range(2, NST):
                    exps(g, k)
                    if k == CB:
                        copy_output(g, 0)

            exps(0, 0)
            exps(0, 1)
            with act.Fori(0, NG - 1) as g:
                steps_from_2(g)
                exps(g + 1, 0)
                copy_output(g, 1)
                exps(g + 1, 1)
            steps_from_2(NG - 1)
            copy_output(NG - 1, 1)

            act.wait_ge(m_taken, MT_ALL)
            def copy_normed(c):
                act.wait_ge(t2_ready, c + 1)
                act.copy(xnT_all[:, :, c * CT:(c + 1) * CT], ps[:, 6:8, :]).then_inc(xnT2_ready, 1)

            for c in range(NCH):
                act.wait_ge(ty_ready, c + 1)
                if c >= 2:
                    act.wait_ge(wo_done, c - 1)
                act.copy(yT[c % 2][:], ps[:, 0:2, :]).then_inc(yT_ready, 1)
                if c == NCH - 1:
                    copy_normed(0)
            for c in range(1, NCH):
                copy_normed(c)

            act.wait_ge(vx_free, 1)
            with act.Fori(0, NCH) as c:
                for m in range(PAIRS):
                    act.wait_ge(qx_ready, c * PAIRS + (m + 1))
                    act.activation(qT[:, m, :], ps[:, 4 + m % 4, :], ACT.Copy, scale=XSCALE).then_inc(qx_taken, 1)
                for u in range(XU + PV_LAG + 2):
                    w = u - T_LAG - 1
                    if 0 <= w < XU and w % 2 == 0:
                        act.wait_ge(tx_ready, c * XU + (w + 1))
                        if w // CB >= 2:
                            act.wait_ge(ox_ready, c * PAIRS + (w // CB - 1))
                        act.copy(pT[0:KC, w // CB % 2, :, w % CB * P:(w % CB + 1) * P],
                                 ps[0:KC, 6, 0:NKC * P].rearrange("p (c q) -> p c q", c=NKC)).then_inc(tx_act, 1)
                    if u < XU:
                        if u >= 4:
                            act.wait_ge(tx_ready, c * XU + (u - 3))
                        act.wait_ge(mx_ready, c * XU + (u + 1))
                        for h in range(2):
                            ins = act.activation(px[:, u % 4, SK * h:SK * h + SK], ps[:, (0, 1, 4, 5)[u % 4], SK * h:SK * h + SK], ACT.Exp,
                                                 bias=nmx[:, u % 4, h:h + 1], accum_out=smx[:, u % 4, h:h + 1])
                        ins.then_inc(ex_ready, 1)
                    w = u - PV_LAG - 1
                    if w % CB == CB - 1 and w > 0 and w // CB % 2 == 0 and w // CB < PAIRS:
                        act.wait_ge(ox_ready, c * PAIRS + (w // CB + 1))
                        act.copy(qT[:, w // CB, :], ps[:, 2, :]).then_inc(ox_act, 1)

            def copy_turned(c):
                act.wait_ge(t3_ready, c + 1)
                act.copy(xnT_h[:, :, c * CT:(c + 1) * CT], ps[:, 4 + c % 2 * 2:6 + c % 2 * 2, :]).then_inc(xnT3_ready, 1)

            def silu_shared(c):
                for m in range(FF + 1):
                    if m < FF:
                        act.wait_ge(gs_ready, c * FF + (m + 1))
                        act.wait_ge(hs_ready, c * FF + (m + 1))
                        act.activation(sgl[:, m % 2, :], ps[:, (2, 6)[m % 2], :], ACT.Silu).then_inc(gs_silu, 1)
                    if m >= 1:
                        act.wait_ge(prod_ready, c * FF + m)
                        act.copy(shT_h[:, m - 1, :], prod[:, (m - 1) % 2, :]).then_inc(shh_ready, 1)

            for c in range(2):
                copy_turned(c)
            silu_shared(0)
            for c in range(2, NCH):
                copy_turned(c)
            for n in range(2):
                act.wait_ge(lgT_ready, 2 * n + 2)
                act.copy(lgT[n][0:2 * E], ps[0:2 * E, 2 * n:2 * n + 2, :]).then_inc(lgT_taken, 1)
            silu_shared(1)
            act.wait_ge(mxl_ready, 1)
            act.activation(emx[:], mx[:], ACT.Exp, scale=-1.0).then_inc(exp_ready, 1)
            act.wait_ge(score_ready, 1)
            for k in range(NBLK):
                act.activation(xn_all[:, k, :], xn_all[:, k, :], ACT.Copy, scale=score[:, k:k + 1]).then_inc(xs_ready, 1)
            silu_shared(2)
            silu_shared(3)

            for s in range(2):
                act.sem_inc(yo_out[s], 16)
            act.wait_ge(zero_rows, 16 * (2 * NT - E))

            def expert_of(i, s, d):
                t, _, _, _ = ahead(i, s, d)
                return (act.value_load(need[0:1, bass.ds(t, 1)], min_val=1, max_val=E),
                        act.value_load(slot[0:1, bass.ds(t, 1)], min_val=0, max_val=WS - 1))

            def part_high(i, s, d, expert=None):
                t, _, _, _ = ahead(i, s, d)
                p = (s + d) % 2
                count, at = expert or expert_of(i, s, d)
                wait_apart(act, "act", w_here, count)
                if not (isinstance(t, int) and t < 2):
                    act.wait_ge(ue_ready, t - 1)
                act.copy(wgu_h[p][:], wgu_s[:, bass.ds(at, 1)].rearrange("p o f n -> p (o f) n")).then_inc(wh_ready, 1)

            def rows_high(i, s, d):
                t, _, _, _ = ahead(i, s, d)
                act.wait_ge(te_ready, t + 1)
                act.copy(xgT_h[(s + d) % 2][:], ps[:, 0, 0:C].rearrange("p (f q) -> p f q", f=FC)).then_inc(xh_ready, 1)

            def silu(i, s, d):
                t, _, _, _ = ahead(i, s, d)
                p = (s + d) % 2
                act.wait_ge(ge_ready, t + 1)
                act.activation(act_s[p][:], ps[:, 2 + 2 * p, :], ACT.Silu).then_inc(silu_ready, 1)

            def take_turned(i, s):
                t, _, _, _ = ahead(i, s, 0)
                act.wait_ge(th_ready, t + 1)
                act.copy(hT[s % 2][:], ps[:, 1, :].rearrange("p (f q) -> p f q", f=FF)).then_inc(hT_ready, 1)

            def take_output(i, s):
                t, _, _, used_before = ahead(i, s, 0)
                p = s % 2
                act.wait_ge(de_ready, t + 2)
                act.wait_ge(yo_out[p], (used_before + 1) * 16)
                act.copy(yo[p][:], ps[:, 6 + p, 0:C]).then_inc(yo_ready, 1)

            def put_rows(i, s, d):
                t, _, _, _ = ahead(i, s, d)
                p = (s + d) % 2
                dst = yg_d.rearrange("(t p) c -> t p c", p=P)[bass.ds(t, 1)].rearrange("o p c -> (o p) c")
                act.wait_ge(yo_ready, t + 1)
                act.dma_start(dst, yo[p][:]).then_inc(yo_out[p], 16)

            act.wait_ge(us_taken, NCH * FF + 2)
            act.wait_ge(tables_ready, 1)
            part_high(0, 0, 0)
            rows_high(0, 0, 0)
            part_high(0, 0, 1)
            silu(0, 0, 0)
            rows_high(0, 0, 1)
            part_high(0, 0, 2)

            def act_tile(i, s, left=NT):
                if left > 3:
                    expert = expert_of(i, s, 3)
                take_turned(i, s)
                if left > 1:
                    silu(i, s, 1)
                if left > 2:
                    rows_high(i, s, 2)
                if not (isinstance(i, int) and i == 0 and s == 0):
                    put_rows(i, s, -1)
                if left > RS:
                    t, slot_, _, _ = ahead(i, s, RS)
                    act.wait_ge(te_ready, t + (1 - RS))
                    load_rows(act, t, slot_)
                if left > 3:
                    part_high(i, s, 3, expert)
                take_output(i, s)
                if left == 1:
                    put_rows(i, s, 0)

            for s in range(RS):
                act_tile(0, s)
            with act.Fori(1, NT // RS - 1) as i:
                for s in range(RS):
                    act_tile(i, s)
            for t in range((NT // RS - 1) * RS, NT):
                act_tile(t // RS, t % RS, left=NT - t)

        @block.tensor
        def _(pe):
            def mm(out_, lhsT, rhs, start, stop):
                return pe.matmul(out_, lhsT, rhs, start=start, stop=stop, skip_group_check=True)

            pe.wait_ge(in_ctx, 32)
            for m in range(PAIRS):
                if m >= 4:
                    pe.wait_ge(kx_act, m - 3)
                    pe.wait_ge(kx_dve, m - 3)
                for t in range(2):
                    ins = mm(ps[:, m % 4, 0:B * SK], wkx_s[:, t, m * P:(m + 1) * P], ctx_s[:, t, :], t == 0, t == 1)
                ins.then_inc(kx_ready, 1)
            pe.wait_ge(in_wvx, 16)
            for n in range(8):
                b, k, half = n // 4, n // 2 % 2, n % 2
                if n >= 4:
                    pe.wait_ge((vc_act, vc_dve)[n % 2], (n - 4) // 2 + 1)
                r0 = b * SK + k * (SK // 2)
                for t in range(2):
                    ins = mm(ps[0:SK // 2, 4 + n % 4, :], ctx_s[:, t, r0:r0 + SK // 2], wvx_s[:, t, half * 512:half * 512 + 512], t == 0, t == 1)
                ins.then_inc(vc_ready, 1)

            def turn_rows(src, bank, done):
                for k in range(CB):
                    for f in range(FC):
                        ins = pe.transpose(ps[:, bank + f, k * P:(k + 1) * P], src(k, f), ident[:])
                ins.then_inc(done, 1)

            pe.wait_ge(ready_const, 1)
            pe.wait_ge(in_qkv, 96)
            pe.wait_ge(vc_act, 4)
            pe.wait_ge(vc_dve, 4)
            pe.wait_ge(kx_act, PAIRS)
            pe.wait_ge(kx_dve, PAIRS)
            for c in range(NCH):
                pe.wait_ge(xn_ready, c + 1)
                turn_rows(lambda k, f: xn_all[:, c * CB + k, f * P:(f + 1) * P], 0, t1_ready)
                pe.wait_ge(xnT_ready, c + 1)
                pe.wait_ge(qk_taken, c + 1)
                for n in range(4):
                    for f in range(FC):
                        ins = mm(ps[:, 2 + n, :], wqkv[:, f, n // 2, n % 2 * P:(n % 2 + 1) * P], xnT[:, f, :], f == 0, f == FC - 1)
                    ins.then_inc(qk_ready, 1)
                pe.wait_ge(v_taken, c + 1)
                for k in range(CB):
                    for f in range(FC):
                        ins = mm(ps[:, 6 + k // 2, k % 2 * C:(k % 2 + 1) * C], xnT[:, f, k * P:(k + 1) * P], wqkv[:, f, 2, :], f == 0, f == FC - 1)
                ins.then_inc(v_ready, 1)

            def max_unit(use, s, u):
                h, qb = UNITS[u]
                keys = (qb + 1) * P
                slot = 2 * use.slot
                pe.wait_ge(m_taken, use.free)
                lhsT = qst[s][0:KROWS, h, qb * P:(qb + 1) * P]
                for k0 in range(0, keys, 512):
                    n = min(512, keys - k0)
                    mm(ps[:, slot + k0 // 512, 0:n], lhsT, kst[s][0:KROWS, h, k0:k0 + n], True, False)
                d = qb * P
                mm(ps[:, slot + d // 512, d % 512:d % 512 + P], identb[:], maskq[:], False, True).then_inc(m_ready, 1)

            def turn_max(use):
                pe.wait_ge(m_taken, use.n + 2)
                pe.transpose(ps[:, 2 * use.slot, 0:P], nmax[:], ident[:]).then_inc(m_ready, 1)

            def turn_output(use, g, qc):
                pe.wait_ge(o_copied, g * 2 + (qc + 2))
                pe.wait_ge(m_taken, use.free)
                for k in range(CB):
                    ins = pe.transpose(ps[:, 2 * use.slot, k * P:(k + 1) * P], osb[:, qc, k * P:(k + 1) * P], ident[:])
                ins.then_inc(m_ready, 1)

            def scores(g, s, k, between=None):
                qc, kb = STEPS[k]
                q0 = max(qc * CT, kb * P)
                n = (qc + 1) * CT - q0
                for h in range(GH):
                    v = k * GH + h
                    bank = 4 + v % S_SLOTS
                    pe.wait_ge(p_ready, g * (NST * GH) + (v + 1))
                    ins = mm(ps[:, bank, 0:n], kst[s][0:KROWS_M, h, kb * P:(kb + 1) * P], qst[s][0:KROWS_M, h, q0:q0 + n], True, False)
                    if kb * P >= qc * CT:
                        ins = mm(ps[:, bank, 0:P], identb[:], maskk[:], False, True)
                    ins.then_inc(s_ready, 1)
                    if between:
                        between(h)

            def values(g, s, k):
                qc, kb = STEPS[k]
                q0 = max(qc * CT, kb * P)
                n = (qc + 1) * CT - q0
                if k in (0, CB):
                    pe.wait_ge(o_copied, g * 2 + (qc + 1))
                pe.wait_ge(p_ready, g * (NST * GH) + (k * GH + GH + S_SLOTS))
                for h in range(GH):
                    ins = mm(ps[VW * h:VW * h + VW, 7, q0 - qc * CT:CT], vp[s][:, kb, h, :], probs[:, (k * GH + h) % P_SLOTS, 0:n],
                             k in (0, CB), k in (CB - 1, NST - 1))
                ins.then_inc(pv_done, 1)

            pe.wait_ge(ready_zero, 3)
            pe.wait_ge(v_taken, NCH + 1)
            pe.wait_ge(qk_taken, NCH + 1)
            pe.wait_ge(q_in[0], 16 * 2 * len(RUNS))
            for u in range(NU):
                max_unit(use_before(u), 0, u)
            turn_max(use_before(NU))

            def with_units(k, use, s):
                units = units_of(k)

                def some(h):
                    for u in units[len(units) * h // GH:len(units) * (h + 1) // GH]:
                        max_unit(use(u), s, u)
                return some

            def stack_in(s, before_):
                pe.wait_ge(q_in[s], (before_ + 1) * (16 * 2 * len(RUNS)))

            def steps_from_2(g, s, next_one):
                for k in range(2, NST):
                    if next_one and k in UNITS_AT:
                        scores(g, s, k, with_units(k, lambda u: use_of(g, "unit", u), (s + 1) % GS))
                    elif next_one and k == SPLIT_STEP:
                        scores(g, s, k, lambda h: turn_max(use_of(g, "max")) if h == 1 else None)
                    else:
                        scores(g, s, k)
                    if k == TURN_STEP:
                        turn_output(use_of(g, "out0"), g, 0)
                    values(g, s, k - 1)

            def turn_group(g, s, i, second_next):
                steps_from_2(g, s, True)
                s1, before_ = (s + 1) % GS, i + (s + 1) // GS
                pe.wait_ge(vp_ready[s1], before_ + 1)
                pe.wait_ge(shift_in[s1], (before_ + 1) * 48)
                early_units = [None, None]
                if second_next:
                    s2 = (s + 2) % GS
                    stack_in(s2, i + (s + 2) // GS)
                    early_units = [with_units(k, lambda u: use_of(g, "early", u), s2) for k in range(2)]
                scores(g + 1, s1, 0, early_units[0])
                values(g, s, NST - 1)
                scores(g + 1, s1, 1, early_units[1])
                turn_output(use_of(g, "out1"), g, 1)
                values(g + 1, s1, 0)

            pe.wait_ge(vp_ready[0], 1)
            pe.wait_ge(shift_in[0], 48)
            stack_in(1, 0)
            for k in range(2):
                scores(0, 0, k, with_units(k, lambda u: use_before(NU + 1 + u), 1))
            values(0, 0, 0)
            with pe.Fori(0, (NG - 2) // GS) as i:
                for s in range(GS):
                    turn_group(i * GS + s, s, i, True)
            turn_group(NG - 2, (NG - 2) % GS, (NG - 2) // GS, False)
            steps_from_2(NG - 1, (NG - 1) % GS, False)
            values(NG - 1, (NG - 1) % GS, NST - 1)
            turn_output(use_of(NG - 1, "out1"), NG - 1, 1)

            pe.wait_ge(in_rest, 64)
            pe.wait_ge(m_taken, MT_ALL)
            pe.wait_ge(p_ready, NG * NST * GH + S_SLOTS)

            def project(c):
                pe.wait_ge(yT_ready, c + 1)
                for k in range(CB):
                    for f in range(FC):
                        ins = mm(ps[:, 2 + c % 2 * 2 + k // 2, k % 2 * C:(k % 2 + 1) * C], yT[c % 2][:, f, k * P:(k + 1) * P], wo_s[:, f, :], f == 0, f == FC - 1)
                ins.then_inc(wo_done, 1)

            def turn_normed(c):
                pe.wait_ge(xn2_ready, c + 1)
                if c >= 1:
                    pe.wait_ge(xnT2_ready, c)
                turn_rows(lambda k, f: xn_all[:, c * CB + k, f * P:(f + 1) * P], 6, t2_ready)

            def turn_y(c):
                b, qb = c // 2, c % 2 * CB
                if c >= 1:
                    pe.wait_ge(yT_ready, c)
                turn_rows(lambda k, f: y_tok[:, qb + k, (b * FC + f) * P:(b * FC + f + 1) * P], 0, ty_ready)

            turn_y(0)
            for c in range(NCH):
                if c + 1 < NCH:
                    turn_y(c + 1)
                if c >= 2:
                    pe.wait_ge(x1_ready, c - 1)
                project(c)
                if c >= 2:
                    turn_normed(c - 2)
            turn_normed(NCH - 2)
            turn_normed(NCH - 1)
            pe.wait_ge(in_cross, 32)
            pe.wait_ge(xnT2_ready, NCH)
            with pe.Fori(0, B) as b:
                wait_apart(pe, "pe", vx_in, b * 64 + 64)
                with pe.Fori(0, S // CT) as cc:
                    c = b * 2 + cc
                    for m in range(PAIRS):
                        if m >= 4:
                            pe.wait_ge(qx_taken, c * PAIRS + (m - 3))
                        for f in range(FC):
                            ins = mm(ps[:, 4 + m % 4, :], wqx_s[:, f, m * P:(m + 1) * P], xnT_all[:, f, bass.ds(c * CT, CT)], f == 0, f == FC - 1)
                        ins.then_inc(qx_ready, 1)
                    pe.wait_ge(qx_taken, c * PAIRS + PAIRS)
                    pe.wait_ge(x2_ready, c + 1)
                    for u in range(XU + PV_LAG + 1):
                        if u < XU:
                            pair, k = u // CB, u % CB
                            if u >= 4:
                                pe.wait_ge(ex_ready, c * XU + (u - 3))
                            mm(ps[:, (0, 1, 4, 5)[u % 4], 0:PK], qT[:, pair, k * P:(k + 1) * P],
                               kx[:, bass.ds(b, 1), pair, :].rearrange("p o k -> p (o k)"), True, True).then_inc(sx_ready, 1)
                        w = u - T_LAG
                        if 0 <= w < XU:
                            pe.wait_ge(px_ready, c * XU + (w + 1))
                            if w >= 2:
                                pe.wait_ge((tx_act, tx_dve)[w % 2], c * (XU // 2) + w // 2)
                            for j in range(NKC):
                                ins = pe.transpose(ps[0:KC, 6 + w % 2, j * P:(j + 1) * P], px[:, w % 4, j * KC:(j + 1) * KC], ident[:])
                            ins.then_inc(tx_ready, 1)
                        w = u - PV_LAG
                        if 0 <= w < XU:
                            pair, k = w // CB, w % CB
                            pe.wait_ge((tx_act, tx_dve)[w % 2], c * (XU // 2) + (w // 2 + 1))
                            if pair >= 2 and k == 0:
                                pe.wait_ge((ox_act, ox_dve)[pair % 2], c * (PAIRS // 2) + pair // 2)
                            for j in range(NKC):
                                ins = mm(ps[:, 2 + pair % 2, k * P:(k + 1) * P], vx[0:KC, pair, j, :], pT[0:KC, pair % 2, j, k * P:(k + 1) * P],
                                         j == 0, j == NKC - 1)
                            if k == CB - 1:
                                ins.then_inc(ox_ready, 1)
                    pe.wait_ge(ox_act, c * (PAIRS // 2) + PAIRS // 2)
                    pe.wait_ge(ox_dve, c * (PAIRS // 2) + PAIRS // 2)
                    for k in range(CB):
                        for m in range(PAIRS):
                            ins = mm(ps[:, k // 2, k % 2 * C:(k % 2 + 1) * C], qT[:, m, k * P:(k + 1) * P], wox_s[:, m, :], m == 0, m == PAIRS - 1)
                    ins.then_inc(wox_done, 1)
                pe.wait_ge(ox_dve, c * (PAIRS // 2) + PAIRS // 2)
                pe.sem_inc(vx_free, 1)

            def turn_for_moe(c):
                pe.wait_ge(xn3_ready, c + 1)
                if c >= 2:
                    pe.wait_ge(xnT3l_ready, c - 1)
                turn_rows(lambda k, f: xn_all[:, c * CB + k, f * P:(f + 1) * P], 4 + c % 2 * 2, t3_ready)

            def shared_expert(c, meanwhile=None):
                xh = xnT_h[:, :, bass.ds(c * CT, CT)]
                xl = xnT_l[:, :, bass.ds(c * CT, CT)]

                def by_parts(out_, parts, start, stop):
                    for n, (a, b_) in enumerate(parts):
                        ins = mm(out_, a, b_, start and n == 0, stop and n == 2)
                    return ins

                for m in range(FF):
                    pe.wait_ge(gs_silu, c * FF + (m + 1))
                    for f in range(FC):
                        wh, wl = wsg_h[:, f, m * P:(m + 1) * P], wsg_l[:, f, m * P:(m + 1) * P]
                        ins = by_parts(ps[:, (2, 6)[m % 2], :], ((wh, xh[:, f, :]), (wh, xl[:, f, :]), (wl, xh[:, f, :])), f == 0, f == FC - 1)
                    ins.then_inc(gs_ready, 1)
                    pe.wait_ge(us_taken, c * FF + (m + 1))
                    for f in range(FC):
                        wh, wl = wsu_h[:, f, m * P:(m + 1) * P], wsu_l[:, f, m * P:(m + 1) * P]
                        ins = by_parts(ps[:, (3, 7)[m % 2], :], ((wh, xh[:, f, :]), (wh, xl[:, f, :]), (wl, xh[:, f, :])), f == 0, f == FC - 1)
                    ins.then_inc(us_ready, 1)
                if meanwhile:
                    meanwhile()
                pe.wait_ge(ds_taken, c + 1)
                for m in range(FF):
                    pe.wait_ge(shl_ready, c * FF + (m + 1))
                    for k in range(CB):
                        h, l = (t[:, m, k * P:(k + 1) * P] for t in (shT_h, shT_l))
                        ins = by_parts(ps[:, 4 + k // 2, k % 2 * C:(k % 2 + 1) * C],
                                       ((h, wsd_h[:, m, :]), (h, wsd_l[:, m, :]), (l, wsd_h[:, m, :])),
                                       m == 0 and k % 2 == 0, m == FF - 1)
                ins.then_inc(ds_ready, 1)

            for c in range(2):
                turn_for_moe(c)
            pe.wait_ge(ws_split, 1)
            pe.wait_ge(xnT3l_ready, 2)
            shared_expert(0)
            pe.wait_ge(ds_taken, 2)
            for c in range(2, NCH):
                turn_for_moe(c)
            pe.wait_ge(x2_ready, NCH + 1)
            for c in range(NCH):
                pe.wait_ge(xnT3l_ready, c + 1)
                rows = slice(c * CT, (c + 1) * CT)
                for f in range(FC):
                    mm(ps[0:2 * E, c, :], wr_hl[:, f, :], xnT_h[:, f, rows], f == 0, f == FC - 1)
                    ins = mm(ps[0:E, c, :], wr_hl[:, f, 0:E], xnT_l[:, f, rows], False, f == FC - 1)
                ins.then_inc(lgT_ready, 1)
            pe.wait_ge(lgT_taken, 2)
            for k in range(NBLK):
                ins = pe.transpose(ps[:, 0, k * 2 * E:(k + 1) * 2 * E], lgT[k // (2 * CB)][0:2 * E, k // CB % 2, k % CB * P:(k % CB + 1) * P], ident[0:2 * E, 0:2 * E])
            ins.then_inc(lg_ready, 1)
            def ranks():
                pe.wait_ge(oh_ready, 1)
                mm(ps[:, 0, 0:NBLK * E], before[:], onehotb[:], True, False)
                for k in range(NBLK - 1):
                    n = NBLK - 1 - k
                    mm(ps[:, 0, (k + 1) * E:NBLK * E], onesb[:], onehotb[:, k:k + 1, :].to_broadcast((P, n, E)), False, k == NBLK - 2)
                for k in range(NBLK):
                    ins = mm(ps[:, 1, 0:E], onesb[:], onehotb[:, k, :], k == 0, k == NBLK - 1)
                ins.then_inc(rank_ready, 1)

            shared_expert(1, ranks)
            shared_expert(2)
            shared_expert(3)

            def turn_tile(i, s, d):
                _, slot_, before_, _ = ahead(i, s, d)
                pe.wait_ge(xg_in[slot_], before_ * 16 + 16)
                for f in range(FC):
                    ins = pe.transpose(ps[:, 0, f * P:(f + 1) * P], xg[slot_][:, f * P:(f + 1) * P], ident[:])
                ins.then_inc(te_ready, 1)

            def gate_up(i, s, d):
                t, _, _, _ = ahead(i, s, d)
                p = (s + d) % 2
                pe.wait_ge(wl_ready, t + 1)
                pe.wait_ge(xl_ready, t + 1)
                for half, done in ((0, ge_ready), (1, ue_ready)):
                    cols = slice(half * F, (half + 1) * F)
                    for f in range(FC):
                        xh, xl, wh, wl = xgT_h[p][:, f, :], xgT_l[p][:, f, :], wgu_h[p][:, f, cols], wgu_l[p][:, f, cols]
                        for n, (a, b_) in enumerate(((xh, wh), (xh, wl), (xl, wh))):
                            ins = mm(ps[:, 2 + 2 * p + half, :], a, b_, f == 0 and n == 0, f == FC - 1 and n == 2)
                    ins.then_inc(done, 1)

            def turn_hidden(i, s):
                t, _, _, _ = ahead(i, s, 0)
                pe.wait_ge(he_ready, t + 1)
                for m in range(FF):
                    ins = pe.transpose(ps[:, 1, m * P:(m + 1) * P], h_tok[s % 2][:, m * P:(m + 1) * P], ident[:])
                ins.then_inc(th_ready, 1)

            def down(i, s):
                t, _, _, _ = ahead(i, s, 0)
                at = pe.value_load(slot[0:1, bass.ds(t, 1)], min_val=0, max_val=WS - 1)
                pe.wait_ge(hT_ready, t + 1)
                for m in range(FF):
                    w = wdn_s[:, bass.ds(at, 1), m, :].rearrange("p o c -> p (o c)")
                    ins = mm(ps[:, 6 + s % 2, 0:C], hT[s % 2][:, m, :], w, m == 0, m == FF - 1)
                ins.then_inc(de_ready, 1)

            pe.sem_inc(de_ready, 1)
            pe.wait_ge(ds_taken, NCH + 1)
            pe.wait_ge(tables_ready, 1)
            turn_tile(0, 0, 0)
            gate_up(0, 0, 0)
            turn_tile(0, 0, 1)

            def tile(i, s, left=NT):
                turn_hidden(i, s)
                if left > 1:
                    gate_up(i, s, 1)
                if left > 2:
                    turn_tile(i, s, 2)
                down(i, s)

            with pe.Fori(0, NT // RS - 1) as i:
                for s in range(RS):
                    tile(i, s)
            for t in range((NT // RS - 1) * RS, NT):
                tile(t // RS, t % RS, left=NT - t)

        @block.vector
        def _(dve):
            chain = Chain(dve, "dve_chain")

            def do(ins):
                chain.add(ins)
                chain.wait()

            def norm_stats(block_of, var, half=0):
                for k in range(CB):
                    ins = dve.bn_stats(stats[:, k, :], block_of(k))
                    chain.add(ins)
                chain.wait_apart("dve")
                for k in range(CB):
                    ins = dve.bn_aggr(mv[:, half, k, :], stats[:, k, :])
                ins.then_inc(var, 1)

            def norm_scale(block_of, out_of, rst, done, turn, half=0):
                dve.wait_ge(rst, turn + 1)
                for k in range(CB):
                    ins = dve.tensor_scalar(out_of(k), block_of(k), mv[:, half, k, 0:1], rstd[:, half, k:k + 1], ALU.subtract, ALU.mult)
                ins.then_inc(done, 1)

            def norm(block_of, out_of, var, rst, done, turn):
                norm_stats(block_of, var)
                norm_scale(block_of, out_of, rst, done, turn)

            dve.sem_inc(v_taken, 1)
            dve.sem_inc(qf_free, 1)
            dve.sem_inc(m_taken, 2)
            dve.sem_inc(pv_done, 2)
            dve.sem_inc(o_copied, 1)
            dve.sem_inc(x2_ready, 1)

            dve.wait_ge(ready_zero, 2)
            for m in range(PAIRS):
                dve.wait_ge(kx_ready, m + 1)
                dve.tensor_copy(kx[XD:P, :, m, SK:PK], ps[XD:P, m % 4, 0:B * SK].rearrange("p (b k) -> p b k", b=B)).then_inc(kx_dve, 1)
            for n in range(1, 8, 2):
                dve.wait_ge(vc_ready, n + 1)
                dve.tensor_copy(vtmp[:, n // 4, n // 2 % 2, 512:1024], ps[0:SK // 2, 4 + n % 4, :]).then_inc(vc_dve, 1)

            dve.wait_ge(in_x, 16)
            with dve.Fori(0, NCH) as c:
                chain.turn(c, CB)
                norm(lambda k: x_all[:, bass.ds(c * CB + k, 1), :].rearrange("p o c -> p (o c)"),
                     lambda k: xn_all[:, bass.ds(c * CB + k, 1), :].rearrange("p o c -> p (o c)"),
                     var_ready, rstd_ready, xn_ready, c)
            chain.turned(NCH)
            dve.wait_ge(in_qkv, 96)
            with dve.Fori(0, B) as b:
                with dve.Fori(0, S // CT) as cc:
                    c = b * 2 + cc
                    dve.wait_ge(hi_ready, c + 1)
                    chain.turn(c, 1)
                    do(dve.tensor_tensor(qr[:], qf[:], qp[:, 0], ALU.subtract))
                    dve.sem_inc(qf_free, 1)
                    dve.wait_ge(mid_out, c * 32 + 32)
                    dve.tensor_copy(qp[:, 1], qr[:]).then_inc(mid_ready, 1)
                    dve.wait_ge(mid_ready, c + 1)
                    dve.wait_ge(lo_out, c * 32 + 32)
                    dve.tensor_tensor(qp[:, 2], qr[:], qp[:, 1], ALU.subtract).then_inc(lo_ready, 1)
                    dve.wait_ge(v_ready, c + 1)
                    for k in range(CB):
                        ins = dve.tensor_tensor(v_all[:, bass.ds(b, 1), :, bass.ds(cc * CB + k, 1), :].rearrange("p o g q n -> p (o g) (q n)"),
                                                ps[:, 6 + k // 2, k % 2 * C:(k % 2 + 1) * C].rearrange("p (g n) -> p g n", g=GH),
                                                bv_s[:].rearrange("p (g n) -> p g n", g=GH), ALU.add)
                    ins.then_inc(v_taken, 1)
                    dve.wait_ge(lo_ready, c + 1)
            chain.turned(NCH)

            def take_max(use, u):
                h, qb = UNITS[u]
                keys = (qb + 1) * P
                slot = 2 * use.slot
                dve.wait_ge(m_ready, use.n + 1)
                dve.tensor_reduce(nmax[:, h * QB + qb:h * QB + qb + 1], ps[:, slot:slot + 2, :].rearrange("p a n -> p (a n)")[:, 0:keys], AX.X, ALU.max,
                                  negate=True).then_inc(m_taken, 1)

            def split_max(use):
                dve.wait_ge(m_ready, use.n + 1)
                t = ps[0:NU, 2 * use.slot, 0:P]
                do(dve.tensor_copy(nmp[:, 0, :], t))
                dve.tensor_tensor(nmr[:], t, nmp[:, 0, :], ALU.subtract).then_inc(m_taken, 1)
                dve.wait_ge(m_taken, use.n + 3)
                do(dve.tensor_copy(nmp[:, 1, :], nmr[:]))
                dve.tensor_tensor(nmp[:, 2, :], nmr[:], nmp[:, 1, :], ALU.subtract).then_inc(shift_ready, 1)

            def take_output(use, g, qc):
                dve.wait_ge(m_ready, use.n + 1)
                o = ps[:, 2 * use.slot, :].rearrange("p (k h w) -> p k h w", k=CB, h=GH)
                do(dve.reciprocal(rsum[:, qc], o[:, :, :, HD:HD + 1]))
                dst = y_tok[:, qc * CB:(qc + 1) * CB, bass.ds(g * (GH * HD), GH * HD)].rearrange("p k (h d) -> p k h d", h=GH)
                dve.tensor_tensor(dst, o[:, :, :, 0:HD], rsum[:, qc].to_broadcast((P, CB, GH, HD)), ALU.mult).then_inc(m_taken, 1)

            def steps_from_2(g, next_one):
                for k in range(2, NST):
                    if next_one and k in UNITS_AT:
                        for u in units_of(k):
                            take_max(use_of(g, "unit", u), u)
                    if next_one and k == SPLIT_STEP:
                        split_max(use_of(g, "max"))
                    if k == TURN_STEP:
                        take_output(use_of(g, "out0"), g, 0)

            for u in range(NU):
                take_max(use_before(u), u)
            split_max(use_before(NU))
            for u in range(NEARLY):
                take_max(use_before(NU + 1 + u), u)
            with dve.Fori(0, (NG - 2) // GS) as i:
                chain.turn(i, 4 * GS)
                for s in range(GS):
                    g = i * GS + s
                    steps_from_2(g, True)
                    for u in range(NEARLY):
                        take_max(use_of(g, "early", u), u)
                    take_output(use_of(g, "out1"), g, 1)
            chain.turned((NG - 2) // GS)
            steps_from_2(NG - 2, True)
            take_output(use_of(NG - 2, "out1"), NG - 2, 1)
            steps_from_2(NG - 1, False)
            take_output(use_of(NG - 1, "out1"), NG - 1, 1)

            dve.wait_ge(bo_added, 1)
            for c in range(NCH + 1):
                if c < NCH:
                    dve.wait_ge(wo_done, c + 1)
                    xc = x_all[:, c * CB:(c + 1) * CB, :]
                    do(dve.tensor_tensor(xc, xc, ps[:, 2 + c % 2 * 2:4 + c % 2 * 2, :].rearrange("p a (k c) -> p (a k) c", k=2), ALU.add))
                    dve.sem_inc(x1_ready, 1)
                    norm_stats(lambda k: x_all[:, c * CB + k, :], var2_ready, c % 2)
                if c >= 1:
                    norm_scale(lambda k: x_all[:, (c - 1) * CB + k, :], lambda k: xn_all[:, (c - 1) * CB + k, :],
                               rstd2_ready, xn2_ready, c - 1, (c - 1) % 2)

            dve.wait_ge(vx_free, 1)
            with dve.Fori(0, NCH) as c:
                chain.turn(c, CB + 1 + XU)
                def rows(k):
                    return x_all[:, bass.ds(c * CB + k, 1), :].rearrange("p o c -> p (o c)")
                xc = x_all[:, bass.ds(c * CB, CB), :]
                for u in range(XU + PV_LAG + 2):
                    w = u - T_LAG - 1
                    if 0 <= w < XU and w % 2 == 1:
                        dve.wait_ge(tx_ready, c * XU + (w + 1))
                        if w // CB >= 2:
                            dve.wait_ge(ox_ready, c * PAIRS + (w // CB - 1))
                        dve.tensor_copy(pT[0:KC, w // CB % 2, :, w % CB * P:(w % CB + 1) * P],
                                        ps[0:KC, 7, 0:NKC * P].rearrange("p (c q) -> p c q", c=NKC)).then_inc(tx_dve, 1)
                    if u < XU:
                        dve.wait_ge(sx_ready, c * XU + (u + 1))
                        dve.tensor_reduce(nmx[:, u % 4, :], ps[:, (0, 1, 4, 5)[u % 4], 0:PK].rearrange("p (h k) -> p h k", h=2), AX.X, ALU.max,
                                          negate=True).then_inc(mx_ready, 1)
                    w = u - 1
                    if 0 <= w < XU:
                        dve.wait_ge(ex_ready, c * XU + (w + 1))
                        do(dve.reciprocal(rsx[:, w % 4, :], smx[:, w % 4, :]))
                        for h in range(2):
                            pp = px[:, w % 4, SK * h:SK * h + SK]
                            ins = dve.tensor_scalar(pp, pp, rsx[:, w % 4, h:h + 1], None, ALU.mult)
                        ins.then_inc(px_ready, 1)
                    w = u - PV_LAG - 1
                    if w % CB == CB - 1 and w > 0 and w // CB % 2 == 1 and w // CB < PAIRS:
                        dve.wait_ge(ox_ready, c * PAIRS + (w // CB + 1))
                        dve.tensor_copy(qT[:, w // CB, :], ps[:, 3, :]).then_inc(ox_dve, 1)
                dve.wait_ge(wox_done, c + 1)
                dve.wait_ge(box_added, c + 1)
                chain.add(dve.tensor_tensor(xc, xc, ps[:, 0:2, :].rearrange("p a (k c) -> p (a k) c", k=2), ALU.add))
                chain.wait_apart("dve")
                dve.sem_inc(x2_ready, 1)
                norm(rows, lambda k: xn_all[:, bass.ds(c * CB + k, 1), :].rearrange("p o c -> p (o c)"),
                     var2_ready, rstd2_ready, xn3_ready, c + NCH)
            chain.turned(NCH)

            dve.sem_inc(hs_ready, 2)
            dve.sem_inc(us_taken, 2)
            dve.sem_inc(ds_taken, 1)
            dve.sem_inc(gs_silu, 2)

            def gate_shared(c, meanwhile=None):
                for m in range(FF + 1):
                    if m < FF:
                        if m >= 2:
                            dve.wait_ge(shl_ready, c * FF + (m - 1))
                        dve.wait_ge(gs_silu, c * FF + (m + 3))
                        dve.wait_ge(us_ready, c * FF + (m + 1))
                        dve.tensor_tensor(prod[:, m % 2, :], sgl[:, m % 2, :], ps[:, (3, 7)[m % 2], :], ALU.mult).then_inc(us_taken, 1)
                        dve.wait_ge(us_taken, c * FF + (m + 3))
                        dve.sem_inc(hs_ready, 1)
                        dve.sem_inc(prod_ready, 1)
                    if m >= 1:
                        dve.wait_ge(shh_ready, c * FF + m)
                        dve.tensor_tensor(shT_l[:, m - 1, :], prod[:, (m - 1) % 2, :], shT_h[:, m - 1, :].bitcast(F32), ALU.subtract).then_inc(shl_ready, 1)
                if meanwhile:
                    meanwhile()
                dve.wait_ge(ds_ready, c + 1)
                xc = x_all[:, bass.ds(c * CB, CB), :]
                do(dve.tensor_tensor(xc, xc, ps[:, 4:6, :].rearrange("p a (k c) -> p (a k) c", k=2), ALU.add))
                dve.sem_inc(ds_taken, 1)

            def turned_low(c):
                dve.wait_ge(xnT3_ready, c + 1)
                dve.tensor_tensor(xnT_l[:, :, c * CT:(c + 1) * CT], ps[:, 4 + c % 2 * 2:6 + c % 2 * 2, :],
                                  xnT_h[:, :, c * CT:(c + 1) * CT].bitcast(F32), ALU.subtract).then_inc(xnT3l_ready, 1)

            turned_low(0)
            turned_low(1)
            gate_shared(0)
            turned_low(2)
            turned_low(3)

            dve.wait_ge(tno_ready, 1)
            dve.wait_ge(lg_ready, 1)
            lg2 = ps[:, 0, 0:2 * NBLK * E].rearrange("p (k h e) -> p k h e", h=2, e=E)
            do(dve.tensor_copy(lg_all[:], lg2[:, :, 0, :]))
            do(dve.tensor_tensor(lg_all[:], lg_all[:], lg2[:, :, 1, :], ALU.add))
            shape = (P, NBLK, E)

            def per_block(t):
                return t[:].rearrange("p (k o) -> p k o", o=1).to_broadcast(shape)

            def per_expert(t):
                return t[:].rearrange("p (o e) -> p o e", o=1).to_broadcast(shape)

            dve.tensor_reduce(mx[:], lg_all[:], AX.X, ALU.max).then_inc(mxl_ready, 1)
            dve.wait_ge(mxl_ready, 1)
            do(dve.tensor_tensor(cand[:], lg_all[:], per_block(mx), ALU.is_ge))
            do(dve.tensor_tensor(cand[:], cand[:], per_expert(em99), ALU.mult))
            do(dve.tensor_reduce(pick[:], cand[:], AX.X, ALU.min))
            do(dve.tensor_tensor(onehot[:], per_expert(em99), per_block(pick), ALU.is_equal))
            dve.tensor_copy(onehotb[:], onehot[:]).then_inc(oh_ready, 1)

            def place_tokens():
                dve.wait_ge(exp_ready, 1)
                do(dve.tensor_scalar(score[:], emx[:], 1.0, None, ALU.add))
                dve.reciprocal(score[:], score[:]).then_inc(score_ready, 1)
                dve.wait_ge(rank_ready, 1)
                do(dve.tensor_tensor(over, ps[:, 1, 0:E].rearrange("p (e o) -> p e o", o=1).to_broadcast((P, E, NBLK)),
                                     steps128[:].rearrange("p (o k) -> p o k", o=1).to_broadcast((P, E, NBLK)), ALU.is_gt))
                do(dve.tensor_reduce(tiles[:], over, AX.X, ALU.add))
                do(dve.tensor_tensor_scan(ends[:], ones_e[:], tiles[:], 0.0, ALU.mult, ALU.add))
                do(dve.tensor_tensor(base_t[:], ends[:], tiles[:], ALU.subtract))
                do(dve.tensor_scalar(base_t[:], base_t[:], float(P), None, ALU.mult))
                do(dve.tensor_tensor(cand[:], ps[:, 0, 0:NBLK * E].rearrange("p (k e) -> p k e", e=E), per_expert(base_t), ALU.add))
                do(dve.tensor_tensor(cand[:], cand[:], onehot[:], ALU.mult))
                do(dve.tensor_reduce(posf[:], cand[:], AX.X, ALU.add))
                dve.tensor_copy(pos[:], posf[:]).then_inc(pos_ready, 1)

            def rows_and_cols(rows, cols):
                n, m = rows.shape[-1], cols.shape[-1]
                return (rows.rearrange("o (n i) -> o n i", i=1).to_broadcast((1, n, m)),
                        cols.rearrange("o (i m) -> o i m", i=1).to_broadcast((1, n, m)))

            def list_experts():
                t1, e1 = tiles[0:1, :], ends[0:1, :]
                do(dve.tensor_scalar(some[:], t1, 0.5, None, ALU.is_ge))
                do(dve.tensor_tensor_scan(upto[:], ones_e[0:1, :], some[:], 0.0, ALU.mult, ALU.add))
                do(dve.tensor_tensor(passed[0:1, 0:E], *rows_and_cols(tno[0:1, 0:E], upto[:]), ALU.is_ge))
                do(dve.tensor_reduce(numbered[:], passed[0:1, 0:E], AX.X, ALU.add))
                do(dve.tensor_scalar(numbered[:], numbered[:], float(E - 1), None, ALU.min))
                dve.tensor_copy(expert[:], numbered[:]).then_inc(list_ready, 1)
                do(dve.tensor_tensor(passed[:], *rows_and_cols(tno[:], e1), ALU.is_ge))
                do(dve.tensor_tensor(passed[:], passed[:], rows_and_cols(tno[:], some[:])[1], ALU.mult))
                do(dve.tensor_reduce(numf[:], passed[:], AX.X, ALU.add))
                do(dve.tensor_scalar(upto1[:], upto[:], -1.0, None, ALU.add))
                do(dve.tensor_tensor(numf[:], numf[:], upto1[0:1, E - 1:E].to_broadcast((1, NTT)), ALU.min))
                do(dve.tensor_scalar(need[:], numf[:], 1.0, None, ALU.add))
                do(dve.tensor_copy(slotf[:], numf[:]))
                for n in range(WS, E, WS):
                    do(dve.tensor_scalar(used[:], numf[:], float(n), float(WS), ALU.is_ge, ALU.mult))
                    do(dve.tensor_tensor(slotf[:], slotf[:], used[:], ALU.subtract))
                do(dve.tensor_copy(slot[:], slotf[:]))
                do(dve.tensor_tensor(passed[0:1, 0:E], *rows_and_cols(tno[0:1, 0:E], upto1[:]), ALU.is_ge))
                do(dve.tensor_tensor(passed[0:1, 0:E], passed[0:1, 0:E], rows_and_cols(upto[:], t1)[1], ALU.mult))
                do(dve.tensor_reduce(endj[:], passed[0:1, 0:E], AX.X, ALU.add))
                do(dve.tensor_tensor(lastj[:], endj[:], e1[:, E - 1:E].to_broadcast((1, E)), ALU.is_ge))
                do(dve.tensor_scalar(lastj[:], lastj[:], float(NT), None, ALU.mult))
                do(dve.tensor_tensor(endj[:], endj[:], lastj[:], ALU.max))
                dve.tensor_scalar(freed[:], endj[:], 1.0, None, ALU.add).then_inc(tables_ready, 1)
                do(dve.tensor_tensor(used[:], ends[0:1, E - 1:E].to_broadcast((1, NTT)), tno[:], ALU.is_gt))
                do(dve.tensor_reduce(usedn[:], used[:].rearrange("o (i s) -> o s i", s=2), AX.X, ALU.add))
                do(dve.tensor_scalar(usedn[:], usedn[:], 16.0, 16.0, ALU.mult, ALU.add))
                dve.tensor_copy(filled[:], usedn[:]).then_inc(filled_ready, 1)

            gate_shared(1, place_tokens)
            gate_shared(2, list_experts)

            def slot_of(i, s, d):
                t, _, _, _ = ahead(i, s, d)
                return dve.value_load(slot[0:1, bass.ds(t, 1)], min_val=0, max_val=WS - 1)

            def part_low(i, s, d, at=None):
                t, _, _, _ = ahead(i, s, d)
                p = (s + d) % 2
                at = slot_of(i, s, d) if at is None else at
                wait_apart(dve, "dve", wh_ready, t + 1)
                dve.tensor_tensor(wgu_l[p][:], wgu_s[:, bass.ds(at, 1)].rearrange("p o f n -> p (o f) n"), wgu_h[p][:].bitcast(F32),
                                  ALU.subtract).then_inc(wl_ready, 1)

            def rows_low(i, s, d):
                t, _, _, _ = ahead(i, s, d)
                p = (s + d) % 2
                dve.wait_ge(xh_ready, t + 1)
                dve.tensor_tensor(xgT_l[p][:], ps[:, 0, 0:C].rearrange("p (f q) -> p f q", f=FC), xgT_h[p][:].bitcast(F32),
                                  ALU.subtract).then_inc(xl_ready, 1)

            def gated(i, s, d):
                t, _, _, _ = ahead(i, s, d)
                p = (s + d) % 2
                dve.wait_ge(silu_ready, t + 1)
                dve.wait_ge(ue_ready, t + 1)
                dve.tensor_tensor(h_tok[p][:], act_s[p][:], ps[:, 3 + 2 * p, :], ALU.mult).then_inc(he_ready, 1)

            gate_shared(3, lambda: part_low(0, 0, 0))
            rows_low(0, 0, 0)
            part_low(0, 0, 1)
            gated(0, 0, 0)
            rows_low(0, 0, 1)
            part_low(0, 0, 2)

            def dve_tile(i, s, left=NT):
                if left > 3:
                    at = slot_of(i, s, 3)
                if left > 1:
                    gated(i, s, 1)
                if left > 2:
                    rows_low(i, s, 2)
                if left > 3:
                    part_low(i, s, 3, at)

            with dve.Fori(0, NT // RS - 1) as i:
                for s in range(RS):
                    dve_tile(i, s)
            for t in range((NT // RS - 1) * RS, NT):
                dve_tile(t // RS, t % RS, left=NT - t)


_OUT = ("out_dram", (B, S, C))


def kernel(**inputs):
    import concourse.bacc as bacc
    from concourse.bass_utils import run_bass_kernel_spmd

    def a(name):
        return np.asarray(inputs[name])

    def by_group(w):
        return w.reshape(-1, H // GH, GH, HD).swapaxes(-1, -2).reshape(w.shape)

    arrays = {
        "x": a("x"), "ctxT": a("ctx_768").transpose(2, 0, 1).reshape(CD, B * SK),
        "wq": by_group(a("L0_attn_Wq")), "bq": by_group(a("L0_attn_bq")),
        "wk": by_group(a("L0_attn_Wk")), "bk": by_group(a("L0_attn_bk")),
        "wv": a("L0_attn_Wv"), "bv": a("L0_attn_bv"), "wo": a("L0_attn_Wo"), "bo": a("L0_attn_bo"),
        "wqx": a("L0_xattn_w_q"), "wkx": a("L0_xattn_w_k"), "wvx": a("L0_xattn_w_v"), "wox": a("L0_xattn_w_o"), "box": a("L0_xattn_b_o"),
        "wr": a("L0_ffn_w_router").T, "wgu": a("L0_ffn_gate_up_proj"), "wdn": a("L0_ffn_down_proj"),
        "wsg": a("L0_ffn_w_gate").T, "wsu": a("L0_ffn_w_up").T, "wsd": a("L0_ffn_w_down").T,
    }
    arrays = {k: np.ascontiguousarray(v) for k, v in arrays.items()}
    nc = bacc.Bacc("TRN2", target_bir_lowering=False, num_devices=1)
    aps = {k: nc.dram_tensor(k + "_dram", v.shape, mybir.dt.from_np(v.dtype), kind="ExternalInput").ap() for k, v in arrays.items()}
    out = nc.dram_tensor(_OUT[0], _OUT[1], F32, kind="ExternalOutput").ap()
    build(nc, **aps, out=out)
    r = run_bass_kernel_spmd(nc, [{k + "_dram": v for k, v in arrays.items()}], core_ids=[0])
    return np.asarray(r.results[0][_OUT[0]])
```
